# Optimizing a Trainium2 kernel written in Bass

```python
import numpy as np
import jax
import jax.numpy as jnp

def _softmax(x, axis=-1):
    return jax.nn.softmax(x, axis=axis)

def _gelu(x):
    return jax.nn.gelu(x, approximate=True)

def _silu(x):
    return jax.nn.silu(x)

def _sigmoid(x):
    return jax.nn.sigmoid(x)

def _layernorm(x, axis=-1, eps=1e-05):
    m = jnp.mean(x, axis=axis, keepdims=True)
    v = jnp.var(x, axis=axis, keepdims=True)
    return (x - m) / jnp.sqrt(v + eps)

def _scatter_add(tgt, idx, src, axis=0):
    return tgt.at[idx].add(src)

def _segment_sum(src, seg, n):
    return jax.ops.segment_sum(src, seg, n)
kernel_name = 'mk_xattn_ffn_d2_seqx_r8_2e4a65'

def setup_inputs(seed: int=0):
    np.random.seed(seed)
    _w = jnp.asarray

    def _rec_inputs():
        import jax
        import jax.numpy as jnp
        _rk = jax.random.key(seed)
        x = -0.000125 + 0.9999 * jax.random.normal(jax.random.fold_in(_rk, 1), (16, 128, 128), jnp.float32)
        _lenS = 128 - jax.random.randint(jax.random.fold_in(_rk, 7), (16,), 0, max(1, 128 // 4) + 1, jnp.int32)
        _lenS2 = 128 - jax.random.randint(jax.random.fold_in(_rk, 8), (16,), 0, max(1, 128 // 4) + 1, jnp.int32)
        _ctx_768P = jax.random.normal(jax.random.fold_in(_rk, 11), (16, 16, 96), jnp.float32)
        _ctx_768c = jax.random.dirichlet(jax.random.fold_in(_rk, 511), 0.3 * jnp.ones((16,), jnp.float32), (16, 128))
        _ctx_768t = jnp.einsum('bsk,bkd->bsd', _ctx_768c, _ctx_768P)
        _ctx_768t = _ctx_768t * jax.lax.rsqrt(jnp.mean(jnp.square(_ctx_768t)) + 1e-12) * 0.953939
        ctx_768 = 0.00272024 + 0.999456 * (_ctx_768t + 0.3 * jax.random.normal(jax.random.fold_in(_rk, 611), (16, 128, 96), jnp.float32))
        return (x, ctx_768)
    x, ctx_768 = _rec_inputs()

    def _L0_xattn_setup():
        import jax, jax.numpy as jnp
        import numpy as np
        N_HEADS = 16
        DIM_EMBED = 128
        DIM_CROSS = 96
        DIM_HEAD = DIM_EMBED // N_HEADS
        key = jax.random.key(seed)
        ks = jax.random.split(key, 10)
        B, Sq, Sk = (8, 512, 77)
        s_e = 1.0 / np.sqrt(DIM_EMBED)
        s_c = 1.0 / np.sqrt(DIM_CROSS)
        return {'x': jax.random.normal(ks[0], (B, Sq, DIM_EMBED), jnp.float32), 'y': jax.random.normal(ks[1], (B, Sk, DIM_CROSS), jnp.float32), 'wq': jax.random.normal(ks[2], (DIM_EMBED, DIM_EMBED), jnp.float32) * s_e, 'bq': jax.random.normal(ks[3], (DIM_EMBED,), jnp.float32) * 0.01, 'wk': jax.random.normal(ks[4], (DIM_CROSS, DIM_EMBED), jnp.float32) * s_c, 'bk': jax.random.normal(ks[5], (DIM_EMBED,), jnp.float32) * 0.01, 'wv': jax.random.normal(ks[6], (DIM_CROSS, DIM_EMBED), jnp.float32) * s_c, 'bv': jax.random.normal(ks[7], (DIM_EMBED,), jnp.float32) * 0.01, 'wo': jax.random.normal(ks[8], (DIM_EMBED, DIM_EMBED), jnp.float32) * s_e, 'bo': jax.random.normal(ks[9], (DIM_EMBED,), jnp.float32) * 0.01}
    _L0_xattn_all = _L0_xattn_setup()
    _L0_xattn_in = {k: v for k, v in _L0_xattn_all.items() if k in ('wq', 'bq', 'wk', 'bk', 'wv', 'bv', 'wo', 'bo')}
    del _L0_xattn_all

    def _L0_ffn_setup():
        import jax, jax.numpy as jnp
        import numpy as np
        key = jax.random.key(seed)
        k1, k2, k3 = jax.random.split(key, 3)
        B, T, D, E = (4, 256, 128, 8)
        x = jax.random.normal(k1, (B, T, D), dtype=jnp.float32)
        gate_w = jax.random.normal(k2, (E, D), dtype=jnp.float32) * (1.0 / np.sqrt(D))
        bound = float(np.sqrt(6.0 / (D + D)))
        We = jax.random.uniform(k3, (E, D, D), dtype=jnp.float32, minval=-bound, maxval=bound)
        return {'x': x, 'gate_w': gate_w, 'We': We}
    _L0_ffn_all = _L0_ffn_setup()
    _L0_ffn_in = {k: v for k, v in _L0_ffn_all.items() if k in ('gate_w', 'We')}
    del _L0_ffn_all

    def _L1_xattn_setup():
        import jax, jax.numpy as jnp
        import numpy as np
        HEADS = 16
        DIM_HEAD = 64
        RANK = 32
        LORA_W = 1.0
        IPA_SCALE = 1.0
        IPA_TOKENS = 4
        SCALE = DIM_HEAD ** (-0.5)

        def _split_heads(t):
            b, n, _ = t.shape
            return t.reshape(b, n, HEADS, DIM_HEAD).transpose(0, 2, 1, 3)

        def _merge_heads(t):
            b, h, n, d = t.shape
            return t.transpose(0, 2, 1, 3).reshape(b, n, h * d)

        def _attention(q_in, k_in, v_in):
            q = _split_heads(q_in)
            k = _split_heads(k_in)
            v = _split_heads(v_in)
            s = jnp.einsum('bhid,bhjd->bhij', q, k) * SCALE
            p = jax.nn.softmax(s, axis=-1)
            o = jnp.einsum('bhij,bhjd->bhid', p, v)
            return _merge_heads(o)

        def _lora(t, down, up, alpha):
            return t @ down @ up * (LORA_W * alpha[0] / RANK)
        key = jax.random.key(seed)
        ks = jax.random.split(key, 20)
        B, N, QD, CD, ID = (8, 512, 128, 96, HEADS * DIM_HEAD)
        CTX = 77 + IPA_TOKENS
        s = 0.02
        return {'x': jax.random.normal(ks[0], (B, N, QD), jnp.float32), 'context': jax.random.normal(ks[1], (B, CTX, CD), jnp.float32), 'Wq': jax.random.normal(ks[2], (QD, ID), jnp.float32) * s, 'Wk': jax.random.normal(ks[3], (CD, ID), jnp.float32) * s, 'Wv': jax.random.normal(ks[4], (CD, ID), jnp.float32) * s, 'Wo': jax.random.normal(ks[5], (ID, QD), jnp.float32) * s, 'bo': jnp.zeros((QD,), jnp.float32), 'q_down': jax.random.normal(ks[6], (QD, RANK), jnp.float32) * s, 'q_up': jax.random.normal(ks[7], (RANK, ID), jnp.float32) * s, 'q_alpha': jnp.ones((1,), jnp.float32) * RANK, 'k_down': jax.random.normal(ks[8], (CD, RANK), jnp.float32) * s, 'k_up': jax.random.normal(ks[9], (RANK, ID), jnp.float32) * s, 'k_alpha': jnp.ones((1,), jnp.float32) * RANK, 'v_down': jax.random.normal(ks[10], (CD, RANK), jnp.float32) * s, 'v_up': jax.random.normal(ks[11], (RANK, ID), jnp.float32) * s, 'v_alpha': jnp.ones((1,), jnp.float32) * RANK, 'o_down': jax.random.normal(ks[12], (ID, RANK), jnp.float32) * s, 'o_up': jax.random.normal(ks[13], (RANK, QD), jnp.float32) * s, 'o_alpha': jnp.ones((1,), jnp.float32) * RANK, 'Wk_ipa': jax.random.normal(ks[14], (CD, ID), jnp.float32) * s, 'Wv_ipa': jax.random.normal(ks[15], (CD, ID), jnp.float32) * s}
    _L1_xattn_all = _L1_xattn_setup()
    _L1_xattn_in = {k: v for k, v in _L1_xattn_all.items() if k in ('Wq', 'Wk', 'Wv', 'Wo', 'bo', 'q_down', 'q_up', 'q_alpha', 'k_down', 'k_up', 'k_alpha', 'v_down', 'v_up', 'v_alpha', 'o_down', 'o_up', 'o_alpha', 'Wk_ipa', 'Wv_ipa')}
    del _L1_xattn_all

    def _L1_ffn_setup():
        import jax, jax.numpy as jnp
        import numpy as np
        import math
        B, S, D = (4, 256, 128)
        E, DFF = (16, 256)
        CAP_FACTOR = 2.0
        ROUTER_HIDDEN = 128
        CAPACITY = int(math.ceil(S * CAP_FACTOR / E))
        key = jax.random.key(seed)
        ks = jax.random.split(key, 6)

        def uinit(k, shape, fan_in):
            bound = math.sqrt(3.0) * math.sqrt(1.0 / 3.0) / math.sqrt(fan_in)
            return jax.random.uniform(k, shape, jnp.float32, -bound, bound)
        return {'hidden_states': jax.random.normal(ks[0], (B, S, D), jnp.float32), 'router_w1': jax.random.normal(ks[1], (D, ROUTER_HIDDEN), jnp.float32) / math.sqrt(D), 'router_w2': jax.random.normal(ks[2], (ROUTER_HIDDEN, E), jnp.float32) / math.sqrt(ROUTER_HIDDEN), 'w1': uinit(ks[3], (E, D, DFF), D), 'w2': uinit(ks[4], (E, D, DFF), D), 'w3': uinit(ks[5], (E, DFF, D), DFF)}
    _L1_ffn_all = _L1_ffn_setup()
    _L1_ffn_in = {k: v for k, v in _L1_ffn_all.items() if k in ('router_w1', 'router_w2', 'w1', 'w2', 'w3')}
    del _L1_ffn_all
    return {'x': x, 'ctx_768': ctx_768, 'L0_xattn_wq': _L0_xattn_in['wq'], 'L0_xattn_bq': _L0_xattn_in['bq'], 'L0_xattn_wk': _L0_xattn_in['wk'], 'L0_xattn_bk': _L0_xattn_in['bk'], 'L0_xattn_wv': _L0_xattn_in['wv'], 'L0_xattn_bv': _L0_xattn_in['bv'], 'L0_xattn_wo': _L0_xattn_in['wo'], 'L0_xattn_bo': _L0_xattn_in['bo'], 'L0_ffn_gate_w': _L0_ffn_in['gate_w'], 'L0_ffn_We': _L0_ffn_in['We'], 'L1_xattn_Wq': _L1_xattn_in['Wq'], 'L1_xattn_Wk': _L1_xattn_in['Wk'], 'L1_xattn_Wv': _L1_xattn_in['Wv'], 'L1_xattn_Wo': _L1_xattn_in['Wo'], 'L1_xattn_bo': _L1_xattn_in['bo'], 'L1_xattn_q_down': _L1_xattn_in['q_down'], 'L1_xattn_q_up': _L1_xattn_in['q_up'], 'L1_xattn_q_alpha': _L1_xattn_in['q_alpha'], 'L1_xattn_k_down': _L1_xattn_in['k_down'], 'L1_xattn_k_up': _L1_xattn_in['k_up'], 'L1_xattn_k_alpha': _L1_xattn_in['k_alpha'], 'L1_xattn_v_down': _L1_xattn_in['v_down'], 'L1_xattn_v_up': _L1_xattn_in['v_up'], 'L1_xattn_v_alpha': _L1_xattn_in['v_alpha'], 'L1_xattn_o_down': _L1_xattn_in['o_down'], 'L1_xattn_o_up': _L1_xattn_in['o_up'], 'L1_xattn_o_alpha': _L1_xattn_in['o_alpha'], 'L1_xattn_Wk_ipa': _L1_xattn_in['Wk_ipa'], 'L1_xattn_Wv_ipa': _L1_xattn_in['Wv_ipa'], 'L1_ffn_router_w1': _L1_ffn_in['router_w1'], 'L1_ffn_router_w2': _L1_ffn_in['router_w2'], 'L1_ffn_w1': _L1_ffn_in['w1'], 'L1_ffn_w2': _L1_ffn_in['w2'], 'L1_ffn_w3': _L1_ffn_in['w3']}

def reference(x, ctx_768, L0_xattn_wq, L0_xattn_bq, L0_xattn_wk, L0_xattn_bk, L0_xattn_wv, L0_xattn_bv, L0_xattn_wo, L0_xattn_bo, L0_ffn_gate_w, L0_ffn_We, L1_xattn_Wq, L1_xattn_Wk, L1_xattn_Wv, L1_xattn_Wo, L1_xattn_bo, L1_xattn_q_down, L1_xattn_q_up, L1_xattn_q_alpha, L1_xattn_k_down, L1_xattn_k_up, L1_xattn_k_alpha, L1_xattn_v_down, L1_xattn_v_up, L1_xattn_v_alpha, L1_xattn_o_down, L1_xattn_o_up, L1_xattn_o_alpha, L1_xattn_Wk_ipa, L1_xattn_Wv_ipa, L1_ffn_router_w1, L1_ffn_router_w2, L1_ffn_w1, L1_ffn_w2, L1_ffn_w3):
    import jax
    import jax.numpy as jnp

    def _L0_xattn_ref(x, y, wq, bq, wk, bk, wv, bv, wo, bo):
        import jax, jax.numpy as jnp
        import numpy as np
        N_HEADS = 16
        DIM_EMBED = 128
        DIM_CROSS = 96
        DIM_HEAD = DIM_EMBED // N_HEADS
        B, Sq, E = x.shape
        H, D = (N_HEADS, DIM_HEAD)
        q = (x @ wq + bq).reshape(B, Sq, H, D).transpose(0, 2, 1, 3)
        k = (y @ wk + bk).reshape(B, -1, H, D).transpose(0, 2, 1, 3)
        v = (y @ wv + bv).reshape(B, -1, H, D).transpose(0, 2, 1, 3)
        scores = jnp.einsum('bhqd,bhkd->bhqk', q, k) / jnp.sqrt(jnp.asarray(D, x.dtype))
        attn = jax.nn.softmax(scores, axis=-1)
        out = jnp.einsum('bhqk,bhkd->bhqd', attn, v)
        out = out.transpose(0, 2, 1, 3).reshape(B, Sq, E)
        return out @ wo + bo

    def _L0_ffn_ref(x, gate_w, We):
        import jax, jax.numpy as jnp
        import numpy as np
        top_k = 2
        logits = jnp.einsum('btd,ed->bte', x, gate_w)
        top_val, top_idx = jax.lax.top_k(logits, top_k)
        top_w = jax.nn.softmax(top_val, axis=-1)
        y_all = jnp.einsum('btd,edm->btem', x, We)
        x_experts = jnp.take_along_axis(y_all, top_idx[..., None], axis=2)
        out = jnp.sum(x_experts * top_w[..., None], axis=2)
        return out

    def _L1_xattn_ref(x, context, Wq, Wk, Wv, Wo, bo, q_down, q_up, q_alpha, k_down, k_up, k_alpha, v_down, v_up, v_alpha, o_down, o_up, o_alpha, Wk_ipa, Wv_ipa):
        import jax, jax.numpy as jnp
        import numpy as np
        HEADS = 16
        DIM_HEAD = 64
        RANK = 32
        LORA_W = 1.0
        IPA_SCALE = 1.0
        IPA_TOKENS = 4
        SCALE = DIM_HEAD ** (-0.5)

        def _split_heads(t):
            b, n, _ = t.shape
            return t.reshape(b, n, HEADS, DIM_HEAD).transpose(0, 2, 1, 3)

        def _merge_heads(t):
            b, h, n, d = t.shape
            return t.transpose(0, 2, 1, 3).reshape(b, n, h * d)

        def _attention(q_in, k_in, v_in):
            q = _split_heads(q_in)
            k = _split_heads(k_in)
            v = _split_heads(v_in)
            s = jnp.einsum('bhid,bhjd->bhij', q, k) * SCALE
            p = jax.nn.softmax(s, axis=-1)
            o = jnp.einsum('bhij,bhjd->bhid', p, v)
            return _merge_heads(o)

        def _lora(t, down, up, alpha):
            return t @ down @ up * (LORA_W * alpha[0] / RANK)
        q_in = x @ Wq + _lora(x, q_down, q_up, q_alpha)
        end = context.shape[1] - IPA_TOKENS
        org_ctx = context[:, :end, :]
        ipa_ctx = context[:, end:, :]
        k_in = org_ctx @ Wk + _lora(org_ctx, k_down, k_up, k_alpha)
        v_in = org_ctx @ Wv + _lora(org_ctx, v_down, v_up, v_alpha)
        out = _attention(q_in, k_in, v_in)
        ipa_k = ipa_ctx @ Wk_ipa
        ipa_v = ipa_ctx @ Wv_ipa
        out_ipa = _attention(q_in, ipa_k, ipa_v)
        out = out + IPA_SCALE * out_ipa
        return out @ Wo + bo + _lora(out, o_down, o_up, o_alpha)

    def _L1_ffn_ref(hidden_states, router_w1, router_w2, w1, w2, w3):
        import jax, jax.numpy as jnp
        import numpy as np
        import math
        B, S, D = (4, 256, 128)
        E, DFF = (16, 256)
        CAP_FACTOR = 2.0
        ROUTER_HIDDEN = 128
        CAPACITY = int(math.ceil(S * CAP_FACTOR / E))
        b, s, d = hidden_states.shape
        e = w1.shape[0]
        cap = CAPACITY
        router_logits = jax.nn.silu(hidden_states @ router_w1) @ router_w2
        expert_probs = jax.nn.softmax(router_logits.transpose(0, 2, 1), axis=-1)
        expert_weights, token_indices = jax.lax.top_k(expert_probs, cap)
        expert_weights = expert_weights / (expert_weights.sum(-1, keepdims=True) + 1e-09)
        expert_inputs = jax.vmap(lambda h, i: h[i])(hidden_states, token_indices)
        gate = jax.nn.silu(jnp.einsum('becd,edf->becf', expert_inputs, w1))
        value = jnp.einsum('becd,edf->becf', expert_inputs, w2)
        expert_out = jnp.einsum('becf,efd->becd', gate * value, w3)
        weighted = expert_out * expert_weights[..., None]

        def combine(idx, vals):
            return jnp.zeros((s, d), vals.dtype).at[idx.reshape(-1)].add(vals.reshape(-1, d))
        output = jax.vmap(combine)(token_indices, weighted)
        return output
    x = x + _L0_xattn_ref(_layernorm(x, axis=-1), ctx_768, L0_xattn_wq, L0_xattn_bq, L0_xattn_wk, L0_xattn_bk, L0_xattn_wv, L0_xattn_bv, L0_xattn_wo, L0_xattn_bo)
    x = x + _L0_ffn_ref(_layernorm(x, axis=-1), L0_ffn_gate_w, L0_ffn_We)
    x = x + _L1_xattn_ref(_layernorm(x, axis=-1), ctx_768, L1_xattn_Wq, L1_xattn_Wk, L1_xattn_Wv, L1_xattn_Wo, L1_xattn_bo, L1_xattn_q_down, L1_xattn_q_up, L1_xattn_q_alpha, L1_xattn_k_down, L1_xattn_k_up, L1_xattn_k_alpha, L1_xattn_v_down, L1_xattn_v_up, L1_xattn_v_alpha, L1_xattn_o_down, L1_xattn_o_up, L1_xattn_o_alpha, L1_xattn_Wk_ipa, L1_xattn_Wv_ipa)
    x = x + _L1_ffn_ref(_layernorm(x, axis=-1), L1_ffn_router_w1, L1_ffn_router_w2, L1_ffn_w1, L1_ffn_w2, L1_ffn_w3)
    return x

_drawn_inputs = setup_inputs


def setup_inputs(seed=0):
    import zlib

    import numpy as np

    out = dict(_drawn_inputs(seed))
    spreads = {'L1_xattn_bo': (0.0, 0.1)}
    factors = {'L0_xattn_bq': 3.415,
     'L0_xattn_bk': 8.0,
     'L1_xattn_Wq': 8.0,
     'L1_xattn_Wk': 8.0,
     'L1_xattn_q_down': 8.0,
     'L1_xattn_q_up': 8.0,
     'L1_xattn_k_down': 8.0,
     'L1_xattn_k_up': 8.0,
     'L1_xattn_v_down': 8.0,
     'L1_xattn_v_up': 8.0,
     'L1_xattn_o_down': 6.69,
     'L1_xattn_o_up': 6.362,
     'L1_xattn_Wk_ipa': 8.0,
     'L1_ffn_router_w1': 8.0,
     'L1_ffn_router_w2': 8.0,
     'L1_ffn_w1': 8.0,
     'L1_ffn_w2': 8.0,
     'L1_ffn_w3': 8.0}
    for name, (base, spread) in spreads.items():
        noise = np.random.default_rng([zlib.crc32(name.encode()), seed]).standard_normal(out[name].shape)
        drawn = base * np.exp(spread * noise) if base else spread * noise
        out[name] = jnp.asarray(drawn.astype(out[name].dtype))
    for name, factor in factors.items():
        out[name] = (out[name] * factor).astype(out[name].dtype)
    return out
```

```python
from contextlib import ExitStack

import concourse.bass as bass
from concourse import mybir

F32 = mybir.dt.float32
BF16 = mybir.dt.bfloat16
I32 = mybir.dt.int32
ALU = mybir.AluOpType
ACT = mybir.ActivationFunctionType
X = mybir.AxisListType.X

B, S, D = 16, 128, 128
C = 96
H = 16
D0 = D // H
D1 = 64
ID = H * D1
RANK = 32
IPA = 4
ORG = S - IPA
E0 = 8
E1, F1 = 16, 256
EG = E1 // 4
CAP = 32
EPS = 1e-5
CH = 4
NCH = H // CH
BANK = 512


def named(make, prefix, names):
    return type(prefix, (), {name: make(f"{prefix}_{name}") for name in names.split()})


def after(eng, sem, value):
    if not isinstance(value, int) or value >= 1:
        eng.wait_ge(sem, value)


def there(b):
    return not isinstance(b, int) or 0 <= b < B


def there_expert(e):
    return not isinstance(e, int) or e < E1


def pipelined(eng, body):
    for b in (-1, 0, 1):
        body(b, b % 2)
    with eng.Fori(0, (B - 4) // 2) as i:
        body(i * 2 + 2, 0)
        body(i * 2 + 3, 1)
    for b in (B - 2, B - 1, B):
        body(b, b % 2)


def by_pairs(eng, body):
    with eng.Fori(0, B // 2) as i:
        body(i * 2, 0)
        body(i * 2 + 1, 1)


def build_program(nc, T, out):
    with ExitStack() as ctx:
        def sb(name, shape, dt=F32):
            return ctx.enter_context(nc.sbuf_tensor(name, shape, dt))

        def sem(name):
            return ctx.enter_context(nc.semaphore(name))

        bank = [ctx.enter_context(nc.psum_tensor(f"bank{n}", [128, BANK], F32)) for n in range(8)]
        MAXB = bank[0]
        SCB = bank[1:3]
        OB = bank[3:5]
        PB = bank[5:7]
        TB = bank[7]

        def blocks(b_, rows=128):
            return b_[0:rows, :].rearrange("p (g n) -> p g n", g=CH)

        ident = sb("ident", [128, 128])
        ident_bf = sb("ident_bf", [128, 128], BF16)
        pick = sb("pick", [128, H, 128], BF16)
        ones_row = sb("ones_row", [1, 128])
        minus_half = sb("minus_half", [128, B])
        x_all = sb("x_all", [128, B, D])
        ctx_all = sb("ctx_all", [128, B, C])
        stats = sb("stats", [128, B, 6])
        mv = sb("mv", [128, B, 2])
        veps = sb("veps", [128, B])
        rstd = sb("rstd", [128, B, 1])

        class Arena:

            def __init__(self, name, size):
                self.tile, self.size = sb(name, [128, size]), size
                self.again()

            def again(self):
                self.at = 0

            def take(self, shape, dt=F32):
                rows, dims = shape[0], shape[1:]
                n = 1
                for d in dims:
                    n *= d
                words = n if dt in (F32, I32) else n // 2
                assert self.at + words <= self.size, (self.at + words, self.size)
                flat = self.tile[0:rows, self.at:self.at + words]
                self.at += words
                if dt != F32:
                    flat = flat.bitcast(dt)
                letters = "abcde"[:len(dims)]
                return flat.rearrange(f"p ({' '.join(letters)}) -> p {' '.join(letters)}",
                                      **dict(zip(letters, dims)))

        early = Arena("early", 15872)
        late = Arena("late", 11776)

        ctx_in = sb("ctx_in", [128, 2, C])
        xn = sb("xn", [128, 2, D])
        xT = sb("xT", [128, 2, 128])
        cT = sb("cT", [C, 2, 128])
        qT = sb("qT", [128, 2, 128])
        q_bf = sb("q_bf", [128, 2, 128], BF16)
        kT = sb("kT", [128, 2, H, ORG + IPA])
        x_bf = sb("x_bf", [128, 2, 128], BF16)
        k_bf = late.take([128, 2, H, 128], BF16)
        qm = early.take([128, 2, H, 128])
        km_bf = early.take([128, 2, H, 128], BF16)
        vm = early.take([128, 2, 2, 8, 136])
        o0T = sb("o0T", [64, 2, 2, 128])
        rsum0 = sb("rsum0", [64, 2, 2, 128])
        hmask = sb("hmask", [128, H])
        v1 = late.take([128, 2, H, D1 + 1])
        negmax = sb("negmax", [128, 128], BF16)
        negmaxT = sb("negmaxT", [128, 2, 128], BF16)
        pT = sb("pT", [128, 2, CH, 128])
        rsum = sb("rsum", [128, 2, H])
        o = sb("o", [128, 2, ID])
        oT = sb("oT", [128, 2, 8, 128])

        wq0 = early.take([D, D])
        wk0 = early.take([C, D])
        bq0 = sb("bq0", [128, 1])
        bk0 = sb("bk0", [128, 1])
        wv0 = early.take([C, D])
        bv0 = early.take([128, D])
        wo0 = early.take([64, 2, D])
        bo0 = sb("bo0", [1, D])

        gate_in = sb("gate_in", [E0, D])
        gateT = early.take([D, E0])
        we = early.take([D, E0, D])
        lower = sb("lower", [128, E0, E0])
        lg = sb("lg", [128, 2, E0])
        beat = sb("beat", [128, 2, E0, E0])
        tie = sb("tie", [128, 2, E0, E0])
        nbeat = sb("nbeat", [128, 2, E0])
        negtop = sb("negtop", [128, 2, 1])
        ew = sb("ew", [128, 2, E0])
        wsum = sb("wsum", [128, 2, 1])
        ffn_w = sb("ffn_w", [128, 2, E0])
        ys = early.take([128, 2, E0, D])
        ysum = sb("ysum", [128, 2, D])

        wq1 = late.take([D, ID])
        wk1 = late.take([C, ID])
        mT = late.take([C, H, D])
        wv1 = late.take([C, ID])
        wo1 = late.take([128, 8, D])
        bo1 = sb("bo1", [1, D])
        alpha = sb("alpha", [128, 4])
        ipa_k = late.take([D, B, H * IPA])
        ipa_v = sb("ipa_v", [H * IPA, B, D])
        ipa_s = sb("ipa_s", [128, 2, H, IPA])
        ipa_max = sb("ipa_max", [128, 2, H])
        ipa_sum = sb("ipa_sum", [128, 2, H])
        ipa_pT = sb("ipa_pT", [H * IPA, 2, 128])
        early.again()
        wki = early.take([C, ID])
        wvi = early.take([C, ID])
        down = early.take([128, 3, RANK])
        down_o = early.take([128, 8, RANK])
        downT = early.take([RANK, 3 + 8, 128])
        up = early.take([RANK, 3, ID])
        up_o = early.take([RANK, D])
        ctx_ipa = early.take([B * IPA, C])
        ctx_ipaT = early.take([C, B * IPA])
        ipa_kT = early.take([128, 8, B, 2, IPA])
        ipa_vT = early.take([128, 8, B, 2, IPA])
        wq1T = early.take([128, 8, D])
        wk1T = early.take([128, 8, C])
        ipa_v_rows = early.take([128, 8, D])
        early.again()
        rw1 = early.take([D, D])
        rw2 = early.take([D, E1])
        rw2_wide = early.take([D, 8 * (D + E1)])
        ew1 = early.take([D, 4, F1])
        ew2 = early.take([D, 4, F1])
        ew3 = early.take([128, 4, F1 // 128, D])
        count_i = early.take([128, 128], I32)
        count = early.take([128, 128])
        eo_all = early.take([128, B, EG, D])
        xn_all = early.take([128, B, D])
        late.again()
        xgT = late.take([D, B, E1, CAP])
        hs = late.take([128, 2, 2, 512])
        late_mark = late.at
        oh_bf = late.take([128, 2, EG, 128], BF16)
        late.at = late_mark
        sg = late.take([128, 2, 512])
        xT4, hT4 = pT, oT
        oh = kT
        ohw = oT
        probs = sb("probs", [128, 2, 128])
        ex_max = sb("ex_max", [128, 2, 1])
        ex_sum = sb("ex_sum", [128, 2, 1])
        top = sb("top", [128, 2, CAP])
        top_at = sb("top_at", [128, 2, CAP], mybir.dt.uint32)
        top_at_f = sb("top_at_f", [128, 2, CAP])
        slot_at = sb("slot_at", [128, B, EG])
        slot_w = sb("slot_w", [128, B, EG])
        ipa_v_dram = nc.dram_tensor("ipa_v_scratch", (B, 2 * IPA, 8, D), F32, kind="Internal").ap()

        block = ctx.enter_context(nc.Block())

        made = named(sem, "made", "consts ident pick hmask vm")
        got = named(sem, "got", "x ctx attn0 ffn0 attn1 ipa route stored")
        ln = named(sem, "ln", "stats mv veps rstd")
        phase_end = sem("phase_end")
        A = named(sem, "a", "ctx_in xn tr xc_T qk qm km v q_sb k_sb v_sb q_bf k_bf smax maxed negT negT_sb "
                            "score exp pv rsum o oTr oT_sb proj x_new stats")

        F = named(sem, "f", "gate_tr gateT lower xn tr xT logit y step ex w ysum ys0 x_new stats")
        FSTEPS = 11

        W = named(sem, "w", "wk1T_ps wk1T mT_ps mT turned downT alpha folded wq1T_ps wq1T ctxT_ps ctxT kv_ps kT vT zeros prod ipa_k ipa_v_rows out back")
        Z = named(sem, "z", "ctx_in xn tr xc_T x_bf k0 k1 k2 k3 v0 v1 k0_sb k1_sb k2_sb k3_sb v0_sb v1_sb k_bf "
                            "smax maxed negT negT_sb score exp pv rsum o oTr0 oTr1 oT_sb proj x_new stats "
                            "ipa_score ipa_step ipa_sub ipa_exp ipa_p ipa_turn ipa_pT")

        R = named(sem, "r", "wide count xn tr xT hid h logit step ex turned slot")
        G = named(sem, "g", "xn row turned oh got xg")
        X1 = named(sem, "x", "w0 w1 w2 w3 gv silu h eo eo_act eo_dve")
        w_in = (X1.w0, X1.w1, X1.w2, X1.w3)
        Y = named(sem, "y", "row sum x_new stored")

        def engines_meet(eng, n):
            eng.drain().then_inc(phase_end, 1)
            eng.wait_ge(phase_end, 5 * n)

        def act_exp(act, Z, keys, width, b, j):
            act.wait_ge(Z.score, b * NCH + j + 1)
            after(act, Z.pv, b * NCH + j - 1)
            act.activation(pT[0:keys, j % 2, :, :], blocks(SCB[j % 2], keys), ACT.Exp,
                           scale=float(width) ** -0.5).then_inc(Z.exp, 1)

        def dve_max(dve, Z, f, j, column, keys):
            dve.wait_ge(Z.smax, f * NCH + j + 1)
            after(dve, Z.negT, f)
            dve.tensor_reduce(negmax[:, column:column + CH], blocks(MAXB)[:, :, 0:keys], X, ALU.max,
                              negate=True).then_inc(Z.maxed, 1)

        def dve_negmaxT(dve, Z, f, uf, width):
            dve.wait_ge(Z.negT, f + 1)
            dve.tensor_copy(negmaxT[0:width, uf, :], TB[0:width, 0:128]).then_inc(Z.negT_sb, 1)

        def dve_xn(dve, Z, b, u):
            dve.tensor_scalar(xn[:, u, :], x_all[:, b, :], mv[:, b, 0:1], rstd[:, b, :],
                              ALU.subtract, ALU.mult).then_inc(Z.xn, 1)

        def dve_residual(dve, Z, t, add):
            dve.tensor_tensor(x_all[:, t, :], add, x_all[:, t, :], ALU.add).then_inc(Z.x_new, 1)
            dve.wait_ge(Z.x_new, t + 1)

        def dve_stats(dve, Z, t):
            dve.bn_stats(stats[:, t, :], x_all[:, t, :]).then_inc(Z.stats, 1)

        def pe_transpose_in(pe, Z, to, f, uf, freed):
            pe.wait_ge(Z.xn, f + 1)
            pe.wait_ge(Z.ctx_in, f + 1)
            after(pe, Z.v_sb, freed)
            pe.transpose(to[:, 0:128], xn[:, uf, :], ident[:, :])
            pe.transpose(to[0:C, 128:256], ctx_in[:, uf, :], ident[:, :]).then_inc(Z.tr, 1)

        def act_transposed_in(act, Z, of, f, uf):
            act.wait_ge(Z.tr, f + 1)
            act.activation(xT[:, uf, :], of[:, 0:128], ACT.Copy).then_inc(Z.xc_T, 1)
            act.activation(cT[:, uf, :], of[0:C, 128:256], ACT.Copy).then_inc(Z.xc_T, 1)

        def pool_ctx(pool, Z, b, u):
            after(pool, Z.tr, b - 1)
            pool.tensor_copy(ctx_in[:, u, :], ctx_all[:, b, :]).then_inc(Z.ctx_in, 1)



        def experts(eng, first, body):
            first(0, 0, 0)
            with eng.Fori(0, EG - 1) as i:
                for q in range(4):
                    body(i * 4 + q, i, q)
            for q in range(4):
                body(E1 - 4 + q, EG - 1, q)

        def rw2_of(b):
            return rw2_wide[:, 128 * (b % 8):128 * (b % 8) + 128]

        def eo_got(q, half, n):
            return bank[4 + 2 * (q % 2) + half][32 * n:32 * n + 32, 0:2 * D].rearrange("p (k d) -> p k d", k=2)

        def eo_rows(g, q, half, n):
            return eo_all[32 * q:32 * q + 32, :, :, :].rearrange("p (h k n) g d -> p h n g k d", h=2, k=2)[:, half, n, g, :, :]

        @block.sync
        def _(sp):
            sp.dma_start(x_all[:, :, :], T["x"].rearrange("b s d -> s b d")).then_inc(got.x, 16)
            sp.dma_start(ctx_all[:, :, :], T["ctx_768"].rearrange("b s c -> s b c")).then_inc(got.ctx, 16)
            sp.dma_start(wq0[:, :], T["L0_xattn_wq"]).then_inc(got.attn0, 16)
            sp.dma_start(wk0[:, :], T["L0_xattn_wk"]).then_inc(got.attn0, 16)
            for bias, name in ((bq0, "L0_xattn_bq"), (bk0, "L0_xattn_bk")):
                sp.dma_start(bias[:, :], T[name].rearrange("(p a) -> p a", a=1)).then_inc(got.attn0, 16)
            sp.dma_start(wv0[:, :], T["L0_xattn_wv"]).then_inc(got.attn0, 16)
            sp.dma_start(bv0[:, :], T["L0_xattn_bv"].rearrange("(a n) -> a n", a=1).broadcast_to((128, D))).then_inc(got.attn0, 16)
            sp.dma_start(wo0[:, :, :], T["L0_xattn_wo"].rearrange("(a p) n -> p a n", a=2)).then_inc(got.attn0, 16)
            sp.dma_start(bo0[:, :], T["L0_xattn_bo"].rearrange("(a n) -> a n", a=1)).then_inc(got.attn0, 16)
            sp.dma_start(gate_in[:, :], T["L0_ffn_gate_w"]).then_inc(got.ffn0, 16)
            sp.dma_start(we[:, :, :], T["L0_ffn_We"].rearrange("e d m -> d e m")).then_inc(got.ffn0, 16)
            for w, name in ((wq1, "Wq"), (wk1, "Wk"), (wv1, "Wv")):
                sp.dma_start(w[:, :], T["L1_xattn_" + name]).then_inc(got.attn1, 16)
            sp.dma_start(wo1[:, :, :], T["L1_xattn_Wo"].rearrange("(c p) n -> p c n", p=128)).then_inc(got.attn1, 16)
            sp.dma_start(bo1[:, :], T["L1_xattn_bo"].rearrange("(a n) -> a n", a=1)).then_inc(got.attn1, 16)
            for n, name in enumerate("qkvo"):
                sp.dma_start(alpha[:, n:n + 1], T[f"L1_xattn_{name}_alpha"].rearrange("(a n) -> a n", a=1)
                             .broadcast_to((128, 1))).then_inc(got.attn1, 16)
            engines_meet(sp, 1)
            engines_meet(sp, 2)
            for n, (name, rows) in enumerate((("q", D), ("k", C), ("v", C))):
                sp.dma_start(down[0:rows, n, :], T[f"L1_xattn_{name}_down"]).then_inc(got.attn1, 16)
                sp.dma_start(up[:, n, :], T[f"L1_xattn_{name}_up"]).then_inc(got.attn1, 16)
            sp.dma_start(down_o[:, :, :], T["L1_xattn_o_down"].rearrange("(c p) r -> p c r", p=128)).then_inc(got.attn1, 16)
            sp.dma_start(up_o[:, :], T["L1_xattn_o_up"]).then_inc(got.attn1, 16)
            sp.dma_start(ctx_ipa[:, :], T["ctx_768"][:, ORG:S, :].rearrange("b j c -> b j c")).then_inc(got.attn1, 16)
            sp.dma_start(wki[:, :], T["L1_xattn_Wk_ipa"]).then_inc(got.attn1, 16)
            sp.dma_start(wvi[:, :], T["L1_xattn_Wv_ipa"]).then_inc(got.attn1, 16)
            sp.wait_ge(W.ipa_v_rows, 2)
            sp.dma_start(ipa_v_dram.rearrange("b r c n -> (b r) c n"), ipa_v_rows[:, :, :]).then_inc(W.out, 16)
            sp.wait_ge(W.out, 16)
            for c in range(8):
                sp.dma_start(ipa_v[8 * c:8 * c + 8, :, :], ipa_v_dram[:, :, c, :].rearrange("b r n -> r b n"))\
                    .then_inc(W.back, 16)
            engines_meet(sp, 3)
            sp.dma_start(rw1[:, :], T["L1_ffn_router_w1"]).then_inc(got.route, 16)
            sp.dma_start(rw2[:, :], T["L1_ffn_router_w2"]).then_inc(got.route, 16)

            def expert_weights(e, q):
                for slot, w in ((ew1, "L1_ffn_w1"), (ew2, "L1_ffn_w2")):
                    sp.dma_start(slot[:, q, :], T[w][e, :, :]).then_inc(w_in[q], 16)
                sp.dma_start(ew3[:, q, :, :], T["L1_ffn_w3"].rearrange("e (c p) n -> e p c n", p=128)[e, :, :, :])\
                    .then_inc(w_in[q], 16)
            for q in range(4):
                expert_weights(q, q)
            engines_meet(sp, 4)
            engines_meet(sp, 5)
            with sp.Fori(0, EG - 1) as i:
                for q in range(4):
                    sp.wait_ge(X1.eo, i * 4 + q + 1)
                    expert_weights(i * 4 + (q + 4), q)
            engines_meet(sp, 6)
            with sp.Fori(0, B) as b:
                sp.wait_ge(Y.x_new, b + 1)
                sp.dma_start(out[b, :, :], x_all[:, b, :]).then_inc(Y.stored, 16)
            sp.wait_ge(Y.stored, 16 * B)

        @block.gpsimd
        def _(pool):
            pool.memset(minus_half[:, :], -0.5).then_inc(made.consts, 1)
            pool.memset(ident[:, :], 0.0).then_inc(made.ident, 1)
            pool.memset(ident_bf[:, :], 0.0).then_inc(made.ident, 1)
            pool.memset(pick[:, :, :], 0.0).then_inc(made.pick, 1)
            pool.wait_ge(made.ident, 2)
            for m in (ident, ident_bf):
                pool.affine_select(out=m[:, :], in_=m[:, :], compare_op=ALU.not_equal, fill=1.0, base=0,
                                   pattern=[[-1, 128]], channel_multiplier=1).then_inc(made.ident, 1)
            pool.memset(ones_row[:, :], 1.0).then_inc(made.ident, 1)
            for j in range(2):
                pool.wait_ge(made.pick, j + 1)
                pool.affine_select(out=pick[:, :, :], in_=pick[:, :, :], compare_op=ALU.not_equal, fill=1.0,
                                   base=-64 * j, pattern=[[-1, H], [0, 128]], channel_multiplier=1)\
                    .then_inc(made.pick, 1)
            pool.memset(hmask[:, :], 1.0).then_inc(made.hmask, 1)
            for base, way in ((0, 1), (D0 - 1, -1)):
                pool.wait_ge(made.hmask, 1 if way == 1 else 2)
                pool.affine_select(out=hmask[:, :], in_=hmask[:, :], compare_op=ALU.is_ge, fill=0.0, base=base,
                                   pattern=[[-D0 * way, H]], channel_multiplier=way).then_inc(made.hmask, 1)
            pool.memset(negmax[:, :], 0.0).then_inc(made.consts, 1)
            pool.wait_ge(got.ctx, 16)

            def rstds(n):
                pool.wait_ge(ln.veps, n)
                pool.tensor_tensor(rstd[:, :, 0], veps[:, :], minus_half[:, :], ALU.pow).then_inc(ln.rstd, 1)
            rstds(1)

            def body(b, u):
                f, uf = b + 1, 1 - u
                if isinstance(b, int) and b == -1:
                    pool_ctx(pool, A, 0, 0)
                    pool_ctx(pool, A, 1, 1)
                if there(b + 2) and not (isinstance(b, int) and b == -1):
                    pool_ctx(pool, A, b + 2, u)
            pipelined(pool, body)
            engines_meet(pool, 1)
            rstds(2)
            pool.memset(lower[:, :, :], 1.0).then_inc(F.lower, 1)
            pool.wait_ge(F.lower, 1)
            pool.affine_select(out=lower[:, :, :], in_=lower[:, :, :], compare_op=ALU.is_ge, fill=0.0, base=-1,
                               pattern=[[1, E0], [-1, E0]], channel_multiplier=0).then_inc(F.lower, 1)
            engines_meet(pool, 2)
            rstds(3)
            pool.memset(ipa_kT[:, :, :, :, :], 0.0).then_inc(W.zeros, 1)
            pool.memset(ipa_vT[:, :, :, :, :], 0.0).then_inc(W.zeros, 1)
            pool.memset(v1[:, :, :, D1:D1 + 1], 1.0).then_inc(W.zeros, 1)
            pool.memset(negmax[:, :], 0.0).then_inc(W.zeros, 1)
            engines_meet(pool, 3)
            pool.memset(rw2_wide[:, :], 0.0).then_inc(R.wide, 1)
            pool.iota(count_i[:, :], [[1, 128]], base=0, channel_multiplier=0).then_inc(R.count, 1)
            pool.wait_ge(R.count, 1)
            pool.tensor_copy(count[:, :], count_i[:, :]).then_inc(R.count, 1)
            pool.wait_ge(got.route, 32)
            pool.wait_ge(R.wide, 1)
            pool.tensor_copy(rw2_wide[:, :].rearrange("p (b n) -> p b n", b=8)[:, :, 0:E1],
                             rw2[:, :].unsqueeze(1).broadcast_to((D, 8, E1))).then_inc(R.wide, 1)

            def body(b, u):
                f, uf = b + 1, 1 - u
                if isinstance(b, int) and b == -1:
                    pool_ctx(pool, Z, 0, 0)
                    pool_ctx(pool, Z, 1, 1)
                if there(b + 2) and not (isinstance(b, int) and b == -1):
                    pool_ctx(pool, Z, b + 2, u)
            pipelined(pool, body)
            engines_meet(pool, 4)
            rstds(4)
            engines_meet(pool, 5)
            engines_meet(pool, 6)

        @block.vector
        def _(dve):
            dve.wait_ge(got.x, 16)

            for b in range(B):
                dve_stats(dve, ln, b)

            def variances(stats_done, n):
                dve.wait_ge(stats_done, B)
                for b in range(B):
                    dve.bn_aggr(mv[:, b, :], stats[:, b, :]).then_inc(ln.mv, 1)
                dve.wait_ge(ln.mv, n * B)
                dve.tensor_scalar(veps[:, :], mv[:, :, 1], EPS, None, ALU.add).then_inc(ln.veps, 1)
            variances(ln.stats, 1)
            dve.memset(vm[:, :, :, :, :], 0.0).then_inc(made.vm, 1)
            dve.wait_ge(made.vm, 1)
            dve.memset(vm[:, :, :, :, 64:64 + D0], 1.0).then_inc(made.vm, 1)
            dve.wait_ge(got.attn0, 16 * 8)
            dve.wait_ge(made.consts, 2)
            dve.wait_ge(made.hmask, 3)
            dve.wait_ge(ln.rstd, 1)
            dve_xn(dve, A, 0, 0)

            def norm(t, ut):
                dve.wait_ge(A.pv, t * NCH + NCH)
                dve.reciprocal(rsum0[:, ut, :, :], OB[ut][64:128, 0:256].rearrange("p (a n) -> p a n", a=2))\
                    .then_inc(A.rsum, 1)
                dve.wait_ge(A.rsum, t + 1)
                dve.tensor_tensor(o0T[:, ut, :, :], OB[ut][0:64, 0:256].rearrange("p (a n) -> p a n", a=2),
                                  rsum0[:, ut, :, :], ALU.mult).then_inc(A.o, 1)

            def body(b, u):
                f, t, uo = b + 1, b - 1, 1 - u
                if there(t):
                    norm(t, uo)
                if there(f):
                    dve.wait_ge(A.q_sb, f + 1)
                    dve.tensor_tensor(qm[:, uo, :, :], qT[:, uo, :].unsqueeze(1).broadcast_to((128, H, 128)),
                                      hmask[:, :].unsqueeze(2).broadcast_to((128, H, 128)), ALU.mult)\
                        .then_inc(A.qm, 1)
                    dve.wait_ge(A.v, f + 1)
                    dve.tensor_tensor(vm[:, uo, :, :, 0:D0],
                                      PB[1][:, 0:D].rearrange("p (a h d) -> p a h d", a=2, h=8),
                                      bv0[:, :].rearrange("p (a h d) -> p a h d", a=2, h=8), ALU.add)\
                        .then_inc(A.v_sb, 1)
                if there(t):
                    dve.wait_ge(A.proj, t + 1)
                    dve_residual(dve, A, t, TB[:, 0:D])
                if there(f):
                    dve_max(dve, A, f, 0, 0, S)
                if there(t):
                    dve_stats(dve, A, t)
                if there(f):
                    for j in range(1, NCH):
                        dve_max(dve, A, f, j, CH * j, S)
                    dve_negmaxT(dve, A, f, uo, H)
                if there(b + 2):
                    dve_xn(dve, A, b + 2, u)
            pipelined(dve, body)
            engines_meet(dve, 1)
            variances(A.stats, 2)
            dve.wait_ge(F.gate_tr, 1)
            dve.tensor_copy(gateT[:, :], TB[:, 0:E0]).then_inc(F.gateT, 1)
            dve.wait_ge(F.lower, 2)
            dve.wait_ge(ln.rstd, 2)
            dve_xn(dve, F, 0, 0)
            dve_xn(dve, F, 1, 1)

            def ffn0(b, u):
                def step(k, ins):
                    ins.then_inc(F.step, 1)
                    dve.wait_ge(F.step, b * FSTEPS + k)

                dve.wait_ge(F.logit, b + 1)
                step(1, dve.tensor_copy(lg[:, u, :], PB[u][:, 0:E0]))
                mine = lg[:, u, :].unsqueeze(2).broadcast_to((128, E0, E0))
                other = lg[:, u, :].unsqueeze(1).broadcast_to((128, E0, E0))
                step(2, dve.tensor_reduce(negtop[:, u, :], lg[:, u, :], X, ALU.max, negate=True))
                dve.tensor_tensor(beat[:, u, :, :], other, mine, ALU.is_gt).then_inc(F.step, 1)
                step(4, dve.tensor_tensor(tie[:, u, :, :], other, mine, ALU.is_ge))
                step(5, dve.tensor_tensor(tie[:, u, :, :], tie[:, u, :, :], lower[:, :, :], ALU.mult))
                step(6, dve.tensor_tensor(beat[:, u, :, :], beat[:, u, :, :], tie[:, u, :, :], ALU.max))
                step(7, dve.tensor_reduce(nbeat[:, u, :], beat[:, u, :, :], X, ALU.add))
                dve.wait_ge(F.ex, b + 1)
                step(8, dve.scalar_tensor_tensor(ew[:, u, :], nbeat[:, u, :], 1.5, ew[:, u, :], ALU.is_lt, ALU.mult))
                step(9, dve.tensor_reduce(wsum[:, u, :], ew[:, u, :], X, ALU.add))
                step(10, dve.reciprocal(wsum[:, u, :], wsum[:, u, :]))
                dve.tensor_scalar(ffn_w[:, u, :], ew[:, u, :], wsum[:, u, :], None, ALU.mult).then_inc(F.w, 1)
                dve.wait_ge(F.w, b + 1)
                dve.wait_ge(F.y, b + 1)
                half = E0 // 2
                dve.tensor_tensor(ys[:, u, half:E0, :], blocks((SCB, OB)[u][1]),
                                  ffn_w[:, u, half:E0].unsqueeze(2).broadcast_to((128, half, D)), ALU.mult)\
                    .then_inc(F.step, 1)
                dve.wait_ge(F.step, b * FSTEPS + 11)
                dve.wait_ge(F.ys0, 4 * b + 4)
                dve.tensor_reduce(ysum[:, u, :], ys[:, u, :, :].rearrange("p e d -> p d e"), X, ALU.add)\
                    .then_inc(F.ysum, 1)
                dve.wait_ge(F.ysum, b + 1)
                dve_residual(dve, F, b, ysum[:, u, :])

            def body(b, u):
                ffn0(b, u)
                if there(b + 2):
                    dve_xn(dve, F, b + 2, u)
                dve_stats(dve, F, b)
            with dve.Fori(0, B // 2 - 1) as i:
                body(i * 2, 0)
                body(i * 2 + 1, 1)
            body(B - 2, 0)
            body(B - 1, 1)
            engines_meet(dve, 2)
            variances(F.stats, 3)

            dve.wait_ge(got.attn1, 16 * 20)
            dve.tensor_scalar(alpha[:, :], alpha[:, :], 1.0 / RANK, None, ALU.mult).then_inc(W.alpha, 1)
            dve.wait_ge(W.turned, 3)
            dve.tensor_copy(downT[:, 0, :], PB[0][0:RANK, 0:128])
            dve.tensor_copy(downT[:, 1:3, 0:C], blocks(PB[0], RANK)[:, 1:3, 0:C]).then_inc(W.downT, 1)
            for n in range(2):
                dve.tensor_copy(downT[:, 3 + 4 * n:7 + 4 * n, :], blocks(SCB[n], RANK)).then_inc(W.downT, 1)
            dve.wait_ge(W.alpha, 1)
            for n, (w, rows) in enumerate(((wq1, D), (wk1, C), (wv1, C))):
                for half in range(2):
                    part = w[:, 512 * half:512 * half + 512]
                    dve.wait_ge(W.prod, 2 * n + half + 1)
                    dve.scalar_tensor_tensor(part, bank[2 * n + half][0:rows, :], alpha[0:rows, n:n + 1], part,
                                             ALU.mult, ALU.add).then_inc(W.folded, 1)
            for half in range(2):
                part = wo1[:, 4 * half:4 * half + 4, :]
                dve.wait_ge(W.prod, 7 + half)
                dve.scalar_tensor_tensor(part, blocks(bank[6 + half]), alpha[:, 3:4], part,
                                         ALU.mult, ALU.add).then_inc(W.folded, 1)
            dve.wait_ge(W.ctxT_ps, 1)
            dve.tensor_copy(ctx_ipaT[:, :], bank[0][0:C, 0:B * IPA]).then_inc(W.ctxT, 1)
            for n in range(2):
                dve.wait_ge(W.wq1T_ps, n + 1)
                dve.tensor_copy(wq1T[:, 4 * n:4 * n + 4, :], blocks(bank[1 + n])).then_inc(W.wq1T, 1)
            for n in range(2):
                dve.wait_ge(W.wk1T_ps, n + 1)
                dve.tensor_copy(wk1T[:, 4 * n:4 * n + 4, :], bank[1 + n][:, 0:4 * C].rearrange("p (c k) -> p c k", c=4))\
                    .then_inc(W.wk1T, 1)
            for n in range(4):
                dve.wait_ge(W.mT_ps, n + 1)
                dve.tensor_copy(mT[:, :, :].rearrange("c (n g t) d -> c n t g d", n=2, t=2)[:, n // 2, n % 2, :, :],
                                blocks(bank[6 + n % 2], C)).then_inc(W.mT, 1)
            dve.wait_ge(W.zeros, 4)
            for n, (to, done) in enumerate(((ipa_kT, W.kT), (ipa_vT, W.vT))):
                dve.wait_ge(W.kv_ps, n + 1)
                for two in range(2):
                    rows = slice(64 * two, 64 * two + 64)
                    dve.tensor_copy(to[rows, :, :, two, :], bank[3 + n][rows, :].rearrange(
                        "p (c b j) -> p c b j", c=8, b=B)).then_inc(done, 1)
            for n in range(2):
                dve.wait_ge(W.prod, 9 + n)
                dve.tensor_copy(ipa_k[:, :, 32 * n:32 * n + 32].rearrange("p b (c r) -> p c b r", c=4),
                                bank[5 + n][:, :].rearrange("p (c b r) -> p c b r", c=4, b=B)).then_inc(W.ipa_k, 1)
            for n in range(2):
                dve.wait_ge(W.prod, 11 + n)
                dve.tensor_copy(ipa_v_rows[:, 4 * n:4 * n + 4, :], blocks(bank[(7, 0)[n]])).then_inc(W.ipa_v_rows, 1)
            engines_meet(dve, 3)

            dve.wait_ge(ln.rstd, 3)
            dve_xn(dve, Z, 0, 0)

            def norm(b, u, j):
                dve.wait_ge(Z.pv, b * NCH + j + 1)
                got_o = OB[j % 2][:, 0:CH * (D1 + 1)].rearrange("p (h d) -> p h d", h=CH)
                sums = rsum[:, u, CH * j:CH * j + CH]
                dve.reciprocal(sums, got_o[:, :, D1]).then_inc(Z.rsum, 1)
                dve.wait_ge(Z.rsum, b * NCH + j + 1)
                dve.tensor_tensor(o[:, u, CH * D1 * j:CH * D1 * (j + 1)].rearrange("p (h d) -> p h d", h=CH),
                                  got_o[:, :, 0:D1], sums.unsqueeze(2).broadcast_to((128, CH, D1)), ALU.mult)\
                    .then_inc(Z.o, 1)

            def ipa_scores(f, uf):
                dve.wait_ge(Z.ipa_score, f + 1)
                sc = TB[:, 0:H * IPA].rearrange("p (h j) -> p h j", h=H)
                dve.tensor_reduce(ipa_max[:, uf, :], sc, X, ALU.max).then_inc(Z.ipa_step, 1)
                dve.wait_ge(Z.ipa_step, f * 3 + 1)
                dve.tensor_tensor(ipa_s[:, uf, :, :], sc, ipa_max[:, uf, :].unsqueeze(2).broadcast_to((128, H, IPA)),
                                  ALU.subtract).then_inc(Z.ipa_sub, 1)

            def ipa_norm(f, uf):
                dve.wait_ge(Z.ipa_exp, f + 1)
                dve.tensor_reduce(ipa_sum[:, uf, :], ipa_s[:, uf, :, :], X, ALU.add).then_inc(Z.ipa_step, 1)
                dve.wait_ge(Z.ipa_step, f * 3 + 2)
                dve.reciprocal(ipa_sum[:, uf, :], ipa_sum[:, uf, :]).then_inc(Z.ipa_step, 1)
                dve.wait_ge(Z.ipa_step, f * 3 + 3)
                dve.tensor_tensor(ipa_s[:, uf, :, :], ipa_s[:, uf, :, :],
                                  ipa_sum[:, uf, :].unsqueeze(2).broadcast_to((128, H, IPA)), ALU.mult)\
                    .then_inc(Z.ipa_p, 1)

            def body(b, u):
                f, t, uo = b + 1, b - 1, 1 - u
                if there(t):
                    norm(t, uo, 3)
                if there(f):
                    ipa_scores(f, uo)
                    dve.wait_ge(Z.k0, f + 1)
                    dve.tensor_copy(kT[:, uo, 0:4, 0:ORG], blocks(PB[0])[:, :, 0:ORG]).then_inc(Z.k0_sb, 1)
                if there(b):
                    norm(b, u, 0)
                if there(f):
                    dve.wait_ge(Z.k2, f + 1)
                    dve.tensor_copy(kT[:, uo, 8:12, 0:ORG], blocks(PB[0])[:, :, 0:ORG]).then_inc(Z.k2_sb, 1)
                    ipa_norm(f, uo)
                if there(t):
                    dve.wait_ge(Z.proj, t + 1)
                    dve_residual(dve, Z, t, TB[:, 0:D])
                if there(f):
                    dve_max(dve, Z, f, 0, 0, ORG)
                if there(t):
                    dve_stats(dve, Z, t)
                if there(f):
                    dve.wait_ge(Z.v0, f + 1)
                    dve.tensor_copy(v1[0:ORG, uo, 0:8, 0:D1], PB[0][0:ORG, :].rearrange("p (h d) -> p h d", h=8))\
                        .then_inc(Z.v0_sb, 1)
                if there(b):
                    norm(b, u, 1)
                if there(f):
                    dve_max(dve, Z, f, 1, CH, ORG)
                    dve_max(dve, Z, f, 2, 2 * CH, ORG)
                    dve.wait_ge(Z.ipa_turn, f + 1)
                    dve.tensor_copy(ipa_pT[:, uo, :], TB[0:H * IPA, 0:128]).then_inc(Z.ipa_pT, 1)
                    dve_max(dve, Z, f, 3, 3 * CH, ORG)
                if there(b):
                    norm(b, u, 2)
                if there(f):
                    dve_negmaxT(dve, Z, f, uo, H)
                if there(b + 2):
                    dve_xn(dve, Z, b + 2, u)
            pipelined(dve, body)
            engines_meet(dve, 4)
            variances(Z.stats, 4)

            dve.wait_ge(ln.rstd, 4)
            for b in range(B):
                dve.tensor_scalar(xn_all[:, b, :], x_all[:, b, :], mv[:, b, 0:1], rstd[:, b, :],
                                  ALU.subtract, ALU.mult).then_inc(R.xn, 1)
            steps = 0

            def step(ins):
                nonlocal steps
                steps += 1
                ins.then_inc(R.step, 1)
                dve.wait_ge(R.step, steps)
            for t in range(2):
                dve.wait_ge(R.logit, t + 1)
                step(dve.tensor_reduce(ex_max[:, t, :], bank[4 + t][:, 0:128], X, ALU.max, negate=True))
                dve.wait_ge(R.ex, t + 1)
                step(dve.tensor_reduce(ex_sum[:, t, :], probs[:, t, :], X, ALU.add))
                step(dve.reciprocal(ex_sum[:, t, :], ex_sum[:, t, :]))
                step(dve.tensor_scalar(probs[:, t, :], probs[:, t, :], ex_sum[:, t, :], None, ALU.mult))
                for n in range(CAP // 8):
                    eight = slice(8 * n, 8 * n + 8)
                    step(dve.max(top[:, t, eight], probs[:, t, :]))
                    step(dve.max_index(top_at[:, t, eight], top[:, t, eight], probs[:, t, :]))
                    if n < CAP // 8 - 1:
                        step(dve.match_replace(probs[:, t, :], top[:, t, eight], probs[:, t, :], -1.0))
                step(dve.tensor_copy(top_at_f[:, t, :], top_at[:, t, :]))
                step(dve.tensor_reduce(ex_sum[:, t, :], top[:, t, :], X, ALU.add))
                step(dve.tensor_scalar(ex_sum[:, t, :], ex_sum[:, t, :], 1e-9, None, ALU.add))
                step(dve.reciprocal(ex_sum[:, t, :], ex_sum[:, t, :]))
                step(dve.tensor_scalar(top[:, t, :], top[:, t, :], ex_sum[:, t, :], None, ALU.mult))
            for t in range(2):
                dve.wait_ge(R.turned, t + 1)
                for n, to in enumerate((slot_at, slot_w)):
                    dve.tensor_copy(to[:, 8 * t:8 * t + 8, :],
                                    bank[6 + t][:, 32 * n:32 * n + 32].rearrange("p (b g) -> p b g", b=8))\
                        .then_inc(R.slot, 1)
            dve.wait_ge(R.slot, 4)
            dve.wait_ge(R.count, 2)

            def body(b, u):
                after(dve, G.got, b - 1)
                dve.tensor_scalar(xn[:, u, :], x_all[:, b, :], mv[:, b, 0:1], rstd[:, b, :],
                                  ALU.subtract, ALU.mult).then_inc(G.xn, 1)
                for g in range(EG):
                    ins = dve.tensor_scalar(oh_bf[:, u, g, :], count[:, :], slot_at[:, b, g:g + 1], None, ALU.is_equal)
                ins.then_inc(G.row, 1)
                t = b - 1
                if there(t):
                    dve.wait_ge(G.got, t + 1)
                    dve.tensor_copy(xgT[:, t, :, :], bank[2 + (1 - u)][:, :].rearrange("p (e s) -> p e s", e=E1))\
                        .then_inc(G.xg, 1)
            body(0, 0)
            body(1, 1)
            with dve.Fori(0, B // 2 - 1) as i:
                body(i * 2 + 2, 0)
                body(i * 2 + 3, 1)
            dve.wait_ge(G.got, B)
            dve.tensor_copy(xgT[:, B - 1, :, :], bank[3][:, :].rearrange("p (e s) -> p e s", e=E1)).then_inc(G.xg, 1)
            engines_meet(dve, 5)

            def gated(e, g, q):
                for c in range(2):
                    dve.wait_ge(X1.silu, 2 * e + c + 1)
                    dve.tensor_tensor(hs[:, q % 2, c, :], sg[:, c, :], bank[2 * c + 1][:, :], ALU.mult)\
                        .then_inc(X1.h, 1)

            def body(e, g, q):
                if there_expert(e + 1):
                    gated(e + 1, g, q + 1)
                dve.wait_ge(X1.eo, e + 1)
                for n in range(4):
                    ins = dve.tensor_copy(eo_rows(g, q, 1, n), eo_got(q, 1, n))
                ins.then_inc(X1.eo_dve, 1)
            dve.drain().then_inc(X1.eo_dve, 2)
            experts(dve, gated, body)
            engines_meet(dve, 6)

            def body(b, u):
                after(dve, Y.sum, b - 1)
                for g in range(EG):
                    ins = dve.tensor_scalar(ohw[:, u, g, :], count[:, :], slot_at[:, b, g:g + 1],
                                            slot_w[:, b, g:g + 1], ALU.is_equal, ALU.mult)
                ins.then_inc(Y.row, 1)
                t = b - 1
                if there(t):
                    residual(t, 1 - u)

            def residual(t, ut):
                dve.wait_ge(Y.sum, t + 1)
                dve.tensor_tensor(x_all[:, t, :], bank[ut][:, 0:D], x_all[:, t, :], ALU.add).then_inc(Y.x_new, 1)
            body(0, 0)
            body(1, 1)
            with dve.Fori(0, B // 2 - 1) as i:
                body(i * 2 + 2, 0)
                body(i * 2 + 3, 1)
            residual(B - 1, 1)

        @block.scalar
        def _(act):
            act.preload_act_table(ACT.Exp)
            act.wait_ge(got.attn0, 16 * 8)
            act.wait_ge(made.hmask, 3)

            def body(b, u):
                f, uf = b + 1, 1 - u
                if there(f):
                    act_transposed_in(act, A, PB[1], f, uf)
                if there(b):
                    act_exp(act, A, S, D0, b, 0)
                if there(f):
                    act.wait_ge(A.qk, f + 1)
                    act.activation(qT[:, uf, :], PB[0][:, 0:128], ACT.Identity, bias=bq0[:, :])\
                        .then_inc(A.q_sb, 1)
                    act.activation(q_bf[:, uf, :], PB[0][:, 0:128], ACT.Identity, bias=bq0[:, :])\
                        .then_inc(A.q_bf, 1)
                    act.activation(kT[:, uf, 0, :], PB[0][:, 128:256], ACT.Identity, bias=bk0[:, :])\
                        .then_inc(A.k_sb, 1)
                    act.wait_ge(A.k_sb, f + 1)
                    for h in range(H):
                        if h == 8 and there(b):
                            act_exp(act, A, S, D0, b, 1)
                        ins = act.activation(km_bf[:, uf, h, :], kT[:, uf, 0, :], ACT.Copy, scale=hmask[:, h:h + 1])
                        if h % CH == CH - 1:
                            ins.then_inc(A.km, 1)
                elif there(b):
                    act_exp(act, A, S, D0, b, 1)
                if there(b):
                    act_exp(act, A, S, D0, b, 2)
                    act_exp(act, A, S, D0, b, 3)
            pipelined(act, body)
            engines_meet(act, 1)

            def body(b, u):
                if there(b):
                    act.wait_ge(F.tr, b + 1)
                    act.activation(xT[:, u, :], (TB, MAXB)[u][:, 0:128], ACT.Copy).then_inc(F.xT, 1)
                t, ut = b - 1, 1 - u
                if there(t):
                    act.wait_ge(F.step, t * FSTEPS + 2)
                    act.activation(ew[:, ut, :], lg[:, ut, :], ACT.Exp, bias=negtop[:, ut, :]).then_inc(F.ex, 1)
                    act.wait_ge(F.w, t + 1)
                    act.wait_ge(F.y, t + 1)
                    for e in range(E0 // 2):
                        act.activation(ys[:, ut, e, :], blocks((SCB, OB)[ut][0])[:, e, :], ACT.Copy,
                                       scale=ffn_w[:, ut, e:e + 1]).then_inc(F.ys0, 1)
            body(0, 0)
            body(1, 1)
            with act.Fori(0, B // 2 - 1) as i:
                body(i * 2 + 2, 0)
                body(i * 2 + 3, 1)
            body(B, 0)
            engines_meet(act, 2)
            engines_meet(act, 3)

            def body(b, u):
                f, t, uo = b + 1, b - 1, 1 - u
                if there(f):
                    act_transposed_in(act, Z, TB, f, uo)
                    act.wait_ge(Z.xc_T, 2 * f + 1)
                    act.activation(x_bf[:, uo, :], xT[:, uo, :], ACT.Copy).then_inc(Z.x_bf, 1)
                if there(b):
                    act_exp(act, Z, ORG, D1, b, 0)
                if there(t):
                    for half, done in enumerate((Z.oTr0, Z.oTr1)):
                        act.wait_ge(done, t + 1)
                        act.activation(oT[:, uo, 4 * half:4 * half + 4, :], blocks(PB[half]), ACT.Copy)\
                            .then_inc(Z.oT_sb, 1)
                if there(b):
                    act_exp(act, Z, ORG, D1, b, 1)
                if there(f):
                    act.wait_ge(Z.ipa_sub, f + 1)
                    act.activation(ipa_s[:, uo, :, :], ipa_s[:, uo, :, :], ACT.Exp, scale=D1 ** -0.5)\
                        .then_inc(Z.ipa_exp, 1)
                    for n, (done, copied, other) in enumerate(((Z.k1, Z.k1_sb, Z.k0_sb), (Z.k3, Z.k3_sb, Z.k2_sb))):
                        act.wait_ge(done, f + 1)
                        act.activation(kT[:, uo, 8 * n + 4:8 * n + 8, 0:ORG], blocks(PB[1])[:, :, 0:ORG], ACT.Copy)\
                            .then_inc(copied, 1)
                        act.wait_ge(other, f + 1)
                        act.wait_ge(copied, f + 1)
                        after(act, Z.smax, (f - 1) * NCH)
                        act.activation(k_bf[:, uo, 8 * n:8 * n + 8, 0:ORG], kT[:, uo, 8 * n:8 * n + 8, 0:ORG], ACT.Copy)\
                            .then_inc(Z.k_bf, 1)
                if there(b):
                    act_exp(act, Z, ORG, D1, b, 2)
                if there(f):
                    act.wait_ge(Z.v1, f + 1)
                    act.activation(v1[0:ORG, uo, 8:16, 0:D1], PB[1][0:ORG, :].rearrange("p (h d) -> p h d", h=8),
                                   ACT.Copy).then_inc(Z.v1_sb, 1)
                if there(b):
                    act_exp(act, Z, ORG, D1, b, 3)
            pipelined(act, body)
            engines_meet(act, 4)
            act.preload_act_table(ACT.Silu)
            for n in range(4):
                act.wait_ge(R.tr, n + 1)
                act.activation(xT4[:, n % 2, :, :], blocks(bank[n % 2]), ACT.Copy).then_inc(R.xT, 1)
                act.wait_ge(R.hid, n + 1)
                act.activation(hT4[:, n % 2, 0:4, :], blocks(bank[2 + n % 2]), ACT.Silu).then_inc(R.h, 1)
            for t in range(2):
                act.wait_ge(R.step, t * (4 + 11 + 5) + 1)
                act.activation(probs[:, t, :], bank[4 + t][:, 0:128], ACT.Exp, bias=ex_max[:, t, :]).then_inc(R.ex, 1)

            def body(b, u):
                act.wait_ge(G.turned, b + 1)
                after(act, G.got, b - 1)
                act.activation(oh[:, u, 0:4, :], blocks(bank[u]), ACT.Copy).then_inc(G.oh, 1)
            body(0, 0)
            body(1, 1)
            with act.Fori(0, B // 2 - 1) as i:
                body(i * 2 + 2, 0)
                body(i * 2 + 3, 1)
            act.preload_act_table(ACT.Silu)
            engines_meet(act, 5)

            def silus(e, g, q):
                for c in range(2):
                    act.wait_ge(X1.gv, 2 * e + c + 1)
                    after(act, X1.h, 2 * e + c - 1)
                    act.activation(sg[:, c, :], bank[2 * c][:, :], ACT.Silu).then_inc(X1.silu, 1)

            def body(e, g, q):
                if there_expert(e + 1):
                    silus(e + 1, g, q + 1)
                act.wait_ge(X1.eo, e + 1)
                for n in range(4):
                    ins = act.activation(eo_rows(g, q, 0, n), eo_got(q, 0, n), ACT.Copy)
                ins.then_inc(X1.eo_act, 1)
            act.drain().then_inc(X1.eo_act, 2)
            experts(act, silus, body)
            engines_meet(act, 6)

        @block.tensor
        def _(pe):
            pe.wait_ge(made.ident, 5)
            pe.wait_ge(made.pick, 3)
            pe.wait_ge(made.vm, 2)
            pe.wait_ge(got.attn0, 16 * 8)

            def maxima(f, uf, j):
                pe.wait_ge(A.km, f * NCH + j + 1)
                after(pe, A.maxed, f * NCH + j)
                pe.matmul(blocks(MAXB), q_bf[:, uf, :], km_bf[:, uf, CH * j:CH * j + CH, :],
                          start=True, stop=True).then_inc(A.smax, 1)

            def scores(b, u, j):
                if j == 0:
                    pe.wait_ge(A.negT_sb, b + 1)
                    pe.wait_ge(A.qm, b + 1)
                    pe.wait_ge(A.k_sb, b + 1)
                after(pe, A.exp, b * NCH + j - 1)
                for g in range(CH):
                    h = CH * j + g
                    to = blocks(SCB[j % 2])[:, g, :]
                    pe.matmul(to, pick[0:H, h, :], negmaxT[0:H, u, :], start=True, stop=False)
                    mm = pe.matmul(to, kT[:, u, 0, :], qm[:, u, h, :], start=False, stop=True)
                mm.then_inc(A.score, 1)

            def values(b, u, j):
                pe.wait_ge(A.exp, b * NCH + j + 1)
                if j == 0:
                    pe.wait_ge(A.v_sb, b + 1)
                    after(pe, A.o, b - 1)
                half = j // 2
                for g in range(CH):
                    h = CH * (j % 2) + g
                    own = vm[:, u, half, :, :].rearrange("p h c -> p (h c)")[:, 128 * h:128 * h + 128]
                    mm = pe.matmul(OB[u][:, half * 128:half * 128 + 128], own, pT[:, j % 2, g, :],
                                   start=(h == 0), stop=(h == 7))
                mm.then_inc(A.pv, 1)

            def body(b, u):
                f, t, uo = b + 1, b - 1, 1 - u
                if there(f):
                    pe_transpose_in(pe, A, PB[1], f, uo, f)
                if there(b):
                    scores(b, u, 0)
                if there(f):
                    pe.wait_ge(A.xc_T, 2 * f + 2)
                    after(pe, A.km, f * NCH)
                    pe.matmul(PB[0][:, 0:128], wq0[:, :], xT[:, uo, :], start=True, stop=True)
                    pe.matmul(PB[0][:, 128:256], wk0[:, :], cT[:, uo, :], start=True, stop=True).then_inc(A.qk, 1)
                    pe.matmul(PB[1][:, 0:D], cT[:, uo, :], wv0[:, :], start=True, stop=True).then_inc(A.v, 1)
                if there(b):
                    scores(b, u, 1)
                if there(t):
                    pe.wait_ge(A.o, t + 1)
                    if there(f):
                        after(pe, A.negT_sb, f)
                    for half in range(2):
                        pe.matmul(TB[:, 0:D], o0T[:, uo, half, :], wo0[:, half, :], start=(half == 0), stop=False)
                    pe.matmul(TB[:, 0:D], ones_row[:, :], bo0[:, :], start=False, stop=True).then_inc(A.proj, 1)
                if there(b):
                    values(b, u, 0)
                if there(f):
                    maxima(f, uo, 0)
                if there(b):
                    scores(b, u, 2)
                if there(f):
                    maxima(f, uo, 1)
                if there(b):
                    values(b, u, 1)
                if there(f):
                    maxima(f, uo, 2)
                if there(b):
                    scores(b, u, 3)
                if there(f):
                    maxima(f, uo, 3)
                if there(b):
                    values(b, u, 2)
                if there(f):
                    after(pe, A.x_new, f - 1)
                    pe.wait_ge(A.maxed, f * NCH + NCH)
                    pe.matmul(TB[0:H, 0:128], negmax[:, 0:H], ident_bf[:, :], start=True, stop=True)\
                        .then_inc(A.negT, 1)
                if there(b):
                    values(b, u, 3)
            pipelined(pe, body)
            engines_meet(pe, 1)
            pe.wait_ge(got.ffn0, 32)
            pe.transpose(TB[:, 0:E0], gate_in[:, :], ident[0:E0, 0:E0]).then_inc(F.gate_tr, 1)
            pe.wait_ge(F.gateT, 1)

            def body(b, u):
                if there(b):
                    pe.wait_ge(F.xn, b + 1)
                    after(pe, F.xT, b - 1)
                    pe.transpose((TB, MAXB)[u][:, 0:128], xn[:, u, :], ident[:, :]).then_inc(F.tr, 1)
                t, ut = b - 1, 1 - u
                if there(t):
                    pe.wait_ge(F.xT, t + 1)
                    after(pe, F.ysum, t - 1)
                    pe.matmul(PB[ut][:, 0:E0], xT[:, ut, :], gateT[:, :], start=True, stop=True).then_inc(F.logit, 1)
                    for half in range(2):
                        mm = pe.matmul(blocks((SCB, OB)[ut][half]), xT[:, ut, :], we[:, 4 * half:4 * half + 4, :],
                                       start=True, stop=True)
                    mm.then_inc(F.y, 1)
            body(0, 0)
            body(1, 1)
            with pe.Fori(0, B // 2 - 1) as i:
                body(i * 2 + 2, 0)
                body(i * 2 + 3, 1)
            body(B, 0)
            engines_meet(pe, 2)

            pe.wait_ge(got.attn1, 16 * 20)
            for n, rows in enumerate((D, C, C)):
                mm = pe.transpose(PB[0][0:RANK, 128 * n:128 * n + rows], down[0:rows, n, :], ident[0:rows, 0:rows])
            mm.then_inc(W.turned, 1)
            for n in range(2):
                for c in range(4):
                    mm = pe.transpose(blocks(SCB[n], RANK)[:, c, :], down_o[:, 4 * n + c, :], ident[:, :])
                mm.then_inc(W.turned, 1)
            pe.wait_ge(W.downT, 3)
            for n, rows in enumerate((D, C, C)):
                for half in range(2):
                    pe.matmul(bank[2 * n + half][0:rows, :], downT[:, n, 0:rows], up[:, n, 512 * half:512 * half + 512],
                              start=True, stop=True).then_inc(W.prod, 1)
            for half in range(2):
                for c in range(4):
                    mm = pe.matmul(blocks(bank[6 + half])[:, c, :], downT[:, 3 + 4 * half + c, :], up_o[:, :],
                                   start=True, stop=True)
                mm.then_inc(W.prod, 1)
            pe.wait_ge(W.folded, 1)
            pe.transpose(bank[0][0:C, 0:B * IPA], ctx_ipa[:, :], ident[0:B * IPA, 0:B * IPA]).then_inc(W.ctxT_ps, 1)
            for n in range(2):
                pe.wait_ge(W.folded, 3)
                for c in range(4):
                    mm = pe.transpose(blocks(bank[1 + n])[:, c, :], wq1[:, 128 * (4 * n + c):128 * (4 * n + c + 1)],
                                      ident[:, :])
                mm.then_inc(W.wq1T_ps, 1)
            for n in range(2):
                pe.wait_ge(W.wq1T, n + 1)
                for c in range(4):
                    mm = pe.transpose(bank[1 + n][:, C * c:C * c + C], wk1[:, 128 * (4 * n + c):128 * (4 * n + c + 1)],
                                      ident[0:C, 0:C])
                mm.then_inc(W.wk1T_ps, 1)
            pe.wait_ge(W.wk1T, 2)
            pe.wait_ge(W.folded, 8)
            for n in range(4):
                after(pe, W.mT, n - 1)
                rows = slice(D1 * (n % 2), D1 * (n % 2) + D1)
                for g in range(CH):
                    c = CH * (n // 2) + g
                    mm = pe.matmul(blocks(bank[6 + n % 2], C)[:, g, :], wk1T[rows, c, :], wq1T[rows, c, :],
                                   start=True, stop=True)
                mm.then_inc(W.mT_ps, 1)
            pe.wait_ge(W.mT, 4)
            pe.wait_ge(W.ctxT, 1)
            for n, w in enumerate((wki, wvi)):
                for c in range(8):
                    mm = pe.matmul(bank[3 + n][:, 64 * c:64 * c + 64], w[:, 128 * c:128 * c + 128], ctx_ipaT[:, :],
                                   start=True, stop=True)
                mm.then_inc(W.kv_ps, 1)
            pe.wait_ge(W.wq1T, 2)
            pe.wait_ge(W.kT, 2)
            for n in range(2):
                for c in range(4):
                    mm = pe.matmul(blocks(bank[5 + n])[:, c, :], wq1T[:, 4 * n + c, :],
                                   ipa_kT[:, 4 * n + c, :, :, :], start=True, stop=True)
                mm.then_inc(W.prod, 1)
            pe.wait_ge(W.vT, 2)
            for n in range(2):
                for c in range(4):
                    mm = pe.matmul(blocks(bank[(7, 0)[n]])[:, c, :], ipa_vT[:, 4 * n + c, :, :, :],
                                   wo1[:, 4 * n + c, :], start=True, stop=True)
                mm.then_inc(W.prod, 1)
            engines_meet(pe, 3)

            def maxima(f, uf, j):
                if j == 0:
                    pe.wait_ge(Z.x_bf, f + 1)
                pe.wait_ge(Z.k_bf, 2 * f + 1 + j // 2)
                after(pe, Z.maxed, f * NCH + j)
                pe.matmul(blocks(MAXB)[:, :, 0:ORG], x_bf[:, uf, :], k_bf[:, uf, CH * j:CH * j + CH, 0:ORG],
                          start=True, stop=True).then_inc(Z.smax, 1)

            def scores(b, u, j):
                if j == 0:
                    for s in (Z.negT_sb, Z.k0_sb, Z.k1_sb, Z.k2_sb, Z.k3_sb):
                        pe.wait_ge(s, b + 1)
                after(pe, Z.exp, b * NCH + j - 1)
                for g in range(CH):
                    h = CH * j + g
                    to = blocks(SCB[j % 2], ORG)[:, g, :]
                    pe.matmul(to, pick[0:H, h, 0:ORG], negmaxT[0:H, u, :], start=True, stop=False)
                    mm = pe.matmul(to, kT[:, u, h, 0:ORG], xT[:, u, :], start=False, stop=True)
                mm.then_inc(Z.score, 1)

            def values(b, u, j):
                pe.wait_ge(Z.exp, b * NCH + j + 1)
                if j == 0:
                    pe.wait_ge(Z.v0_sb, b + 1)
                    pe.wait_ge(Z.v1_sb, b + 1)
                after(pe, Z.o, b * NCH + j - 1)
                for g in range(CH):
                    mm = pe.matmul(OB[j % 2][:, (D1 + 1) * g:(D1 + 1) * (g + 1)], pT[0:ORG, j % 2, g, :],
                                   v1[0:ORG, u, CH * j + g, :], start=True, stop=True)
                mm.then_inc(Z.pv, 1)

            def keys(n, uf, f, done, freed_by):
                after(pe, *freed_by)
                for g in range(CH):
                    mm = pe.matmul(blocks(PB[n % 2])[:, g, 0:ORG], mT[:, CH * n + g, :], cT[:, uf, 0:ORG],
                                   start=True, stop=True)
                mm.then_inc(done, 1)

            def body(b, u):
                f, t, uo = b + 1, b - 1, 1 - u
                if there(f):
                    pe.wait_ge(Z.xn, f + 1)
                    pe.wait_ge(Z.ctx_in, f + 1)
                    after(pe, Z.negT_sb, f)
                    pe.transpose(TB[:, 0:128], xn[:, uo, :], ident[:, :])
                    pe.transpose(TB[0:C, 128:256], ctx_in[:, uo, :], ident[:, :]).then_inc(Z.tr, 1)
                if there(b):
                    scores(b, u, 0)
                if there(t):
                    pe.wait_ge(Z.o, t * NCH + NCH)
                    pe.wait_ge(Z.v0_sb, t + 2) if there(b) else None
                    pe.wait_ge(Z.v1_sb, t + 2) if there(b) else None
                    for half, done in enumerate((Z.oTr0, Z.oTr1)):
                        for c in range(4):
                            n = 4 * half + c
                            mm = pe.transpose(blocks(PB[half])[:, c, :], o[:, uo, 128 * n:128 * n + 128], ident[:, :])
                        mm.then_inc(done, 1)
                if there(b):
                    scores(b, u, 1)
                if there(f):
                    pe.wait_ge(Z.xc_T, 2 * f + 2)
                    pe.matmul(TB[:, 0:H * IPA], xT[:, uo, :], ipa_k[:, f, :], start=True, stop=True)\
                        .then_inc(Z.ipa_score, 1)
                    if there(t):
                        pe.wait_ge(Z.oT_sb, 2 * t + 2)
                    keys(0, uo, f, Z.k0, (Z.v0_sb, f))
                    keys(1, uo, f, Z.k1, (Z.v1_sb, f))
                if there(b):
                    values(b, u, 0)
                if there(f):
                    keys(2, uo, f, Z.k2, (Z.k0_sb, f + 1))
                    keys(3, uo, f, Z.k3, (Z.k1_sb, f + 1))
                if there(t):
                    pe.wait_ge(Z.oT_sb, 2 * t + 2)
                    if there(f):
                        pe.wait_ge(Z.ipa_sub, f + 1)
                    for c in range(8):
                        pe.matmul(TB[:, 0:D], oT[:, uo, c, :], wo1[:, c, :], start=(c == 0), stop=False)
                    if isinstance(t, int) and t == 0:
                        pe.wait_ge(W.back, 16 * 8)
                    pe.matmul(TB[:, 0:D], ipa_pT[:, uo, :], ipa_v[:, t, :], start=False, stop=False)
                    pe.matmul(TB[:, 0:D], ones_row[:, :], bo1[:, :], start=False, stop=True).then_inc(Z.proj, 1)
                if there(b):
                    scores(b, u, 2)
                if there(f):
                    maxima(f, uo, 0)
                    for n, (done, freed) in enumerate(((Z.v0, Z.k2_sb), (Z.v1, Z.k3_sb))):
                        pe.wait_ge(freed, f + 1)
                        pe.matmul(PB[n][0:ORG, :], cT[:, uo, 0:ORG], wv1[:, 512 * n:512 * n + 512],
                                  start=True, stop=True).then_inc(done, 1)
                if there(b):
                    values(b, u, 1)
                if there(f):
                    maxima(f, uo, 1)
                if there(b):
                    scores(b, u, 3)
                if there(f):
                    maxima(f, uo, 2)
                    after(pe, Z.x_new, f - 1)
                    pe.wait_ge(Z.ipa_p, f + 1)
                    pe.matmul(TB[0:H * IPA, 0:128], ipa_s[:, uo, :, :].rearrange("p h j -> p (h j)"), ident[:, :],
                              start=True, stop=True).then_inc(Z.ipa_turn, 1)
                    maxima(f, uo, 3)
                if there(b):
                    values(b, u, 2)
                if there(f):
                    pe.wait_ge(Z.maxed, f * NCH + NCH)
                    pe.wait_ge(Z.ipa_pT, f + 1)
                    pe.matmul(TB[0:H, 0:128], negmax[:, 0:H], ident_bf[:, :], start=True, stop=True).then_inc(Z.negT, 1)
                if there(b):
                    values(b, u, 3)
            pipelined(pe, body)
            engines_meet(pe, 4)

            pe.wait_ge(R.wide, 2)
            for n in range(4):
                pe.wait_ge(R.xn, 4 * n + 4)
                after(pe, R.xT, n - 1)
                for k in range(4):
                    mm = pe.transpose(blocks(bank[n % 2])[:, k, :], xn_all[:, 4 * n + k, :], ident[:, :])
                mm.then_inc(R.tr, 1)
                pe.wait_ge(R.xT, n + 1)
                after(pe, R.h, n - 1)
                pe.matmul(bank[2 + n % 2][:, :], rw1[:, :], xT4[:, n % 2, :, :], start=True, stop=True).then_inc(R.hid, 1)
                pe.wait_ge(R.h, n + 1)
                for k in range(4):
                    b = 4 * n + k
                    mm = pe.matmul(bank[4 + n // 2][:, 0:128], rw2_of(b), hT4[:, n % 2, k, :],
                                   start=(b % 8 == 0), stop=(b % 8 == 7))
                if n % 2:
                    mm.then_inc(R.logit, 1)
            ident4 = ident[:, :].rearrange("p (b g q) -> p q b g", b=8, g=EG)
            for t in range(2):
                pe.wait_ge(R.step, (t + 1) * (4 + 11 + 5))
                for n, what in enumerate((top_at_f, top)):
                    for q in range(4):
                        mm = pe.matmul(bank[6 + t][32 * q:32 * q + 32, 32 * n:32 * n + 32], what[:, t, :],
                                       ident4[:, q, :, :], start=True, stop=True)
                mm.then_inc(R.turned, 1)

            def body(b, u):
                pe.wait_ge(G.row, b + 1)
                after(pe, G.oh, b - 1)
                for g in range(EG):
                    mm = pe.matmul(blocks(bank[u])[:, g, :], oh_bf[:, u, g, :], ident_bf[:, :], start=True, stop=True)
                mm.then_inc(G.turned, 1)
                pe.wait_ge(G.oh, b + 1)
                after(pe, G.xg, b - 1)
                pe.matmul(bank[2 + u][:, :], xn[:, u, :], oh[:, u, 0:4, :], start=True, stop=True).then_inc(G.got, 1)
            body(0, 0)
            body(1, 1)
            with pe.Fori(0, B // 2 - 1) as i:
                body(i * 2 + 2, 0)
                body(i * 2 + 3, 1)
            engines_meet(pe, 5)

            def inner(e, g, q):
                pe.wait_ge(w_in[q % 4], 48 * (g + q // 4 + 1))
                for c in range(2):
                    after(pe, X1.h, 2 * e + c - 1)
                    for n, w in enumerate((ew1, ew2)):
                        mm = pe.matmul(bank[2 * c + n][:, :], w[:, q % 4, 128 * c:128 * c + 128], xgT[:, :, e, :],
                                       start=True, stop=True)
                    mm.then_inc(X1.gv, 1)

            def body(e, g, q):
                if there_expert(e + 1):
                    inner(e + 1, g, q + 1)
                pe.wait_ge(X1.h, 2 * e + 2)
                pe.wait_ge(X1.eo_act, e + 1)
                pe.wait_ge(X1.eo_dve, e + 1)
                for k in range(4):
                    for c in range(2):
                        mm = pe.matmul(bank[4 + 2 * (q % 2) + k // 2][:, D * (k % 2):D * (k % 2) + D],
                                       hs[:, q % 2, c, 128 * k:128 * k + 128], ew3[:, q % 4, c, :],
                                       start=(c == 0), stop=(c == 1))
                mm.then_inc(X1.eo, 1)
            experts(pe, inner, body)
            engines_meet(pe, 6)

            def body(b, u):
                pe.wait_ge(Y.row, b + 1)
                after(pe, Y.x_new, b - 1)
                for g in range(EG):
                    mm = pe.matmul(bank[u][:, 0:D], ohw[:, u, g, :], eo_all[:, b, g, :], start=(g == 0), stop=(g == 3))
                mm.then_inc(Y.sum, 1)
            body(0, 0)
            body(1, 1)
            with pe.Fori(0, B // 2 - 1) as i:
                body(i * 2 + 2, 0)
                body(i * 2 + 3, 1)


def kernel(**inputs):
    import numpy as _np
    import concourse.bacc as _bacc
    from concourse.bass_utils import run_bass_kernel_spmd as _run

    nc = _bacc.Bacc("TRN2", target_bir_lowering=False, num_devices=1)
    arrays, tensors = {}, {}
    for name, value in inputs.items():
        a = _np.ascontiguousarray(value)
        arrays[f"in_{name}_dram"] = a
        tensors[name] = nc.dram_tensor(f"in_{name}_dram", a.shape, mybir.dt.from_np(a.dtype), kind="ExternalInput").ap()
    out = nc.dram_tensor("out_0_dram", (B, S, D), F32, kind="ExternalOutput").ap()
    build_program(nc, tensors, out)
    r = _run(nc, [arrays], core_ids=[0])
    return r.results[0]["out_0_dram"]
```

```python
from contextlib import ExitStack

import concourse.bass as bass
from concourse import mybir

F32 = mybir.dt.float32
BF16 = mybir.dt.bfloat16
I32 = mybir.dt.int32
ALU = mybir.AluOpType
ACT = mybir.ActivationFunctionType
X = mybir.AxisListType.X

B, S, D = 16, 128, 128
C = 96
H = 16
D0 = D // H
D1 = 64
ID = H * D1
RANK = 32
IPA = 4
ORG = S - IPA
E0 = 8
E1, F1 = 16, 256
EG = E1 // 4
CAP = 32
EPS = 1e-5
CH = 4
NCH = H // CH
BANK = 512


def named(make, prefix, names):
    return type(prefix, (), {name: make(f"{prefix}_{name}") for name in names.split()})


def after(eng, sem, value):
    if not isinstance(value, int) or value >= 1:
        eng.wait_ge(sem, value)


def there(b):
    return not isinstance(b, int) or 0 <= b < B


def there_expert(e):
    return not isinstance(e, int) or e < E1


def pipelined(eng, body):
    for b in (-1, 0, 1):
        body(b, b % 2)
    with eng.Fori(0, (B - 4) // 2) as i:
        body(i * 2 + 2, 0)
        body(i * 2 + 3, 1)
    for b in (B - 2, B - 1, B):
        body(b, b % 2)


def by_pairs(eng, body):
    with eng.Fori(0, B // 2) as i:
        body(i * 2, 0)
        body(i * 2 + 1, 1)


def build_program(nc, T, out):
    with ExitStack() as ctx:
        def sb(name, shape, dt=F32):
            return ctx.enter_context(nc.sbuf_tensor(name, shape, dt))

        def sem(name):
            return ctx.enter_context(nc.semaphore(name))

        bank = [ctx.enter_context(nc.psum_tensor(f"bank{n}", [128, BANK], F32)) for n in range(8)]
        MAXB = bank[0]
        SCB = bank[1:3]
        OB = bank[3:5]
        PB = bank[5:7]
        TB = bank[7]

        def blocks(b_, rows=128):
            return b_[0:rows, :].rearrange("p (g n) -> p g n", g=CH)

        ident = sb("ident", [128, 128])
        ident_bf = sb("ident_bf", [128, 128], BF16)
        pick = sb("pick", [128, H, 128], BF16)
        ones_row = sb("ones_row", [1, 128])
        minus_half = sb("minus_half", [128, B])
        x_all = sb("x_all", [128, B, D])
        ctx_all = sb("ctx_all", [128, B, C])
        stats = sb("stats", [128, B, 6])
        mv = sb("mv", [128, B, 2])
        veps = sb("veps", [128, B])
        rstd = sb("rstd", [128, B, 1])

        class Arena:

            def __init__(self, name, size):
                self.tile, self.size = sb(name, [128, size]), size
                self.again()

            def again(self):
                self.at = 0

            def take(self, shape, dt=F32):
                rows, dims = shape[0], shape[1:]
                n = 1
                for d in dims:
                    n *= d
                words = n if dt in (F32, I32) else n // 2
                assert self.at + words <= self.size, (self.at + words, self.size)
                flat = self.tile[0:rows, self.at:self.at + words]
                self.at += words
                if dt != F32:
                    flat = flat.bitcast(dt)
                letters = "abcde"[:len(dims)]
                return flat.rearrange(f"p ({' '.join(letters)}) -> p {' '.join(letters)}",
                                      **dict(zip(letters, dims)))

        early = Arena("early", 15872)
        late = Arena("late", 11776)

        ctx_in = sb("ctx_in", [128, 2, C])
        xn = sb("xn", [128, 2, D])
        xT = sb("xT", [128, 2, 128])
        cT = sb("cT", [C, 2, 128])
        qT = sb("qT", [128, 2, 128])
        q_bf = sb("q_bf", [128, 2, 128], BF16)
        kT = sb("kT", [128, 2, H, ORG + IPA])
        x_bf = sb("x_bf", [128, 2, 128], BF16)
        k_bf = late.take([128, 2, H, 128], BF16)
        qm = early.take([128, 2, H, 128])
        km_bf = early.take([128, 2, H, 128], BF16)
        vm = early.take([128, 2, 2, 8, 136])
        attn0_slots = early.at
        o0T = sb("o0T", [64, 2, 2, 128])
        rsum0 = sb("rsum0", [64, 2, 2, 128])
        hmask = sb("hmask", [128, H])
        v1 = late.take([128, 2, H, D1 + 1])
        negmax = sb("negmax", [128, 128], BF16)
        negmaxT = sb("negmaxT", [128, 2, 128], BF16)
        pT = sb("pT", [128, 2, CH, 128])
        rsum = sb("rsum", [128, 2, H])
        o = sb("o", [128, 2, ID])
        oT = sb("oT", [128, 2, 8, 128])

        attn1_slots = late.at
        wq0 = early.take([D, D])
        wk0 = early.take([C, D])
        bq0 = sb("bq0", [128, 1])
        bk0 = sb("bk0", [128, 1])
        wv0 = early.take([C, D])
        bv0 = early.take([128, D])
        wo0 = early.take([64, 2, D])
        bo0 = sb("bo0", [1, D])

        gate_in = sb("gate_in", [E0, D])
        gateT = early.take([D, E0])
        we = early.take([D, E0, D])
        lower = sb("lower", [128, E0, E0])
        ys = early.take([128, 2, E0, D])
        ysum = sb("ysum", [128, 2, D])

        attn0_end, early.at = early.at, 0
        xn0 = early.take([128, B, D])
        xT0 = early.take([128, B, 128])
        lg = early.take([128, B, E0])
        beat = early.take([128, B, E0, E0])
        tie = early.take([128, B, E0, E0])
        nbeat = early.take([128, B, E0])
        top0 = early.take([128, B])
        ew = early.take([128, B, E0])
        wsum = early.take([128, B])
        ffn_w = early.take([128, B, E0])
        downT = early.take([RANK, 3 + 8, 128])
        ctx_ipaT = early.take([C, B * IPA])
        assert early.at <= attn0_slots
        early.at = attn0_end

        wq1 = late.take([D, ID])
        wk1 = late.take([C, ID])
        mT = late.take([C, H, D])
        wv1 = late.take([C, ID])
        wo1 = late.take([128, 8, D])
        bo1 = sb("bo1", [1, D])
        alpha = sb("alpha", [128, 4])
        ipa_k = late.take([D, B, H * IPA])
        ipa_v = sb("ipa_v", [H * IPA, B, D])
        ipa_s = sb("ipa_s", [128, 2, H, IPA])
        ipa_max = sb("ipa_max", [128, 2, H])
        ipa_sum = sb("ipa_sum", [128, 2, H])
        ipa_pT = sb("ipa_pT", [H * IPA, 2, 128])
        late_end, late.at = late.at, 0
        down = late.take([128, 3, RANK])
        down_o = late.take([128, 8, RANK])
        up = late.take([RANK, 3, ID])
        up_o = late.take([RANK, D])
        ctx_ipa = late.take([B * IPA, C])
        assert late.at <= attn1_slots
        late.at = late_end
        wki, wvi = o[0:C, 0, :], o[0:C, 1, :]
        wq1T, ipa_v_rows = oT[:, 0, :, :], oT[:, 1, :, :]
        wk1T = kT[:, 1, 0:8, 0:C]
        ipa_kT, ipa_vT = (kT[:, 0, 8 * n:8 * n + 8, :].rearrange("p c (b t j) -> p c b t j", b=B, t=2) for n in (0, 1))
        early.again()
        rw1 = early.take([D, D])
        rw2 = early.take([D, E1])
        rw2_wide = early.take([D, 8 * (D + E1)])
        ew1 = early.take([D, 4, F1])
        ew2 = early.take([D, 4, F1])
        ew3 = early.take([128, 4, F1 // 128, D])
        count_i = early.take([128, 128], I32)
        count = early.take([128, 128])
        eo_all = early.take([128, B, EG, D])
        xn_all = early.take([128, B, D])
        late.again()
        xgT = late.take([D, B, E1, CAP])
        hs = late.take([128, 2, 2, 512])
        late_mark = late.at
        oh_bf = late.take([128, 2, EG, 128], BF16)
        late.at = late_mark
        sg = late.take([128, 2, 512])
        xT4, hT4 = pT, oT
        oh = kT
        ohw = oT
        probs = sb("probs", [128, 2, 128])
        ex_max = sb("ex_max", [128, 2, 1])
        ex_sum = sb("ex_sum", [128, 2, 1])
        top = sb("top", [128, 2, CAP])
        top_at = sb("top_at", [128, 2, CAP], mybir.dt.uint32)
        top_at_f = sb("top_at_f", [128, 2, CAP])
        slot_at = sb("slot_at", [128, B, EG])
        slot_w = sb("slot_w", [128, B, EG])
        ipa_v_dram = nc.dram_tensor("ipa_v_scratch", (B, 2 * IPA, 8, D), F32, kind="Internal").ap()

        block = ctx.enter_context(nc.Block())

        made = named(sem, "made", "consts ident pick hmask vm")
        got = named(sem, "got", "x ctx attn0 ffn0 attn1 ipa route stored")
        ln = named(sem, "ln", "stats mv veps rstd")
        phase_end = sem("phase_end")
        A = named(sem, "a", "ctx_in xn tr xc_T qk qm km v q_sb k_sb v_sb q_bf k_bf smax maxed negT negT_sb "
                            "score exp pv rsum o oTr oT_sb proj x_new stats")

        F = named(sem, "f", "gate_tr gateT lower xn tr xT logit step ex slot y ys0 ys1 ysum x_new stats")

        W = named(sem, "w", "turned downT alpha whole folded mT_ps mT ctxT_ps ctxT kv_ps kT vT zeros prod ipa_k ipa_v_rows out back")
        Z = named(sem, "z", "ctx_in xn tr xc_T x_bf k0 k1 k2 k3 v0 v1 k0_sb k1_sb k2_sb k3_sb v0_sb v1_sb k_bf "
                            "smax maxed negT negT_sb score exp pv rsum o oTr0 oTr1 oT_sb proj x_new stats "
                            "ipa_score ipa_step ipa_sub ipa_exp ipa_p ipa_turn ipa_pT")

        R = named(sem, "r", "wide count xn tr xT hid h logit step ex turned slot")
        G = named(sem, "g", "xn row turned oh got xg")
        X1 = named(sem, "x", "w0 w1 w2 w3 gv silu h eo eo_act eo_dve")
        w_in = (X1.w0, X1.w1, X1.w2, X1.w3)
        Y = named(sem, "y", "row sum x_new stored")

        def engines_meet(eng, n):
            eng.drain().then_inc(phase_end, 1)
            eng.wait_ge(phase_end, 5 * n)

        def act_exp(act, Z, keys, width, b, j):
            act.wait_ge(Z.score, b * NCH + j + 1)
            after(act, Z.pv, b * NCH + j - 1)
            act.activation(pT[0:keys, j % 2, :, :], blocks(SCB[j % 2], keys), ACT.Exp,
                           scale=float(width) ** -0.5).then_inc(Z.exp, 1)

        def dve_max(dve, Z, f, j, column, keys):
            dve.wait_ge(Z.smax, f * NCH + j + 1)
            after(dve, Z.negT, f)
            dve.tensor_reduce(negmax[:, column:column + CH], blocks(MAXB)[:, :, 0:keys], X, ALU.max,
                              negate=True).then_inc(Z.maxed, 1)

        def dve_negmaxT(dve, Z, f, uf, width):
            dve.wait_ge(Z.negT, f + 1)
            dve.tensor_copy(negmaxT[0:width, uf, :], TB[0:width, 0:128]).then_inc(Z.negT_sb, 1)

        def dve_xn(dve, Z, b, u):
            dve.tensor_scalar(xn[:, u, :], x_all[:, b, :], mv[:, b, 0:1], rstd[:, b, :],
                              ALU.subtract, ALU.mult).then_inc(Z.xn, 1)

        def dve_residual(dve, Z, t, add):
            dve.tensor_tensor(x_all[:, t, :], add, x_all[:, t, :], ALU.add).then_inc(Z.x_new, 1)
            dve.wait_ge(Z.x_new, t + 1)

        def dve_stats(dve, Z, t):
            dve.bn_stats(stats[:, t, :], x_all[:, t, :]).then_inc(Z.stats, 1)

        def pe_transpose_in(pe, Z, to, f, uf, freed):
            pe.wait_ge(Z.xn, f + 1)
            pe.wait_ge(Z.ctx_in, f + 1)
            after(pe, Z.v_sb, freed)
            pe.transpose(to[:, 0:128], xn[:, uf, :], ident[:, :])
            pe.transpose(to[0:C, 128:256], ctx_in[:, uf, :], ident[:, :]).then_inc(Z.tr, 1)

        def act_transposed_in(act, Z, of, f, uf):
            act.wait_ge(Z.tr, f + 1)
            act.activation(xT[:, uf, :], of[:, 0:128], ACT.Copy).then_inc(Z.xc_T, 1)
            act.activation(cT[:, uf, :], of[0:C, 128:256], ACT.Copy).then_inc(Z.xc_T, 1)

        def pool_ctx(pool, Z, b, u):
            after(pool, Z.tr, b - 1)
            pool.tensor_copy(ctx_in[:, u, :], ctx_all[:, b, :]).then_inc(Z.ctx_in, 1)



        def experts(eng, first, body):
            first(0, 0, 0)
            with eng.Fori(0, EG - 1) as i:
                for q in range(4):
                    body(i * 4 + q, i, q)
            for q in range(4):
                body(E1 - 4 + q, EG - 1, q)

        def rw2_of(b):
            return rw2_wide[:, 128 * (b % 8):128 * (b % 8) + 128]

        def eo_got(q, half, n):
            return bank[4 + 2 * (q % 2) + half][32 * n:32 * n + 32, 0:2 * D].rearrange("p (k d) -> p k d", k=2)

        def eo_rows(g, q, half, n):
            return eo_all[32 * q:32 * q + 32, :, :, :].rearrange("p (h k n) g d -> p h n g k d", h=2, k=2)[:, half, n, g, :, :]

        @block.sync
        def _(sp):
            sp.dma_start(x_all[:, :, :], T["x"].rearrange("b s d -> s b d")).then_inc(got.x, 16)
            sp.dma_start(ctx_all[:, :, :], T["ctx_768"].rearrange("b s c -> s b c")).then_inc(got.ctx, 16)
            sp.dma_start(wq0[:, :], T["L0_xattn_wq"]).then_inc(got.attn0, 16)
            sp.dma_start(wk0[:, :], T["L0_xattn_wk"]).then_inc(got.attn0, 16)
            for bias, name in ((bq0, "L0_xattn_bq"), (bk0, "L0_xattn_bk")):
                sp.dma_start(bias[:, :], T[name].rearrange("(p a) -> p a", a=1)).then_inc(got.attn0, 16)
            sp.dma_start(wv0[:, :], T["L0_xattn_wv"]).then_inc(got.attn0, 16)
            sp.dma_start(bv0[:, :], T["L0_xattn_bv"].rearrange("(a n) -> a n", a=1).broadcast_to((128, D))).then_inc(got.attn0, 16)
            sp.dma_start(wo0[:, :, :], T["L0_xattn_wo"].rearrange("(a p) n -> p a n", a=2)).then_inc(got.attn0, 16)
            sp.dma_start(bo0[:, :], T["L0_xattn_bo"].rearrange("(a n) -> a n", a=1)).then_inc(got.attn0, 16)
            sp.dma_start(gate_in[:, :], T["L0_ffn_gate_w"]).then_inc(got.ffn0, 16)
            sp.dma_start(we[:, :, :], T["L0_ffn_We"].rearrange("e d m -> d e m")).then_inc(got.ffn0, 16)
            for w, name in ((wq1, "Wq"), (wk1, "Wk"), (wv1, "Wv")):
                sp.dma_start(w[:, :], T["L1_xattn_" + name]).then_inc(got.attn1, 16)
            sp.dma_start(wo1[:, :, :], T["L1_xattn_Wo"].rearrange("(c p) n -> p c n", p=128)).then_inc(got.attn1, 16)
            sp.dma_start(bo1[:, :], T["L1_xattn_bo"].rearrange("(a n) -> a n", a=1)).then_inc(got.attn1, 16)
            for n, name in enumerate("qkvo"):
                sp.dma_start(alpha[:, n:n + 1], T[f"L1_xattn_{name}_alpha"].rearrange("(a n) -> a n", a=1)
                             .broadcast_to((128, 1))).then_inc(got.attn1, 16)
            for n, (name, rows) in enumerate((("q", D), ("k", C), ("v", C))):
                sp.dma_start(down[0:rows, n, :], T[f"L1_xattn_{name}_down"]).then_inc(got.attn1, 16)
                sp.dma_start(up[:, n, :], T[f"L1_xattn_{name}_up"]).then_inc(got.attn1, 16)
            sp.dma_start(down_o[:, :, :], T["L1_xattn_o_down"].rearrange("(c p) r -> p c r", p=128)).then_inc(got.attn1, 16)
            sp.dma_start(up_o[:, :], T["L1_xattn_o_up"]).then_inc(got.attn1, 16)
            sp.dma_start(ctx_ipa[:, :], T["ctx_768"][:, ORG:S, :].rearrange("b j c -> b j c")).then_inc(got.attn1, 16)
            sp.dma_start(wki[:, :], T["L1_xattn_Wk_ipa"]).then_inc(got.attn1, 16)
            sp.dma_start(wvi[:, :], T["L1_xattn_Wv_ipa"]).then_inc(got.attn1, 16)
            engines_meet(sp, 1)
            sp.wait_ge(W.ipa_v_rows, 2)
            sp.dma_start(ipa_v_dram.rearrange("b r c n -> (b r) c n"), ipa_v_rows[:, :, :]).then_inc(W.out, 16)
            sp.wait_ge(W.out, 16)
            for c in range(8):
                sp.dma_start(ipa_v[8 * c:8 * c + 8, :, :], ipa_v_dram[:, :, c, :].rearrange("b r n -> r b n"))\
                    .then_inc(W.back, 16)
            engines_meet(sp, 2)
            sp.dma_start(rw1[:, :], T["L1_ffn_router_w1"]).then_inc(got.route, 16)
            sp.dma_start(rw2[:, :], T["L1_ffn_router_w2"]).then_inc(got.route, 16)

            def expert_weights(e, q):
                for slot, w in ((ew1, "L1_ffn_w1"), (ew2, "L1_ffn_w2")):
                    sp.dma_start(slot[:, q, :], T[w][e, :, :]).then_inc(w_in[q], 16)
                sp.dma_start(ew3[:, q, :, :], T["L1_ffn_w3"].rearrange("e (c p) n -> e p c n", p=128)[e, :, :, :])\
                    .then_inc(w_in[q], 16)
            for q in range(4):
                expert_weights(q, q)
            engines_meet(sp, 3)
            engines_meet(sp, 4)
            with sp.Fori(0, EG - 1) as i:
                for q in range(4):
                    sp.wait_ge(X1.eo, i * 4 + q + 1)
                    expert_weights(i * 4 + (q + 4), q)
            engines_meet(sp, 5)
            with sp.Fori(0, B) as b:
                sp.wait_ge(Y.x_new, b + 1)
                sp.dma_start(out[b, :, :], x_all[:, b, :]).then_inc(Y.stored, 16)
            sp.wait_ge(Y.stored, 16 * B)

        @block.gpsimd
        def _(pool):
            pool.memset(minus_half[:, :], -0.5).then_inc(made.consts, 1)
            pool.memset(ident[:, :], 0.0).then_inc(made.ident, 1)
            pool.memset(ident_bf[:, :], 0.0).then_inc(made.ident, 1)
            pool.memset(pick[:, :, :], 0.0).then_inc(made.pick, 1)
            pool.wait_ge(made.ident, 2)
            for m in (ident, ident_bf):
                pool.affine_select(out=m[:, :], in_=m[:, :], compare_op=ALU.not_equal, fill=1.0, base=0,
                                   pattern=[[-1, 128]], channel_multiplier=1).then_inc(made.ident, 1)
            pool.memset(ones_row[:, :], 1.0).then_inc(made.ident, 1)
            for j in range(2):
                pool.wait_ge(made.pick, j + 1)
                pool.affine_select(out=pick[:, :, :], in_=pick[:, :, :], compare_op=ALU.not_equal, fill=1.0,
                                   base=-64 * j, pattern=[[-1, H], [0, 128]], channel_multiplier=1)\
                    .then_inc(made.pick, 1)
            pool.memset(hmask[:, :], 1.0).then_inc(made.hmask, 1)
            for base, way in ((0, 1), (D0 - 1, -1)):
                pool.wait_ge(made.hmask, 1 if way == 1 else 2)
                pool.affine_select(out=hmask[:, :], in_=hmask[:, :], compare_op=ALU.is_ge, fill=0.0, base=base,
                                   pattern=[[-D0 * way, H]], channel_multiplier=way).then_inc(made.hmask, 1)
            pool.memset(negmax[:, :], 0.0).then_inc(made.consts, 1)
            pool.wait_ge(got.ctx, 16)

            def rstds(n):
                pool.wait_ge(ln.veps, n)
                pool.tensor_tensor(rstd[:, :, 0], veps[:, :], minus_half[:, :], ALU.pow).then_inc(ln.rstd, 1)
            rstds(1)

            def body(b, u):
                f, uf = b + 1, 1 - u
                if isinstance(b, int) and b == -1:
                    pool_ctx(pool, A, 0, 0)
                    pool_ctx(pool, A, 1, 1)
                if there(b + 2) and not (isinstance(b, int) and b == -1):
                    pool_ctx(pool, A, b + 2, u)
            pipelined(pool, body)
            engines_meet(pool, 1)
            rstds(2)
            pool.memset(ipa_kT, 0.0).then_inc(W.zeros, 1)
            pool.memset(ipa_vT, 0.0).then_inc(W.zeros, 1)
            pool.memset(lower[:, :, :], 1.0).then_inc(F.lower, 1)
            pool.wait_ge(F.lower, 1)
            pool.affine_select(out=lower[:, :, :], in_=lower[:, :, :], compare_op=ALU.is_ge, fill=0.0, base=-1,
                               pattern=[[1, E0], [-1, E0]], channel_multiplier=0).then_inc(F.lower, 1)

            def body(b, u):
                pool.wait_ge(F.xT, b // 4 + 1 if isinstance(b, int) else B // 4)
                after(pool, F.y, b - 1)
                pool.tensor_copy(xT[:, u, :], xT0[:, b, :]).then_inc(F.slot, 1)
            body(0, 0)
            body(1, 1)
            with pool.Fori(0, B // 2 - 1) as i:
                body(i * 2 + 2, 0)
                body(i * 2 + 3, 1)
            pool.wait_ge(W.prod, 4)
            pool.memset(v1[:, :, :, D1:D1 + 1], 1.0)
            engines_meet(pool, 2)
            rstds(3)
            pool.memset(rw2_wide[:, :], 0.0).then_inc(R.wide, 1)
            pool.iota(count_i[:, :], [[1, 128]], base=0, channel_multiplier=0).then_inc(R.count, 1)
            pool.wait_ge(R.count, 1)
            pool.tensor_copy(count[:, :], count_i[:, :]).then_inc(R.count, 1)
            pool.wait_ge(got.route, 32)
            pool.wait_ge(R.wide, 1)
            pool.tensor_copy(rw2_wide[:, :].rearrange("p (b n) -> p b n", b=8)[:, :, 0:E1],
                             rw2[:, :].unsqueeze(1).broadcast_to((D, 8, E1))).then_inc(R.wide, 1)

            def body(b, u):
                f, uf = b + 1, 1 - u
                if isinstance(b, int) and b == -1:
                    pool_ctx(pool, Z, 0, 0)
                    pool_ctx(pool, Z, 1, 1)
                if there(b + 2) and not (isinstance(b, int) and b == -1):
                    pool_ctx(pool, Z, b + 2, u)
            pipelined(pool, body)
            engines_meet(pool, 3)
            rstds(4)

            def body(b, u):
                pool.wait_ge(R.tr, 4)
                after(pool, G.got, b - 1)
                pool.tensor_copy(xn[:, u, :], xn_all[:, b, :]).then_inc(G.xn, 1)
            body(0, 0)
            body(1, 1)
            with pool.Fori(0, B // 2 - 1) as i:
                body(i * 2 + 2, 0)
                body(i * 2 + 3, 1)
            engines_meet(pool, 4)
            engines_meet(pool, 5)

        @block.vector
        def _(dve):
            dve.wait_ge(got.x, 16)

            for b in range(B):
                dve_stats(dve, ln, b)

            def variances(stats_done, n):
                dve.wait_ge(stats_done, B)
                for b in range(B):
                    dve.bn_aggr(mv[:, b, :], stats[:, b, :]).then_inc(ln.mv, 1)
                dve.wait_ge(ln.mv, n * B)
                dve.tensor_scalar(veps[:, :], mv[:, :, 1], EPS, None, ALU.add).then_inc(ln.veps, 1)
            variances(ln.stats, 1)
            dve.memset(vm[:, :, :, :, :], 0.0).then_inc(made.vm, 1)
            dve.wait_ge(made.vm, 1)
            dve.memset(vm[:, :, :, :, 64:64 + D0], 1.0).then_inc(made.vm, 1)
            dve.wait_ge(got.attn0, 16 * 8)
            dve.wait_ge(made.consts, 2)
            dve.wait_ge(made.hmask, 3)
            dve.wait_ge(ln.rstd, 1)
            dve_xn(dve, A, 0, 0)

            def norm(t, ut):
                dve.wait_ge(A.pv, t * NCH + NCH)
                dve.reciprocal(rsum0[:, ut, :, :], OB[ut][64:128, 0:256].rearrange("p (a n) -> p a n", a=2))\
                    .then_inc(A.rsum, 1)
                dve.wait_ge(A.rsum, t + 1)
                dve.tensor_tensor(o0T[:, ut, :, :], OB[ut][0:64, 0:256].rearrange("p (a n) -> p a n", a=2),
                                  rsum0[:, ut, :, :], ALU.mult).then_inc(A.o, 1)

            def body(b, u):
                f, t, uo = b + 1, b - 1, 1 - u
                if there(t):
                    norm(t, uo)
                if there(f):
                    dve.wait_ge(A.q_sb, f + 1)
                    dve.tensor_tensor(qm[:, uo, :, :], qT[:, uo, :].unsqueeze(1).broadcast_to((128, H, 128)),
                                      hmask[:, :].unsqueeze(2).broadcast_to((128, H, 128)), ALU.mult)\
                        .then_inc(A.qm, 1)
                    dve.wait_ge(A.v, f + 1)
                    dve.tensor_tensor(vm[:, uo, :, :, 0:D0],
                                      PB[1][:, 0:D].rearrange("p (a h d) -> p a h d", a=2, h=8),
                                      bv0[:, :].rearrange("p (a h d) -> p a h d", a=2, h=8), ALU.add)\
                        .then_inc(A.v_sb, 1)
                if there(t):
                    dve.wait_ge(A.proj, t + 1)
                    dve_residual(dve, A, t, TB[:, 0:D])
                if there(f):
                    dve_max(dve, A, f, 0, 0, S)
                if there(t):
                    dve_stats(dve, A, t)
                if there(f):
                    for j in range(1, NCH):
                        dve_max(dve, A, f, j, CH * j, S)
                    dve_negmaxT(dve, A, f, uo, H)
                if there(b + 2):
                    dve_xn(dve, A, b + 2, u)
            pipelined(dve, body)
            engines_meet(dve, 1)
            variances(A.stats, 2)
            dve.wait_ge(F.gate_tr, 1)
            dve.tensor_copy(gateT[:, :], TB[:, 0:E0]).then_inc(F.gateT, 1)
            dve.wait_ge(F.lower, 2)
            dve.wait_ge(ln.rstd, 2)
            for b in range(B):
                dve.tensor_scalar(xn0[:, b, :], x_all[:, b, :], mv[:, b, 0:1], rstd[:, b, :],
                                  ALU.subtract, ALU.mult).then_inc(F.xn, 1)
            steps = 0

            def step(ins):
                nonlocal steps
                steps += 1
                ins.then_inc(F.step, 1)
                dve.wait_ge(F.step, steps)
            each, pairs = (128, B, E0), (128, B, E0, E0)
            dve.wait_ge(F.logit, B)
            step(dve.tensor_copy(lg[:, :, :], PB[0][:, 0:B * E0].rearrange("p (b e) -> p b e", b=B)))
            step(dve.tensor_reduce(top0[:, :], lg[:, :, :], X, ALU.max))
            step(dve.tensor_tensor(ew[:, :, :], lg[:, :, :], top0[:, :].unsqueeze(2).broadcast_to(each), ALU.subtract))
            mine = lg[:, :, :].unsqueeze(3).broadcast_to(pairs)
            other = lg[:, :, :].unsqueeze(2).broadcast_to(pairs)
            step(dve.tensor_tensor(tie[:, :, :, :], other, mine, ALU.is_ge))
            step(dve.tensor_tensor(tie[:, :, :, :], tie[:, :, :, :], lower[:, :, :].unsqueeze(1).broadcast_to(pairs),
                                   ALU.mult))
            step(dve.tensor_tensor(beat[:, :, :, :], other, mine, ALU.is_gt))
            step(dve.tensor_tensor(beat[:, :, :, :], beat[:, :, :, :], tie[:, :, :, :], ALU.max))
            step(dve.tensor_reduce(nbeat[:, :, :], beat[:, :, :, :], X, ALU.add))
            dve.wait_ge(F.ex, 1)
            step(dve.scalar_tensor_tensor(ew[:, :, :], nbeat[:, :, :], 1.5, ew[:, :, :], ALU.is_lt, ALU.mult))
            step(dve.tensor_reduce(wsum[:, :], ew[:, :, :], X, ALU.add))
            step(dve.reciprocal(wsum[:, :], wsum[:, :]))
            step(dve.tensor_tensor(ffn_w[:, :, :], ew[:, :, :], wsum[:, :].unsqueeze(2).broadcast_to(each), ALU.mult))

            def body(b, u):
                t, half = b - 1, E0 // 2
                if there(b):
                    dve.wait_ge(F.y, b + 1)
                    dve.tensor_tensor(ys[:, u, half:E0, :], blocks((SCB, OB)[u][1]),
                                      ffn_w[:, b, half:E0].unsqueeze(2).broadcast_to((128, half, D)), ALU.mult)\
                        .then_inc(F.ys1, 1)
                if there(t):
                    dve.wait_ge(F.ysum, t + 1)
                    dve_residual(dve, F, t, ysum[:, 1 - u, :])
                if there(b):
                    dve.wait_ge(F.ys1, b + 1)
                    dve.wait_ge(F.ys0, 4 * b + 4)
                    dve.tensor_reduce(ysum[:, u, :], ys[:, u, :, :].rearrange("p e d -> p d e"), X, ALU.add)\
                        .then_inc(F.ysum, 1)
                if there(t):
                    dve_stats(dve, F, t)
            body(0, 0)
            body(1, 1)
            with dve.Fori(0, B // 2 - 1) as i:
                body(i * 2 + 2, 0)
                body(i * 2 + 3, 1)
            body(B, 0)
            engines_meet(dve, 2)
            variances(F.stats, 3)

            dve.wait_ge(ln.rstd, 3)
            dve_xn(dve, Z, 0, 0)

            def norm(b, u, j):
                dve.wait_ge(Z.pv, b * NCH + j + 1)
                got_o = OB[j % 2][:, 0:CH * (D1 + 1)].rearrange("p (h d) -> p h d", h=CH)
                sums = rsum[:, u, CH * j:CH * j + CH]
                dve.reciprocal(sums, got_o[:, :, D1]).then_inc(Z.rsum, 1)
                dve.wait_ge(Z.rsum, b * NCH + j + 1)
                dve.tensor_tensor(o[:, u, CH * D1 * j:CH * D1 * (j + 1)].rearrange("p (h d) -> p h d", h=CH),
                                  got_o[:, :, 0:D1], sums.unsqueeze(2).broadcast_to((128, CH, D1)), ALU.mult)\
                    .then_inc(Z.o, 1)

            def ipa_scores(f, uf):
                dve.wait_ge(Z.ipa_score, f + 1)
                sc = TB[:, 0:H * IPA].rearrange("p (h j) -> p h j", h=H)
                dve.tensor_reduce(ipa_max[:, uf, :], sc, X, ALU.max).then_inc(Z.ipa_step, 1)
                dve.wait_ge(Z.ipa_step, f * 3 + 1)
                dve.tensor_tensor(ipa_s[:, uf, :, :], sc, ipa_max[:, uf, :].unsqueeze(2).broadcast_to((128, H, IPA)),
                                  ALU.subtract).then_inc(Z.ipa_sub, 1)

            def ipa_norm(f, uf):
                dve.wait_ge(Z.ipa_exp, f + 1)
                dve.tensor_reduce(ipa_sum[:, uf, :], ipa_s[:, uf, :, :], X, ALU.add).then_inc(Z.ipa_step, 1)
                dve.wait_ge(Z.ipa_step, f * 3 + 2)
                dve.reciprocal(ipa_sum[:, uf, :], ipa_sum[:, uf, :]).then_inc(Z.ipa_step, 1)
                dve.wait_ge(Z.ipa_step, f * 3 + 3)
                dve.tensor_tensor(ipa_s[:, uf, :, :], ipa_s[:, uf, :, :],
                                  ipa_sum[:, uf, :].unsqueeze(2).broadcast_to((128, H, IPA)), ALU.mult)\
                    .then_inc(Z.ipa_p, 1)

            def body(b, u):
                f, t, uo = b + 1, b - 1, 1 - u
                if there(t):
                    norm(t, uo, 3)
                if there(f):
                    ipa_scores(f, uo)
                    dve.wait_ge(Z.k0, f + 1)
                    dve.tensor_copy(kT[:, uo, 0:4, 0:ORG], blocks(PB[0])[:, :, 0:ORG]).then_inc(Z.k0_sb, 1)
                if there(b):
                    norm(b, u, 0)
                if there(f):
                    dve.wait_ge(Z.k2, f + 1)
                    dve.tensor_copy(kT[:, uo, 8:12, 0:ORG], blocks(PB[0])[:, :, 0:ORG]).then_inc(Z.k2_sb, 1)
                    ipa_norm(f, uo)
                if there(t):
                    dve.wait_ge(Z.proj, t + 1)
                    dve_residual(dve, Z, t, TB[:, 0:D])
                if there(f):
                    dve_max(dve, Z, f, 0, 0, ORG)
                if there(t):
                    dve_stats(dve, Z, t)
                if there(f):
                    dve.wait_ge(Z.v0, f + 1)
                    dve.tensor_copy(v1[0:ORG, uo, 0:8, 0:D1], PB[0][0:ORG, :].rearrange("p (h d) -> p h d", h=8))\
                        .then_inc(Z.v0_sb, 1)
                if there(b):
                    norm(b, u, 1)
                if there(f):
                    dve_max(dve, Z, f, 1, CH, ORG)
                    dve_max(dve, Z, f, 2, 2 * CH, ORG)
                    dve.wait_ge(Z.ipa_turn, f + 1)
                    dve.tensor_copy(ipa_pT[:, uo, :], TB[0:H * IPA, 0:128]).then_inc(Z.ipa_pT, 1)
                    dve_max(dve, Z, f, 3, 3 * CH, ORG)
                if there(b):
                    norm(b, u, 2)
                if there(f):
                    dve_negmaxT(dve, Z, f, uo, H)
                if there(b + 2):
                    dve_xn(dve, Z, b + 2, u)
            pipelined(dve, body)
            engines_meet(dve, 3)
            variances(Z.stats, 4)

            dve.wait_ge(ln.rstd, 4)
            for b in range(B):
                dve.tensor_scalar(xn_all[:, b, :], x_all[:, b, :], mv[:, b, 0:1], rstd[:, b, :],
                                  ALU.subtract, ALU.mult).then_inc(R.xn, 1)
            steps = 0

            def step(ins):
                nonlocal steps
                steps += 1
                ins.then_inc(R.step, 1)
                dve.wait_ge(R.step, steps)
            for t in range(2):
                dve.wait_ge(R.logit, t + 1)
                step(dve.tensor_reduce(ex_max[:, t, :], bank[4 + t][:, 0:128], X, ALU.max, negate=True))
                dve.wait_ge(R.ex, t + 1)
                step(dve.tensor_reduce(ex_sum[:, t, :], probs[:, t, :], X, ALU.add))
                step(dve.reciprocal(ex_sum[:, t, :], ex_sum[:, t, :]))
                step(dve.tensor_scalar(probs[:, t, :], probs[:, t, :], ex_sum[:, t, :], None, ALU.mult))
                for n in range(CAP // 8):
                    eight = slice(8 * n, 8 * n + 8)
                    step(dve.max(top[:, t, eight], probs[:, t, :]))
                    step(dve.max_index(top_at[:, t, eight], top[:, t, eight], probs[:, t, :]))
                    if n < CAP // 8 - 1:
                        step(dve.match_replace(probs[:, t, :], top[:, t, eight], probs[:, t, :], -1.0))
                step(dve.tensor_copy(top_at_f[:, t, :], top_at[:, t, :]))
                step(dve.tensor_reduce(ex_sum[:, t, :], top[:, t, :], X, ALU.add))
                step(dve.tensor_scalar(ex_sum[:, t, :], ex_sum[:, t, :], 1e-9, None, ALU.add))
                step(dve.reciprocal(ex_sum[:, t, :], ex_sum[:, t, :]))
                step(dve.tensor_scalar(top[:, t, :], top[:, t, :], ex_sum[:, t, :], None, ALU.mult))
            for t in range(2):
                dve.wait_ge(R.turned, t + 1)
                for n, to in enumerate((slot_at, slot_w)):
                    dve.tensor_copy(to[:, 8 * t:8 * t + 8, :],
                                    bank[6 + t][:, 32 * n:32 * n + 32].rearrange("p (b g) -> p b g", b=8))\
                        .then_inc(R.slot, 1)
            dve.wait_ge(R.slot, 4)
            dve.wait_ge(R.count, 2)

            def body(b, u):
                after(dve, G.turned, b - 1)
                for g in range(EG):
                    ins = dve.tensor_scalar(oh_bf[:, u, g, :], count[:, :], slot_at[:, b, g:g + 1], None, ALU.is_equal)
                ins.then_inc(G.row, 1)
            body(0, 0)
            body(1, 1)
            with dve.Fori(0, B // 2 - 1) as i:
                body(i * 2 + 2, 0)
                body(i * 2 + 3, 1)
            engines_meet(dve, 4)

            def gated(e, g, q):
                for c in range(2):
                    dve.wait_ge(X1.silu, 2 * e + c + 1)
                    dve.tensor_tensor(hs[:, q % 2, c, :], sg[:, c, :], bank[2 * c + 1][:, :], ALU.mult)\
                        .then_inc(X1.h, 1)

            def body(e, g, q):
                if there_expert(e + 1):
                    gated(e + 1, g, q + 1)
                dve.wait_ge(X1.eo, e + 1)
                for n in range(4):
                    ins = dve.tensor_copy(eo_rows(g, q, 1, n), eo_got(q, 1, n))
                ins.then_inc(X1.eo_dve, 1)
            dve.drain().then_inc(X1.eo_dve, 2)
            experts(dve, gated, body)
            engines_meet(dve, 5)

            def body(b, u):
                after(dve, Y.sum, b - 1)
                for g in range(EG):
                    ins = dve.tensor_scalar(ohw[:, u, g, :], count[:, :], slot_at[:, b, g:g + 1],
                                            slot_w[:, b, g:g + 1], ALU.is_equal, ALU.mult)
                ins.then_inc(Y.row, 1)
                t = b - 1
                if there(t):
                    residual(t, 1 - u)

            def residual(t, ut):
                dve.wait_ge(Y.sum, t + 1)
                dve.tensor_tensor(x_all[:, t, :], bank[ut][:, 0:D], x_all[:, t, :], ALU.add).then_inc(Y.x_new, 1)
            body(0, 0)
            body(1, 1)
            with dve.Fori(0, B // 2 - 1) as i:
                body(i * 2 + 2, 0)
                body(i * 2 + 3, 1)
            residual(B - 1, 1)

        @block.scalar
        def _(act):
            act.preload_act_table(ACT.Exp)
            act.wait_ge(got.attn0, 16 * 8)
            act.wait_ge(made.hmask, 3)

            def body(b, u):
                f, uf = b + 1, 1 - u
                if there(f):
                    act_transposed_in(act, A, PB[1], f, uf)
                if there(b):
                    act_exp(act, A, S, D0, b, 0)
                if there(f):
                    act.wait_ge(A.qk, f + 1)
                    act.activation(qT[:, uf, :], PB[0][:, 0:128], ACT.Identity, bias=bq0[:, :])\
                        .then_inc(A.q_sb, 1)
                    act.activation(q_bf[:, uf, :], PB[0][:, 0:128], ACT.Identity, bias=bq0[:, :])\
                        .then_inc(A.q_bf, 1)
                    act.activation(kT[:, uf, 0, :], PB[0][:, 128:256], ACT.Identity, bias=bk0[:, :])\
                        .then_inc(A.k_sb, 1)
                    act.wait_ge(A.k_sb, f + 1)
                    for h in range(H):
                        if h == 8 and there(b):
                            act_exp(act, A, S, D0, b, 1)
                        ins = act.activation(km_bf[:, uf, h, :], kT[:, uf, 0, :], ACT.Copy, scale=hmask[:, h:h + 1])
                        if h % CH == CH - 1:
                            ins.then_inc(A.km, 1)
                elif there(b):
                    act_exp(act, A, S, D0, b, 1)
                if there(b):
                    act_exp(act, A, S, D0, b, 2)
                    act_exp(act, A, S, D0, b, 3)
            pipelined(act, body)
            engines_meet(act, 1)

            act.wait_ge(got.attn1, 16 * 20)
            act.activation(alpha[:, :], alpha[:, :], ACT.Copy, scale=1.0 / RANK).then_inc(W.alpha, 1)
            act.wait_ge(W.alpha, 1)
            act.wait_ge(W.turned, 3)
            for n, rows in enumerate((D, C, C)):
                act.activation(downT[:, n, 0:rows], blocks(PB[0], RANK)[:, n, 0:rows], ACT.Copy,
                               scale=alpha[0:RANK, n:n + 1]).then_inc(W.downT, 1)
            for n in range(2):
                act.activation(downT[:, 3 + 4 * n:7 + 4 * n, :], blocks(SCB[n], RANK), ACT.Copy,
                               scale=alpha[0:RANK, 3:4]).then_inc(W.downT, 1)

            def folded(n, to, got_w):
                act.wait_ge(W.whole, n)
                act.activation(to, got_w, ACT.Copy).then_inc(W.folded, 1)
            for n in range(2):
                folded(n + 1, wq1T[:, 4 * n:4 * n + 4, :], blocks(OB[n]))
            for n in range(4):
                act.wait_ge(F.tr, n + 1)
                act.activation(xT0[:, 4 * n:4 * n + 4, :], blocks((TB, MAXB)[n % 2]), ACT.Copy).then_inc(F.xT, 1)
            act.wait_ge(F.step, 3)
            act.activation(ew[:, :, :], ew[:, :, :], ACT.Exp).then_inc(F.ex, 1)
            for n in range(2):
                folded(n + 3, wk1T[:, 4 * n:4 * n + 4, :], bank[(3, 4)[n]][:, 0:4 * C].rearrange("p (c k) -> p c k", c=4))
            for n in range(2):
                folded(n + 5, wv1[:, 512 * n:512 * n + 512], SCB[n][0:C, :])
            for n in range(2):
                folded(n + 7, wo1[:, 4 * n:4 * n + 4, :], blocks((PB[1], TB)[n]))
            for n in range(4):
                act.wait_ge(W.mT_ps, n + 1)
                act.activation(mT[:, :, :].rearrange("c (n g t) d -> c n t g d", n=2, t=2)[:, n // 2, n % 2, :, :],
                               blocks(bank[3 + n % 2], C), ACT.Copy).then_inc(W.mT, 1)
            act.wait_ge(W.ctxT_ps, 1)
            act.activation(ctx_ipaT[:, :], bank[0][0:C, 0:B * IPA], ACT.Copy).then_inc(W.ctxT, 1)
            act.wait_ge(W.zeros, 2)
            for n, (to, done) in enumerate(((ipa_kT, W.kT), (ipa_vT, W.vT))):
                act.wait_ge(W.kv_ps, n + 1)
                for two in range(2):
                    rows = slice(64 * two, 64 * two + 64)
                    act.activation(to[rows, :, :, two, :], bank[1 + n][rows, :].rearrange(
                        "p (c b j) -> p c b j", c=8, b=B), ACT.Copy).then_inc(done, 1)
            for n in range(2):
                act.wait_ge(W.prod, 1 + n)
                act.activation(ipa_k[:, :, 32 * n:32 * n + 32].rearrange("p b (c r) -> p c b r", c=4),
                               bank[3 + n][:, :].rearrange("p (c b r) -> p c b r", c=4, b=B), ACT.Copy).then_inc(W.ipa_k, 1)
            for n in range(2):
                act.wait_ge(W.prod, 3 + n)
                act.activation(ipa_v_rows[:, 4 * n:4 * n + 4, :], blocks(bank[(0, 7)[n]]), ACT.Copy)\
                    .then_inc(W.ipa_v_rows, 1)
            act.wait_ge(F.step, 12)

            def body(b, u):
                act.wait_ge(F.y, b + 1)
                after(act, F.ysum, b - 1)
                for e in range(E0 // 2):
                    act.activation(ys[:, u, e, :], blocks((SCB, OB)[u][0])[:, e, :], ACT.Copy,
                                   scale=ffn_w[:, b, e:e + 1]).then_inc(F.ys0, 1)
            body(0, 0)
            body(1, 1)
            with act.Fori(0, B // 2 - 1) as i:
                body(i * 2 + 2, 0)
                body(i * 2 + 3, 1)
            engines_meet(act, 2)

            def body(b, u):
                f, t, uo = b + 1, b - 1, 1 - u
                if there(f):
                    act_transposed_in(act, Z, TB, f, uo)
                    act.wait_ge(Z.xc_T, 2 * f + 1)
                    act.activation(x_bf[:, uo, :], xT[:, uo, :], ACT.Copy).then_inc(Z.x_bf, 1)
                if there(b):
                    act_exp(act, Z, ORG, D1, b, 0)
                if there(t):
                    for half, done in enumerate((Z.oTr0, Z.oTr1)):
                        act.wait_ge(done, t + 1)
                        act.activation(oT[:, uo, 4 * half:4 * half + 4, :], blocks(PB[half]), ACT.Copy)\
                            .then_inc(Z.oT_sb, 1)
                if there(b):
                    act_exp(act, Z, ORG, D1, b, 1)
                if there(f):
                    act.wait_ge(Z.ipa_sub, f + 1)
                    act.activation(ipa_s[:, uo, :, :], ipa_s[:, uo, :, :], ACT.Exp, scale=D1 ** -0.5)\
                        .then_inc(Z.ipa_exp, 1)
                    for n, (done, copied, other) in enumerate(((Z.k1, Z.k1_sb, Z.k0_sb), (Z.k3, Z.k3_sb, Z.k2_sb))):
                        act.wait_ge(done, f + 1)
                        act.activation(kT[:, uo, 8 * n + 4:8 * n + 8, 0:ORG], blocks(PB[1])[:, :, 0:ORG], ACT.Copy)\
                            .then_inc(copied, 1)
                        act.wait_ge(other, f + 1)
                        act.wait_ge(copied, f + 1)
                        after(act, Z.smax, (f - 1) * NCH)
                        act.activation(k_bf[:, uo, 8 * n:8 * n + 8, 0:ORG], kT[:, uo, 8 * n:8 * n + 8, 0:ORG], ACT.Copy)\
                            .then_inc(Z.k_bf, 1)
                if there(b):
                    act_exp(act, Z, ORG, D1, b, 2)
                if there(f):
                    act.wait_ge(Z.v1, f + 1)
                    act.activation(v1[0:ORG, uo, 8:16, 0:D1], PB[1][0:ORG, :].rearrange("p (h d) -> p h d", h=8),
                                   ACT.Copy).then_inc(Z.v1_sb, 1)
                if there(b):
                    act_exp(act, Z, ORG, D1, b, 3)
            pipelined(act, body)
            engines_meet(act, 3)
            act.preload_act_table(ACT.Silu)
            for n in range(4):
                act.wait_ge(R.tr, n + 1)
                act.activation(xT4[:, n % 2, :, :], blocks(bank[n % 2]), ACT.Copy).then_inc(R.xT, 1)
                act.wait_ge(R.hid, n + 1)
                act.activation(hT4[:, n % 2, 0:4, :], blocks(bank[2 + n % 2]), ACT.Silu).then_inc(R.h, 1)
            for t in range(2):
                act.wait_ge(R.step, t * (4 + 11 + 5) + 1)
                act.activation(probs[:, t, :], bank[4 + t][:, 0:128], ACT.Exp, bias=ex_max[:, t, :]).then_inc(R.ex, 1)

            def body(b, u):
                t = b - 1
                if there(b):
                    act.wait_ge(G.turned, b + 1)
                    after(act, G.got, b - 1)
                    act.activation(oh[:, u, 0:4, 0:128], blocks(bank[u]), ACT.Copy).then_inc(G.oh, 1)
                if there(t):
                    act.wait_ge(G.got, t + 1)
                    act.activation(xgT[:, t, :, :], bank[2 + (1 - u)][:, :].rearrange("p (e s) -> p e s", e=E1), ACT.Copy)\
                        .then_inc(G.xg, 1)
            body(0, 0)
            body(1, 1)
            with act.Fori(0, B // 2 - 1) as i:
                body(i * 2 + 2, 0)
                body(i * 2 + 3, 1)
            body(B, 0)
            act.preload_act_table(ACT.Silu)
            engines_meet(act, 4)

            def silus(e, g, q):
                for c in range(2):
                    act.wait_ge(X1.gv, 2 * e + c + 1)
                    after(act, X1.h, 2 * e + c - 1)
                    act.activation(sg[:, c, :], bank[2 * c][:, :], ACT.Silu).then_inc(X1.silu, 1)

            def body(e, g, q):
                if there_expert(e + 1):
                    silus(e + 1, g, q + 1)
                act.wait_ge(X1.eo, e + 1)
                for n in range(4):
                    ins = act.activation(eo_rows(g, q, 0, n), eo_got(q, 0, n), ACT.Copy)
                ins.then_inc(X1.eo_act, 1)
            act.drain().then_inc(X1.eo_act, 2)
            experts(act, silus, body)
            engines_meet(act, 5)

        @block.tensor
        def _(pe):
            pe.wait_ge(made.ident, 5)
            pe.wait_ge(made.pick, 3)
            pe.wait_ge(made.vm, 2)
            pe.wait_ge(got.attn0, 16 * 8)

            def maxima(f, uf, j):
                pe.wait_ge(A.km, f * NCH + j + 1)
                after(pe, A.maxed, f * NCH + j)
                pe.matmul(blocks(MAXB), q_bf[:, uf, :], km_bf[:, uf, CH * j:CH * j + CH, :],
                          start=True, stop=True).then_inc(A.smax, 1)

            def scores(b, u, j):
                if j == 0:
                    pe.wait_ge(A.negT_sb, b + 1)
                    pe.wait_ge(A.qm, b + 1)
                    pe.wait_ge(A.k_sb, b + 1)
                after(pe, A.exp, b * NCH + j - 1)
                for g in range(CH):
                    h = CH * j + g
                    to = blocks(SCB[j % 2])[:, g, :]
                    pe.matmul(to, pick[0:H, h, :], negmaxT[0:H, u, :], start=True, stop=False)
                    mm = pe.matmul(to, kT[:, u, 0, :], qm[:, u, h, :], start=False, stop=True)
                mm.then_inc(A.score, 1)

            def values(b, u, j):
                pe.wait_ge(A.exp, b * NCH + j + 1)
                if j == 0:
                    pe.wait_ge(A.v_sb, b + 1)
                    after(pe, A.o, b - 1)
                half = j // 2
                for g in range(CH):
                    h = CH * (j % 2) + g
                    own = vm[:, u, half, :, :].rearrange("p h c -> p (h c)")[:, 128 * h:128 * h + 128]
                    mm = pe.matmul(OB[u][:, half * 128:half * 128 + 128], own, pT[:, j % 2, g, :],
                                   start=(h == 0), stop=(h == 7))
                mm.then_inc(A.pv, 1)

            def body(b, u):
                f, t, uo = b + 1, b - 1, 1 - u
                if there(f):
                    pe_transpose_in(pe, A, PB[1], f, uo, f)
                if there(b):
                    scores(b, u, 0)
                if there(f):
                    pe.wait_ge(A.xc_T, 2 * f + 2)
                    after(pe, A.km, f * NCH)
                    pe.matmul(PB[0][:, 0:128], wq0[:, :], xT[:, uo, :], start=True, stop=True)
                    pe.matmul(PB[0][:, 128:256], wk0[:, :], cT[:, uo, :], start=True, stop=True).then_inc(A.qk, 1)
                    pe.matmul(PB[1][:, 0:D], cT[:, uo, :], wv0[:, :], start=True, stop=True).then_inc(A.v, 1)
                if there(b):
                    scores(b, u, 1)
                if there(t):
                    pe.wait_ge(A.o, t + 1)
                    if there(f):
                        after(pe, A.negT_sb, f)
                    for half in range(2):
                        pe.matmul(TB[:, 0:D], o0T[:, uo, half, :], wo0[:, half, :], start=(half == 0), stop=False)
                    pe.matmul(TB[:, 0:D], ones_row[:, :], bo0[:, :], start=False, stop=True).then_inc(A.proj, 1)
                if there(b):
                    values(b, u, 0)
                if there(f):
                    maxima(f, uo, 0)
                if there(b):
                    scores(b, u, 2)
                if there(f):
                    maxima(f, uo, 1)
                if there(b):
                    values(b, u, 1)
                if there(f):
                    maxima(f, uo, 2)
                if there(b):
                    scores(b, u, 3)
                if there(f):
                    maxima(f, uo, 3)
                if there(b):
                    values(b, u, 2)
                if there(f):
                    after(pe, A.x_new, f - 1)
                    pe.wait_ge(A.maxed, f * NCH + NCH)
                    pe.matmul(TB[0:H, 0:128], negmax[:, 0:H], ident_bf[:, :], start=True, stop=True)\
                        .then_inc(A.negT, 1)
                if there(b):
                    values(b, u, 3)
            pipelined(pe, body)
            engines_meet(pe, 1)
            pe.wait_ge(got.attn1, 16 * 20)
            for n, rows in enumerate((D, C, C)):
                mm = pe.transpose(PB[0][0:RANK, 128 * n:128 * n + rows], down[0:rows, n, :], ident[0:rows, 0:rows])
            mm.then_inc(W.turned, 1)
            for n in range(2):
                for c in range(4):
                    mm = pe.transpose(blocks(SCB[n], RANK)[:, c, :], down_o[:, 4 * n + c, :], ident[:, :])
                mm.then_inc(W.turned, 1)

            def turned_weights(n, w, part, rows, to):
                for c in range(4):
                    block_c = slice(128 * (4 * n + c), 128 * (4 * n + c) + 128)
                    pe.matmul(to[:, rows * c:rows * c + rows], w[:, block_c], ident[0:rows, 0:rows], start=True, stop=False)
                    mm = pe.matmul(to[:, rows * c:rows * c + rows], up[:, part, block_c], downT[:, part, 0:rows],
                                   start=False, stop=True)
                mm.then_inc(W.whole, 1)
            pe.wait_ge(W.downT, 5)
            for n in range(2):
                turned_weights(n, wq1, 0, D, OB[n])
            pe.wait_ge(got.ffn0, 32)
            pe.transpose(TB[:, 0:E0], gate_in[:, :], ident[0:E0, 0:E0]).then_inc(F.gate_tr, 1)
            pe.wait_ge(F.gateT, 1)

            def logits(n):
                pe.wait_ge(F.xT, n + 1)
                for b in range(4 * n, 4 * n + 4):
                    pe.matmul(PB[0][:, E0 * b:E0 * b + E0], xT0[:, b, :], gateT[:, :], start=True, stop=True)\
                        .then_inc(F.logit, 1)
            for n in range(4):
                pe.wait_ge(F.xn, 4 * n + 4)
                after(pe, F.xT, n - 1)
                for k in range(4):
                    mm = pe.transpose(blocks((TB, MAXB)[n % 2])[:, k, :], xn0[:, 4 * n + k, :], ident[:, :])
                mm.then_inc(F.tr, 1)
                if n >= 1:
                    logits(n - 1)
            logits(3)

            for n in range(2):
                pe.wait_ge(W.folded, n + 1)
                turned_weights(n, wk1, 1, C, OB[n])
            for n in range(2):
                part = slice(512 * n, 512 * n + 512)
                pe.matmul(SCB[n][0:C, :], ident[0:C, 0:C], wv1[:, part], start=True, stop=False)
                pe.matmul(SCB[n][0:C, :], downT[:, 2, 0:C], up[:, 2, part], start=False, stop=True).then_inc(W.whole, 1)
            pe.wait_ge(F.xT, 4)
            for n, to in enumerate((PB[1], TB)):
                for c in range(4):
                    pe.matmul(blocks(to)[:, c, :], ident[:, :], wo1[:, 4 * n + c, :], start=True, stop=False)
                    mm = pe.matmul(blocks(to)[:, c, :], downT[:, 3 + 4 * n + c, :], up_o[:, :], start=False, stop=True)
                mm.then_inc(W.whole, 1)
            for n in range(4):
                pe.wait_ge(W.folded, 4) if n == 0 else None
                after(pe, W.mT, n - 1)
                rows = slice(D1 * (n % 2), D1 * (n % 2) + D1)
                for g in range(CH):
                    c = CH * (n // 2) + g
                    mm = pe.matmul(blocks(bank[3 + n % 2], C)[:, g, :], wk1T[rows, c, :], wq1T[rows, c, :],
                                   start=True, stop=True)
                mm.then_inc(W.mT_ps, 1)
            pe.transpose(bank[0][0:C, 0:B * IPA], ctx_ipa[:, :], ident[0:B * IPA, 0:B * IPA]).then_inc(W.ctxT_ps, 1)
            pe.wait_ge(W.ctxT, 1)
            pe.wait_ge(W.folded, 8)
            for n, w in enumerate((wki, wvi)):
                for c in range(8):
                    mm = pe.matmul(bank[1 + n][:, 64 * c:64 * c + 64], w[:, 128 * c:128 * c + 128], ctx_ipaT[:, :],
                                   start=True, stop=True)
                mm.then_inc(W.kv_ps, 1)
            pe.wait_ge(W.mT, 4)
            pe.wait_ge(W.kT, 2)
            for n in range(2):
                for c in range(4):
                    mm = pe.matmul(blocks(bank[3 + n])[:, c, :], wq1T[:, 4 * n + c, :],
                                   ipa_kT[:, 4 * n + c, :, :, :], start=True, stop=True)
                mm.then_inc(W.prod, 1)
            pe.wait_ge(W.vT, 2)
            for n in range(2):
                for c in range(4):
                    mm = pe.matmul(blocks(bank[(0, 7)[n]])[:, c, :], ipa_vT[:, 4 * n + c, :, :, :],
                                   wo1[:, 4 * n + c, :], start=True, stop=True)
                mm.then_inc(W.prod, 1)
            pe.wait_ge(W.ipa_k, 2)

            def body(b, u):
                pe.wait_ge(F.slot, b + 1)
                if there(b - 2):
                    pe.wait_ge(F.ys0, 4 * (b - 1))
                    pe.wait_ge(F.ys1, b - 1)
                for half in range(2):
                    mm = pe.matmul(blocks((SCB, OB)[u][half]), xT[:, u, :], we[:, 4 * half:4 * half + 4, :],
                                   start=True, stop=True)
                mm.then_inc(F.y, 1)
            body(0, 0)
            body(1, 1)
            with pe.Fori(0, B // 2 - 1) as i:
                body(i * 2 + 2, 0)
                body(i * 2 + 3, 1)
            engines_meet(pe, 2)

            def maxima(f, uf, j):
                if j == 0:
                    pe.wait_ge(Z.x_bf, f + 1)
                pe.wait_ge(Z.k_bf, 2 * f + 1 + j // 2)
                after(pe, Z.maxed, f * NCH + j)
                pe.matmul(blocks(MAXB)[:, :, 0:ORG], x_bf[:, uf, :], k_bf[:, uf, CH * j:CH * j + CH, 0:ORG],
                          start=True, stop=True).then_inc(Z.smax, 1)

            def scores(b, u, j):
                if j == 0:
                    for s in (Z.negT_sb, Z.k0_sb, Z.k1_sb, Z.k2_sb, Z.k3_sb):
                        pe.wait_ge(s, b + 1)
                after(pe, Z.exp, b * NCH + j - 1)
                for g in range(CH):
                    h = CH * j + g
                    to = blocks(SCB[j % 2], ORG)[:, g, :]
                    pe.matmul(to, pick[0:H, h, 0:ORG], negmaxT[0:H, u, :], start=True, stop=False)
                    mm = pe.matmul(to, kT[:, u, h, 0:ORG], xT[:, u, :], start=False, stop=True)
                mm.then_inc(Z.score, 1)

            def values(b, u, j):
                pe.wait_ge(Z.exp, b * NCH + j + 1)
                if j == 0:
                    pe.wait_ge(Z.v0_sb, b + 1)
                    pe.wait_ge(Z.v1_sb, b + 1)
                after(pe, Z.o, b * NCH + j - 1)
                for g in range(CH):
                    mm = pe.matmul(OB[j % 2][:, (D1 + 1) * g:(D1 + 1) * (g + 1)], pT[0:ORG, j % 2, g, :],
                                   v1[0:ORG, u, CH * j + g, :], start=True, stop=True)
                mm.then_inc(Z.pv, 1)

            def keys(n, uf, f, done, freed_by):
                after(pe, *freed_by)
                for g in range(CH):
                    mm = pe.matmul(blocks(PB[n % 2])[:, g, 0:ORG], mT[:, CH * n + g, :], cT[:, uf, 0:ORG],
                                   start=True, stop=True)
                mm.then_inc(done, 1)

            def body(b, u):
                f, t, uo = b + 1, b - 1, 1 - u
                if there(f):
                    pe.wait_ge(Z.xn, f + 1)
                    pe.wait_ge(Z.ctx_in, f + 1)
                    after(pe, Z.negT_sb, f)
                    pe.transpose(TB[:, 0:128], xn[:, uo, :], ident[:, :])
                    pe.transpose(TB[0:C, 128:256], ctx_in[:, uo, :], ident[:, :]).then_inc(Z.tr, 1)
                if there(b):
                    scores(b, u, 0)
                if there(t):
                    pe.wait_ge(Z.o, t * NCH + NCH)
                    pe.wait_ge(Z.v0_sb, t + 2) if there(b) else None
                    pe.wait_ge(Z.v1_sb, t + 2) if there(b) else None
                    for half, done in enumerate((Z.oTr0, Z.oTr1)):
                        for c in range(4):
                            n = 4 * half + c
                            mm = pe.transpose(blocks(PB[half])[:, c, :], o[:, uo, 128 * n:128 * n + 128], ident[:, :])
                        mm.then_inc(done, 1)
                if there(b):
                    scores(b, u, 1)
                if there(f):
                    pe.wait_ge(Z.xc_T, 2 * f + 2)
                    pe.matmul(TB[:, 0:H * IPA], xT[:, uo, :], ipa_k[:, f, :], start=True, stop=True)\
                        .then_inc(Z.ipa_score, 1)
                    if there(t):
                        pe.wait_ge(Z.oT_sb, 2 * t + 2)
                    keys(0, uo, f, Z.k0, (Z.v0_sb, f))
                    keys(1, uo, f, Z.k1, (Z.v1_sb, f))
                if there(b):
                    values(b, u, 0)
                if there(f):
                    keys(2, uo, f, Z.k2, (Z.k0_sb, f + 1))
                    keys(3, uo, f, Z.k3, (Z.k1_sb, f + 1))
                if there(t):
                    pe.wait_ge(Z.oT_sb, 2 * t + 2)
                    if there(f):
                        pe.wait_ge(Z.ipa_sub, f + 1)
                    for c in range(8):
                        pe.matmul(TB[:, 0:D], oT[:, uo, c, :], wo1[:, c, :], start=(c == 0), stop=False)
                    if isinstance(t, int) and t == 0:
                        pe.wait_ge(W.back, 16 * 8)
                    pe.matmul(TB[:, 0:D], ipa_pT[:, uo, :], ipa_v[:, t, :], start=False, stop=False)
                    pe.matmul(TB[:, 0:D], ones_row[:, :], bo1[:, :], start=False, stop=True).then_inc(Z.proj, 1)
                if there(b):
                    scores(b, u, 2)
                if there(f):
                    maxima(f, uo, 0)
                    for n, (done, freed) in enumerate(((Z.v0, Z.k2_sb), (Z.v1, Z.k3_sb))):
                        pe.wait_ge(freed, f + 1)
                        pe.matmul(PB[n][0:ORG, :], cT[:, uo, 0:ORG], wv1[:, 512 * n:512 * n + 512],
                                  start=True, stop=True).then_inc(done, 1)
                if there(b):
                    values(b, u, 1)
                if there(f):
                    maxima(f, uo, 1)
                if there(b):
                    scores(b, u, 3)
                if there(f):
                    maxima(f, uo, 2)
                    after(pe, Z.x_new, f - 1)
                    pe.wait_ge(Z.ipa_p, f + 1)
                    pe.matmul(TB[0:H * IPA, 0:128], ipa_s[:, uo, :, :].rearrange("p h j -> p (h j)"), ident[:, :],
                              start=True, stop=True).then_inc(Z.ipa_turn, 1)
                    maxima(f, uo, 3)
                if there(b):
                    values(b, u, 2)
                if there(f):
                    pe.wait_ge(Z.maxed, f * NCH + NCH)
                    pe.wait_ge(Z.ipa_pT, f + 1)
                    pe.matmul(TB[0:H, 0:128], negmax[:, 0:H], ident_bf[:, :], start=True, stop=True).then_inc(Z.negT, 1)
                if there(b):
                    values(b, u, 3)
            pipelined(pe, body)
            engines_meet(pe, 3)

            pe.wait_ge(R.wide, 2)
            def turn(n):
                pe.wait_ge(R.xn, 4 * n + 4)
                after(pe, R.xT, n - 1)
                for k in range(4):
                    mm = pe.transpose(blocks(bank[n % 2])[:, k, :], xn_all[:, 4 * n + k, :], ident[:, :])
                mm.then_inc(R.tr, 1)
            turn(0)
            for n in range(4):
                if n < 3:
                    turn(n + 1)
                pe.wait_ge(R.xT, n + 1)
                after(pe, R.h, n - 1)
                pe.matmul(bank[2 + n % 2][:, :], rw1[:, :], xT4[:, n % 2, :, :], start=True, stop=True).then_inc(R.hid, 1)
                pe.wait_ge(R.h, n + 1)
                for k in range(4):
                    b = 4 * n + k
                    mm = pe.matmul(bank[4 + n // 2][:, 0:128], rw2_of(b), hT4[:, n % 2, k, :],
                                   start=(b % 8 == 0), stop=(b % 8 == 7))
                if n % 2:
                    mm.then_inc(R.logit, 1)
            ident4 = ident[:, :].rearrange("p (b g q) -> p q b g", b=8, g=EG)
            for t in range(2):
                pe.wait_ge(R.step, (t + 1) * (4 + 11 + 5))
                for n, what in enumerate((top_at_f, top)):
                    for q in range(4):
                        mm = pe.matmul(bank[6 + t][32 * q:32 * q + 32, 32 * n:32 * n + 32], what[:, t, :],
                                       ident4[:, q, :, :], start=True, stop=True)
                mm.then_inc(R.turned, 1)

            def body(b, u):
                t = b - 1
                if there(b):
                    pe.wait_ge(G.row, b + 1)
                    after(pe, G.oh, b - 1)
                    for g in range(EG):
                        mm = pe.matmul(blocks(bank[u])[:, g, :], oh_bf[:, u, g, :], ident_bf[:, :],
                                       start=True, stop=True)
                    mm.then_inc(G.turned, 1)
                if there(t):
                    pe.wait_ge(G.oh, t + 1)
                    pe.wait_ge(G.xn, t + 1)
                    after(pe, G.xg, t - 1)
                    pe.matmul(bank[2 + (1 - u)][:, :], xn[:, 1 - u, :], oh[:, 1 - u, 0:4, 0:128], start=True, stop=True)\
                        .then_inc(G.got, 1)
            body(0, 0)
            body(1, 1)
            with pe.Fori(0, B // 2 - 1) as i:
                body(i * 2 + 2, 0)
                body(i * 2 + 3, 1)
            body(B, 0)
            engines_meet(pe, 4)

            def inner(e, g, q):
                pe.wait_ge(w_in[q % 4], 48 * (g + q // 4 + 1))
                for c in range(2):
                    after(pe, X1.h, 2 * e + c - 1)
                    for n, w in enumerate((ew1, ew2)):
                        mm = pe.matmul(bank[2 * c + n][:, :], w[:, q % 4, 128 * c:128 * c + 128], xgT[:, :, e, :],
                                       start=True, stop=True)
                    mm.then_inc(X1.gv, 1)

            def body(e, g, q):
                if there_expert(e + 1):
                    inner(e + 1, g, q + 1)
                pe.wait_ge(X1.h, 2 * e + 2)
                pe.wait_ge(X1.eo_act, e + 1)
                pe.wait_ge(X1.eo_dve, e + 1)
                for k in range(4):
                    for c in range(2):
                        mm = pe.matmul(bank[4 + 2 * (q % 2) + k // 2][:, D * (k % 2):D * (k % 2) + D],
                                       hs[:, q % 2, c, 128 * k:128 * k + 128], ew3[:, q % 4, c, :],
                                       start=(c == 0), stop=(c == 1))
                mm.then_inc(X1.eo, 1)
            experts(pe, inner, body)
            engines_meet(pe, 5)

            def body(b, u):
                pe.wait_ge(Y.row, b + 1)
                after(pe, Y.x_new, b - 1)
                for g in range(EG):
                    mm = pe.matmul(bank[u][:, 0:D], ohw[:, u, g, :], eo_all[:, b, g, :], start=(g == 0), stop=(g == 3))
                mm.then_inc(Y.sum, 1)
            body(0, 0)
            body(1, 1)
            with pe.Fori(0, B // 2 - 1) as i:
                body(i * 2 + 2, 0)
                body(i * 2 + 3, 1)


def kernel(**inputs):
    import numpy as _np
    import concourse.bacc as _bacc
    from concourse.bass_utils import run_bass_kernel_spmd as _run

    nc = _bacc.Bacc("TRN2", target_bir_lowering=False, num_devices=1)
    arrays, tensors = {}, {}
    for name, value in inputs.items():
        a = _np.ascontiguousarray(value)
        arrays[f"in_{name}_dram"] = a
        tensors[name] = nc.dram_tensor(f"in_{name}_dram", a.shape, mybir.dt.from_np(a.dtype), kind="ExternalInput").ap()
    out = nc.dram_tensor("out_0_dram", (B, S, D), F32, kind="ExternalOutput").ap()
    build_program(nc, tensors, out)
    r = _run(nc, [arrays], core_ids=[0])
    return r.results[0]["out_0_dram"]
```

```python
from contextlib import ExitStack

import concourse.bass as bass
from concourse import mybir

F32 = mybir.dt.float32
BF16 = mybir.dt.bfloat16
I32 = mybir.dt.int32
ALU = mybir.AluOpType
ACT = mybir.ActivationFunctionType
X = mybir.AxisListType.X

B, S, D = 16, 128, 128
C = 96
H = 16
D0 = D // H
D1 = 64
ID = H * D1
RANK = 32
IPA = 4
ORG = S - IPA
E0 = 8
E1, F1 = 16, 256
EG = E1 // 4
CAP = 32
EPS = 1e-5
CH = 4
NCH = H // CH
BANK = 512


def named(make, prefix, names):
    return type(prefix, (), {name: make(f"{prefix}_{name}") for name in names.split()})


def after(eng, sem, value):
    if not isinstance(value, int) or value >= 1:
        eng.wait_ge(sem, value)


def there(b):
    return not isinstance(b, int) or 0 <= b < B


def there_expert(e):
    return not isinstance(e, int) or e < E1


def pipelined(eng, body, before_last=None):
    for b in (-1, 0, 1):
        body(b, b % 2)
    with eng.Fori(0, (B - 4) // 4) as i:
        for k in range(4):
            body(i * 4 + (k + 2), k % 2)
    for b in (B - 2, B - 1, B):
        if b == B - 1 and before_last:
            before_last()
        body(b, b % 2)


def build_program(nc, T, out):
    with ExitStack() as ctx:
        def sb(name, shape, dt=F32):
            return ctx.enter_context(nc.sbuf_tensor(name, shape, dt))

        def sem(name):
            return ctx.enter_context(nc.semaphore(name))

        bank = [ctx.enter_context(nc.psum_tensor(f"bank{n}", [128, BANK], F32)) for n in range(8)]
        MAXB = bank[0]
        SCB = bank[1:3]
        OB = bank[3:5]
        PB = bank[5:7]
        TB = bank[7]

        def blocks(b_, rows=128):
            return b_[0:rows, :].rearrange("p (g n) -> p g n", g=CH)

        ident = sb("ident", [128, 128])
        ident_bf = sb("ident_bf", [128, 128], BF16)
        pick = sb("pick", [H, H, 128], BF16)
        minus_half = sb("minus_half", [128, B])
        x_all = sb("x_all", [128, B, D])
        ctx_all = sb("ctx_all", [128, B, C])
        stats = sb("stats", [128, B, 6])
        mv = sb("mv", [128, B, 2])
        veps = sb("veps", [128, B])
        rstd = sb("rstd", [128, B, 1])

        class Arena:

            def __init__(self, name, size):
                self.tile, self.size = sb(name, [128, size]), size
                self.again()

            def again(self):
                self.at = 0

            def take(self, shape, dt=F32):
                rows, dims = shape[0], shape[1:]
                n = 1
                for d in dims:
                    n *= d
                words = n if dt in (F32, I32) else n // 2
                assert self.at + words <= self.size, (self.at + words, self.size)
                flat = self.tile[0:rows, self.at:self.at + words]
                self.at += words
                if dt != F32:
                    flat = flat.bitcast(dt)
                letters = "abcde"[:len(dims)]
                return flat.rearrange(f"p ({' '.join(letters)}) -> p {' '.join(letters)}",
                                      **dict(zip(letters, dims)))

        early = Arena("early", 15872)
        late = Arena("late", 11776)
        wide = Arena("wide", 8192)

        ctx_in = sb("ctx_in", [128, 2, 128])
        xn = sb("xn", [128, 2, D])
        xT = sb("xT", [128, 2, 128])
        cT = sb("cT", [128, 2, 128])
        qT = sb("qT", [128, 2, 128])
        q_bf = sb("q_bf", [128, 2, 128], BF16)
        kT = wide.take([128, 2, H, S])
        x_bf = sb("x_bf", [128, 2, 128], BF16)
        k_bf = late.take([128, 2, H, 128], BF16)
        qm = early.take([128, 2, H, 128])
        km_bf = early.take([128, 2, H, 128], BF16)
        vm = early.take([128, 2, 2, 8, 136])
        attn0_slots = early.at
        o0T = sb("o0T", [64 + 1, 2, 2, 128])
        rsum0 = sb("rsum0", [64, 2, 2, 128])
        hmask = sb("hmask", [128, H])
        v1 = late.take([128, 2, H, D1 + 1])
        negmax = sb("negmax", [128, 128], BF16)
        negmaxT = sb("negmaxT", [128, 2, 128], BF16)
        pT = sb("pT", [128, 2, CH, 128])
        rsum = sb("rsum", [128, 2, H])
        o = wide.take([128, 2, ID])
        oT = wide.take([128, 2, 8, 128])

        attn1_slots = late.at
        wq0 = early.take([D, D])
        wk0 = early.take([C, D])
        bq0 = sb("bq0", [128, 1])
        bk0 = sb("bk0", [128, 1])
        wv0 = early.take([C, D])
        bv0 = early.take([128, D])
        wo0 = early.take([64 + 1, 2, D])

        gate_in = sb("gate_in", [E0, D])
        gateT = early.take([D, E0])
        we = early.take([D, E0, D])
        lower = sb("lower", [128, E0, E0])
        ys = early.take([128, 2, E0, D])
        ysum = sb("ysum", [128, 2, D])

        attn0_end, early.at = early.at, 0
        xn0 = early.take([128, B, D])
        xT0 = early.take([128, B, 128])
        lg = early.take([128, B, E0])
        beat = early.take([128, B, E0, E0])
        tie = early.take([128, B, E0, E0])
        nbeat = early.take([128, B, E0])
        top0 = early.take([128, B])
        ew = early.take([128, B, E0])
        wsum = early.take([128, B])
        ffn_w = early.take([128, B, E0])
        downT = early.take([RANK, 1 + 8, 128])
        ctx_ipaT = early.take([C, B * IPA])
        assert early.at <= attn0_slots
        early.at = attn0_end

        wq1 = late.take([D, ID])
        wk1 = late.take([C + RANK, ID])
        mT = late.take([128, H, D])
        wv1 = late.take([C + RANK, ID])
        wo1 = late.take([128, 8, D])
        alpha = sb("alpha", [128, 4])
        ipa_k = late.take([D, B, H * IPA])
        ipa_v = sb("ipa_v", [H * IPA + 1, B, D])
        ipa_s = sb("ipa_s", [128, 2, H, IPA])
        ipa_max = sb("ipa_max", [128, 2, H])
        ipa_sum = sb("ipa_sum", [128, 2, H])
        ipa_pT = sb("ipa_pT", [H * IPA + 1, 2, 128])
        late_end, late.at = late.at, 0
        down = late.take([128, 3, RANK])
        down_o = late.take([128, 8, RANK])
        up_q = late.take([RANK, ID])
        ext = late.take([C + RANK, 2, C])
        up_o = late.take([RANK, D])
        ctx_ipa = late.take([B * IPA, C])
        assert late.at <= attn1_slots
        late.at = late_end
        wki, wvi = o[0:C, 0, :], o[0:C, 1, :]
        wq1T, ipa_v_rows = oT[:, 0, :, :], oT[:, 1, :, :]
        wk1T = kT[:, 1, 0:8, 0:C]
        ipa_kT, ipa_vT = (kT[:, 0, 8 * n:8 * n + 8, :].rearrange("p c (b t j) -> p c b t j", b=B, t=2) for n in (0, 1))
        early.again()
        rw1 = early.take([D, D])
        rw2 = early.take([D, E1])
        rw2_wide = early.take([D, 8 * (D + E1)])
        ew1 = early.take([D, 4, F1])
        ew2 = early.take([D, 4, F1])
        ew3 = early.take([128, 4, F1 // 128, D])
        count_i = early.take([128, 128], I32)
        count = early.take([128, 128])
        eo_all = early.take([128, B, EG, D])
        xn_all = early.take([128, B, D])
        late.again()
        xgT = late.take([D, B, E1, CAP])
        hs = late.take([128, 2, 2, 512])
        late_mark = late.at
        oh_bf = late.take([128, 2, EG, 128], BF16)
        late.at = late_mark
        sg = late.take([128, 2, 512])
        xT4, hT4 = (kT[:, n, :, :].rearrange("p (n k) t -> p n k t", n=4) for n in range(2))
        oh = kT
        wide.again()
        ohw = wide.take([128, B, EG, 128])
        probs = sb("probs", [128, 2, 128])
        ex_max = sb("ex_max", [128, 2, 1])
        ex_sum = sb("ex_sum", [128, 2, 1])
        top = sb("top", [128, 2, CAP])
        top_at = sb("top_at", [128, 2, CAP], mybir.dt.uint32)
        top_at_f = sb("top_at_f", [128, 2, CAP])
        slot_at = sb("slot_at", [128, B, EG])
        slot_w = sb("slot_w", [128, B, EG])
        ipa_v_dram = nc.dram_tensor("ipa_v_scratch", (B, 2 * IPA, 8, D), F32, kind="Internal").ap()

        block = ctx.enter_context(nc.Block())

        made = named(sem, "made", "ext consts ident pick hmask vm0 vm1 ones pad")
        got = named(sem, "got", "x0 x ctx0 ctx attn0 ffn0 attn1 ipa route stored")
        ln = named(sem, "ln", "stats mv veps rstd")
        phase_end = sem("phase_end")
        A = named(sem, "a", "ctx_in xn tr xc_T qk qm km km_pool v q_sb k_sb v_sb q_bf k_bf smax maxed negT negT_sb "
                            "score exp pv rsum o oTr oT_sb proj x_new stats")

        F = named(sem, "f", "gate_tr gateT lower xn tr xT logit step ex slot y ys0 ys1 ysum x_new stats")

        W = named(sem, "w", "turned downT alpha zeros made taken out back")
        Z = named(sem, "z", "ctx_in xn tr xc_T x_bf k0 k1 k2 k3 v0 v1 k0_sb k1_sb k2_sb k3_sb v0_sb v1_sb k_bf "
                            "smax maxed negT negT_sb score exp pv rsum o oTr0 oTr1 oT_sb proj x_new stats "
                            "ipa_score ipa_step ipa_sub ipa_exp ipa_p ipa_turn ipa_pT")

        R = named(sem, "r", "wide count xn tr xT hid h logit step ex turned slot")
        G = named(sem, "g", "xn row turned oh got xg")
        X1 = named(sem, "x", "w0 w1 w2 w3 gv silu h eo eo_act eo_dve")
        w_in = (X1.w0, X1.w1, X1.w2, X1.w3)
        Y = named(sem, "y", "sum x_new stored")

        turn_bank = [bank[n] for n in (0, 3, 4, 7)]

        def down_rows(n):
            return slice(0, RANK) if n == 0 else slice(C, C + RANK)

        FOLDS = 19

        def fold_bank(s):
            return OB[s] if s < 2 else bank[(6, 7, 0, 5)[(s - 2) % 4]]

        def engines_meet(eng, n):
            eng.drain().then_inc(phase_end, 1)
            eng.wait_ge(phase_end, 5 * n)

        def act_exp(act, Z, keys, width, b, j):
            act.wait_ge(Z.score, b * NCH + j + 1)
            after(act, Z.pv, b * NCH + j - 1)
            act.activation(pT[0:keys, j % 2, :, :], blocks(SCB[j % 2], keys), ACT.Exp,
                           scale=float(width) ** -0.5).then_inc(Z.exp, 1)

        def dve_max(dve, Z, f, j, column, keys):
            dve.wait_ge(Z.smax, f * NCH + j + 1)
            after(dve, Z.negT, f)
            dve.tensor_reduce(negmax[:, column:column + CH], blocks(MAXB)[:, :, 0:keys], X, ALU.max,
                              negate=True).then_inc(Z.maxed, 1)

        def dve_negmaxT(dve, Z, f, uf, to):
            dve.wait_ge(Z.negT, f + 1)
            dve.tensor_copy(negmaxT[0:H, uf, :], to[0:H, 0:128]).then_inc(Z.negT_sb, 1)

        def dve_xn(dve, Z, b, u):
            dve.tensor_scalar(xn[:, u, :], x_all[:, b, :], mv[:, b, 0:1], rstd[:, b, :],
                              ALU.subtract, ALU.mult).then_inc(Z.xn, 1)

        def dve_residual(dve, Z, t, add):
            dve.tensor_tensor(x_all[:, t, :], add, x_all[:, t, :], ALU.add).then_inc(Z.x_new, 1)
            dve.wait_ge(Z.x_new, t + 1)

        def dve_stats(dve, Z, t):
            dve.bn_stats(stats[:, t, :], x_all[:, t, :]).then_inc(Z.stats, 1)

        def pe_transpose_in(pe, Z, to, f, uf, freed):
            pe.wait_ge(Z.xn, f + 1)
            pe.wait_ge(Z.ctx_in, f + 1)
            after(pe, Z.v_sb, freed)
            pe.transpose(to[:, 0:128], xn[:, uf, :], ident[:, :])
            pe.transpose(to[:, 128:256], ctx_in[:, uf, :], ident[:, :]).then_inc(Z.tr, 1)

        def act_transposed_in(act, Z, of, f, uf):
            act.wait_ge(Z.tr, f + 1)
            act.activation(xT[:, uf, :], of[:, 0:128], ACT.Copy).then_inc(Z.xc_T, 1)
            act.activation(cT[:, uf, :], of[:, 128:256], ACT.Copy).then_inc(Z.xc_T, 1)

        def empty_values(eng, u, made_vm):
            eng.memset(vm[:, u, :, :, :], 0.0).then_inc(made_vm, 1)
            eng.wait_ge(made_vm, 1)
            eng.memset(vm[:, u, :, :, 64:64 + D0], 1.0).then_inc(made_vm, 1)

        def pool_ctx(pool, Z, b, u):
            after(pool, Z.tr, b - 1)
            pool.tensor_copy(ctx_in[:, u, 0:C], ctx_all[:, b, :]).then_inc(Z.ctx_in, 1)



        def experts(eng, first, body):
            first(0, 0, 0)
            with eng.Fori(0, EG - 1) as i:
                for q in range(4):
                    body(i * 4 + q, i, q)
            for q in range(4):
                body(E1 - 4 + q, EG - 1, q)

        def rw2_of(b):
            return rw2_wide[:, 128 * (b % 8):128 * (b % 8) + 128]

        def eo_got(q, half, n):
            return bank[4 + 2 * (q % 2) + half][32 * n:32 * n + 32, 0:2 * D].rearrange("p (k d) -> p k d", k=2)

        def eo_rows(g, q, half, n):
            return eo_all[32 * q:32 * q + 32, :, :, :].rearrange("p (h k n) g d -> p h n g k d", h=2, k=2)[:, half, n, g, :, :]

        @block.sync
        def _(sp):
            def load(first, end, x_done, ctx_done):
                sp.dma_start(x_all[:, first:end, :], T["x"][first:end, :, :].rearrange("b s d -> s b d")).then_inc(x_done, 16)
                sp.dma_start(ctx_all[:, first:end, :], T["ctx_768"][first:end, :, :].rearrange("b s c -> s b c"))\
                    .then_inc(ctx_done, 16)
            load(0, 2, got.x0, got.ctx0)
            sp.dma_start(wq0[:, :], T["L0_xattn_wq"]).then_inc(got.attn0, 16)
            sp.dma_start(wk0[:, :], T["L0_xattn_wk"]).then_inc(got.attn0, 16)
            for bias, name in ((bq0, "L0_xattn_bq"), (bk0, "L0_xattn_bk")):
                sp.dma_start(bias[:, :], T[name].rearrange("(p a) -> p a", a=1)).then_inc(got.attn0, 16)
            sp.dma_start(wv0[:, :], T["L0_xattn_wv"]).then_inc(got.attn0, 16)
            sp.dma_start(bv0[:, :], T["L0_xattn_bv"].rearrange("(a n) -> a n", a=1).broadcast_to((128, D))).then_inc(got.attn0, 16)
            sp.dma_start(wo0[0:64, :, :], T["L0_xattn_wo"].rearrange("(a p) n -> p a n", a=2)).then_inc(got.attn0, 16)
            sp.dma_start(wo0[64:65, 1, :], T["L0_xattn_bo"].rearrange("(a n) -> a n", a=1)).then_inc(got.attn0, 16)
            load(2, B, got.x, got.ctx)
            sp.dma_start(gate_in[:, :], T["L0_ffn_gate_w"]).then_inc(got.ffn0, 16)
            sp.dma_start(we[:, :, :], T["L0_ffn_We"].rearrange("e d m -> d e m")).then_inc(got.ffn0, 16)
            for w, rows, name in ((wq1, D, "Wq"), (wk1, C, "Wk"), (wv1, C, "Wv")):
                sp.dma_start(w[0:rows, :], T["L1_xattn_" + name]).then_inc(got.attn1, 16)
            sp.dma_start(wo1[:, :, :], T["L1_xattn_Wo"].rearrange("(c p) n -> p c n", p=128)).then_inc(got.attn1, 16)
            sp.dma_start(ipa_v[H * IPA:H * IPA + 1, :, :], T["L1_xattn_bo"].rearrange("(a b n) -> a b n", a=1, b=1)
                         .broadcast_to((1, B, D))).then_inc(got.attn1, 16)
            for n, name in enumerate("qkvo"):
                sp.dma_start(alpha[:, n:n + 1], T[f"L1_xattn_{name}_alpha"].rearrange("(a n) -> a n", a=1)
                             .broadcast_to((128, 1))).then_inc(got.attn1, 16)
            for n, (name, rows) in enumerate((("q", D), ("k", C), ("v", C))):
                sp.dma_start(down[0:rows, n, :], T[f"L1_xattn_{name}_down"]).then_inc(got.attn1, 16)
                sp.dma_start((up_q[:, :], wk1[C:C + RANK, :], wv1[C:C + RANK, :])[n], T[f"L1_xattn_{name}_up"])\
                    .then_inc(got.attn1, 16)
            sp.dma_start(down_o[:, :, :], T["L1_xattn_o_down"].rearrange("(c p) r -> p c r", p=128)).then_inc(got.attn1, 16)
            sp.dma_start(up_o[:, :], T["L1_xattn_o_up"]).then_inc(got.attn1, 16)
            sp.dma_start(ctx_ipa[:, :], T["ctx_768"][:, ORG:S, :].rearrange("b j c -> b j c")).then_inc(got.attn1, 16)
            sp.dma_start(wki[:, :], T["L1_xattn_Wk_ipa"]).then_inc(got.attn1, 16)
            sp.dma_start(wvi[:, :], T["L1_xattn_Wv_ipa"]).then_inc(got.attn1, 16)
            engines_meet(sp, 1)
            sp.wait_ge(W.taken, FOLDS)
            sp.dma_start(ipa_v_dram.rearrange("b r c n -> (b r) c n"), ipa_v_rows[:, :, :]).then_inc(W.out, 16)
            sp.wait_ge(W.out, 16)
            for c in range(8):
                sp.dma_start(ipa_v[8 * c:8 * c + 8, :, :], ipa_v_dram[:, :, c, :].rearrange("b r n -> r b n"))\
                    .then_inc(W.back, 16)
            engines_meet(sp, 2)
            sp.dma_start(rw1[:, :], T["L1_ffn_router_w1"]).then_inc(got.route, 16)
            sp.dma_start(rw2[:, :], T["L1_ffn_router_w2"]).then_inc(got.route, 16)

            def expert_weights(e, q):
                for slot, w in ((ew1, "L1_ffn_w1"), (ew2, "L1_ffn_w2")):
                    sp.dma_start(slot[:, q, :], T[w][e, :, :]).then_inc(w_in[q], 16)
                sp.dma_start(ew3[:, q, :, :], T["L1_ffn_w3"].rearrange("e (c p) n -> e p c n", p=128)[e, :, :, :])\
                    .then_inc(w_in[q], 16)
            for q in range(4):
                expert_weights(q, q)
            engines_meet(sp, 3)
            engines_meet(sp, 4)
            with sp.Fori(0, EG - 1) as i:
                for q in range(4):
                    sp.wait_ge(X1.eo, i * 4 + q + 1)
                    expert_weights(i * 4 + (q + 4), q)
            engines_meet(sp, 5)
            with sp.Fori(0, B) as b:
                sp.wait_ge(Y.x_new, b + 1)
                sp.dma_start(out[b, :, :], x_all[:, b, :]).then_inc(Y.stored, 16)
            sp.wait_ge(Y.stored, 16 * B)

        @block.gpsimd
        def _(pool):
            pool.memset(minus_half[:, :], -0.5).then_inc(made.consts, 1)
            pool.memset(ident[:, :], 0.0).then_inc(made.ident, 1)
            pool.memset(ident_bf[:, :], 0.0).then_inc(made.ident, 1)
            pool.wait_ge(made.ident, 2)
            for m in (ident, ident_bf):
                pool.affine_select(out=m[:, :], in_=m[:, :], compare_op=ALU.not_equal, fill=1.0, base=0,
                                   pattern=[[-1, 128]], channel_multiplier=1).then_inc(made.ident, 1)
            pool.memset(hmask[:, :], 1.0).then_inc(made.hmask, 1)
            for base, way in ((0, 1), (D0 - 1, -1)):
                pool.wait_ge(made.hmask, 1 if way == 1 else 2)
                pool.affine_select(out=hmask[:, :], in_=hmask[:, :], compare_op=ALU.is_ge, fill=0.0, base=base,
                                   pattern=[[-D0 * way, H]], channel_multiplier=way).then_inc(made.hmask, 1)
            pool.memset(negmax[:, :], 0.0).then_inc(made.consts, 1)
            pool.tensor_copy(ext[:, :, :], ident[:, 0:C].unsqueeze(1).broadcast_to((128, 2, C))).then_inc(made.ext, 1)

            def rstds(n, first, end):
                pool.wait_ge(ln.veps, 2 * n - 1 if first == 0 else 2 * n)
                pool.tensor_tensor(rstd[:, first:end, 0], veps[:, first:end], minus_half[:, first:end], ALU.pow)\
                    .then_inc(ln.rstd, 1)
            pool.memset(ctx_in[:, :, C:128], 0.0).then_inc(made.pad, 1)
            pool.wait_ge(got.ctx0, 16)
            pool_ctx(pool, A, 0, 0)
            pool_ctx(pool, A, 1, 1)
            rstds(1, 0, 2)
            pool.memset(pick[:, :, :], 0.0).then_inc(made.pick, 1)
            pool.wait_ge(made.pick, 1)
            pool.affine_select(out=pick[:, :, :], in_=pick[:, :, :], compare_op=ALU.not_equal, fill=1.0,
                               base=0, pattern=[[-1, H], [0, 128]], channel_multiplier=1).then_inc(made.pick, 1)

            def body(b, u):
                f, uf = b + 1, 1 - u
                if isinstance(b, int) and b == 0:
                    empty_values(pool, 1, made.vm1)
                    rstds(1, 2, B)
                    pool.wait_ge(got.ctx, 16)
                if there(f):
                    pool.wait_ge(A.k_sb, f + 1)
                    after(pool, A.smax, (f - 1) * NCH)
                    half = (128, H // 2, 128)
                    pool.tensor_tensor(km_bf[:, uf, H // 2:H, :], kT[:, uf, 0, :].unsqueeze(1).broadcast_to(half),
                                       hmask[:, H // 2:H].unsqueeze(2).broadcast_to(half), ALU.mult)\
                        .then_inc(A.km_pool, 1)
                if there(b + 2) and not (isinstance(b, int) and b == -1):
                    pool_ctx(pool, A, b + 2, u)
            pipelined(pool, body)
            rstds(2, 0, B - 2)
            rstds(2, B - 2, B)
            engines_meet(pool, 1)
            pool.memset(ipa_kT, 0.0).then_inc(W.zeros, 1)
            pool.memset(ipa_vT, 0.0).then_inc(W.zeros, 1)
            pool.memset(lower[:, :, :], 1.0).then_inc(F.lower, 1)
            pool.wait_ge(F.lower, 1)
            pool.affine_select(out=lower[:, :, :], in_=lower[:, :, :], compare_op=ALU.is_ge, fill=0.0, base=-1,
                               pattern=[[1, E0], [-1, E0]], channel_multiplier=0).then_inc(F.lower, 1)
            pool.wait_ge(F.lower, 2)
            pool.memset(mT[C:128, :, :], 0.0).then_inc(made.pad, 1)
            pool.wait_ge(made.pad, 2)
            pool.wait_ge(W.made, 19)
            pool.memset(v1[:, :, :, D1:D1 + 1], 1.0)
            rstds(3, 0, B - 2)
            rstds(3, B - 2, B)
            engines_meet(pool, 2)

            def body(b, u):
                f, uf = b + 1, 1 - u
                if isinstance(b, int) and b == -1:
                    pool_ctx(pool, Z, 0, 0)
                    pool_ctx(pool, Z, 1, 1)
                if there(b + 2) and not (isinstance(b, int) and b == -1):
                    pool_ctx(pool, Z, b + 2, u)
            pipelined(pool, body)
            pool.memset(rw2_wide[:, :], 0.0).then_inc(R.wide, 1)
            pool.iota(count_i[:, :], [[1, 128]], base=0, channel_multiplier=0).then_inc(R.count, 1)
            pool.wait_ge(R.count, 1)
            pool.tensor_copy(count[:, :], count_i[:, :]).then_inc(R.count, 1)
            pool.wait_ge(got.route, 32)
            pool.wait_ge(R.wide, 1)
            pool.tensor_copy(rw2_wide[:, :].rearrange("p (b n) -> p b n", b=8)[:, :, 0:E1],
                             rw2[:, :].unsqueeze(1).broadcast_to((D, 8, E1))).then_inc(R.wide, 1)
            rstds(4, 0, B - 2)
            rstds(4, B - 2, B)
            engines_meet(pool, 3)

            def body(b, u):
                pool.wait_ge(R.tr, 4)
                after(pool, G.got, b - 1)
                pool.tensor_copy(xn[:, u, :], xn_all[:, b, :]).then_inc(G.xn, 1)
            body(0, 0)
            body(1, 1)
            with pool.Fori(0, B // 2 - 1) as i:
                body(i * 2 + 2, 0)
                body(i * 2 + 3, 1)
            engines_meet(pool, 4)
            engines_meet(pool, 5)

        @block.vector
        def _(dve):
            for ones in (o0T[64:65, :, :, :], ipa_pT[H * IPA:H * IPA + 1, :, :]):
                dve.memset(ones, 1.0).then_inc(made.ones, 1)

            def variances(stats_done, n, first, end):
                dve.wait_ge(stats_done, end)
                for b in range(first, end):
                    dve.bn_aggr(mv[:, b, :], stats[:, b, :]).then_inc(ln.mv, 1)
                dve.wait_ge(ln.mv, (n - 1) * B + end)
                dve.tensor_scalar(veps[:, first:end], mv[:, first:end, 1], EPS, None, ALU.add).then_inc(ln.veps, 1)

            def first_statistics(first, end, loaded):
                dve.wait_ge(loaded, 16)
                for b in range(first, end):
                    dve_stats(dve, ln, b)
                variances(ln.stats, 1, first, end)
            first_statistics(0, 2, got.x0)
            dve.wait_ge(ln.rstd, 1)
            dve_xn(dve, A, 0, 0)
            empty_values(dve, 0, made.vm0)
            dve.wait_ge(got.attn0, 16 * 8)
            dve.wait_ge(made.consts, 2)
            dve.wait_ge(made.hmask, 3)

            def normalize(to, first, end, rstds_done, done):
                dve.wait_ge(ln.rstd, rstds_done)
                for b in range(first, end):
                    dve.tensor_scalar(to[:, b, :], x_all[:, b, :], mv[:, b, 0:1], rstd[:, b, :],
                                      ALU.subtract, ALU.mult).then_inc(done, 1)

            def norm(t, ut):
                dve.wait_ge(A.pv, t * NCH + NCH)
                dve.reciprocal(rsum0[:, ut, :, :], OB[ut][64:128, 0:256].rearrange("p (a n) -> p a n", a=2))\
                    .then_inc(A.rsum, 1)
                dve.wait_ge(A.rsum, t + 1)
                dve.tensor_tensor(o0T[0:64, ut, :, :], OB[ut][0:64, 0:256].rearrange("p (a n) -> p a n", a=2),
                                  rsum0[:, ut, :, :], ALU.mult).then_inc(A.o, 1)

            def body(b, u):
                f, t, uo = b + 1, b - 1, 1 - u
                if isinstance(b, int) and b == 0:
                    first_statistics(2, B, got.x)
                if there(t):
                    norm(t, uo)
                if isinstance(b, int) and b == B:
                    normalize(xn0, 0, B - 2, 3, F.xn)
                if there(f):
                    dve.wait_ge(A.q_sb, f + 1)
                    dve.tensor_tensor(qm[:, uo, :, :], qT[:, uo, :].unsqueeze(1).broadcast_to((128, H, 128)),
                                      hmask[:, :].unsqueeze(2).broadcast_to((128, H, 128)), ALU.mult)\
                        .then_inc(A.qm, 1)
                    if isinstance(f, int) and f < 2:
                        dve.wait_ge((made.vm0, made.vm1)[f], 2)
                    dve.wait_ge(A.v, f + 1)
                    dve.tensor_tensor(vm[:, uo, :, :, 0:D0],
                                      PB[1][:, 0:D].rearrange("p (a h d) -> p a h d", a=2, h=8),
                                      bv0[:, :].rearrange("p (a h d) -> p a h d", a=2, h=8), ALU.add)\
                        .then_inc(A.v_sb, 1)
                if isinstance(b, int) and b == 0:
                    dve.wait_ge(ln.rstd, 2)
                if there(b + 2):
                    dve_xn(dve, A, b + 2, u)
                if there(t):
                    dve.wait_ge(A.proj, t + 1)
                    dve_residual(dve, A, t, TB[:, 0:D])
                if there(f):
                    dve_max(dve, A, f, 0, 0, S)
                if there(t):
                    dve_stats(dve, A, t)
                if there(f):
                    for j in range(1, NCH):
                        dve_max(dve, A, f, j, CH * j, S)
                    dve_negmaxT(dve, A, f, uo, TB)
            pipelined(dve, body, lambda: variances(A.stats, 2, 0, B - 2))
            variances(A.stats, 2, B - 2, B)
            engines_meet(dve, 1)
            dve.wait_ge(F.gate_tr, 1)
            dve.tensor_copy(gateT[:, :], TB[:, 0:E0]).then_inc(F.gateT, 1)
            dve.wait_ge(F.lower, 2)
            normalize(xn0, B - 2, B, 4, F.xn)
            steps = 0

            def step(ins):
                nonlocal steps
                steps += 1
                ins.then_inc(F.step, 1)
                dve.wait_ge(F.step, steps)
            each, pairs = (128, B, E0), (128, B, E0, E0)
            dve.wait_ge(F.logit, 4)
            step(dve.tensor_copy(lg[:, :, :], PB[0][:, 0:B * E0].rearrange("p (b e) -> p b e", b=B)))
            step(dve.tensor_reduce(top0[:, :], lg[:, :, :], X, ALU.max))
            step(dve.tensor_tensor(ew[:, :, :], lg[:, :, :], top0[:, :].unsqueeze(2).broadcast_to(each), ALU.subtract))
            mine = lg[:, :, :].unsqueeze(3).broadcast_to(pairs)
            other = lg[:, :, :].unsqueeze(2).broadcast_to(pairs)
            step(dve.tensor_tensor(tie[:, :, :, :], other, mine, ALU.is_ge))
            step(dve.tensor_tensor(tie[:, :, :, :], tie[:, :, :, :], lower[:, :, :].unsqueeze(1).broadcast_to(pairs),
                                   ALU.mult))
            step(dve.tensor_tensor(beat[:, :, :, :], other, mine, ALU.is_gt))
            step(dve.tensor_tensor(beat[:, :, :, :], beat[:, :, :, :], tie[:, :, :, :], ALU.max))
            step(dve.tensor_reduce(nbeat[:, :, :], beat[:, :, :, :], X, ALU.add))
            dve.wait_ge(F.ex, 1)
            step(dve.scalar_tensor_tensor(ew[:, :, :], nbeat[:, :, :], 1.5, ew[:, :, :], ALU.is_lt, ALU.mult))
            step(dve.tensor_reduce(wsum[:, :], ew[:, :, :], X, ALU.add))
            step(dve.reciprocal(wsum[:, :], wsum[:, :]))
            step(dve.tensor_tensor(ffn_w[:, :, :], ew[:, :, :], wsum[:, :].unsqueeze(2).broadcast_to(each), ALU.mult))

            def body(b, u):
                t, half = b - 1, E0 // 2
                if there(b):
                    dve.wait_ge(F.y, b + 1)
                    dve.tensor_tensor(ys[:, u, half:E0, :], blocks((SCB, OB)[u][1]),
                                      ffn_w[:, b, half:E0].unsqueeze(2).broadcast_to((128, half, D)), ALU.mult)\
                        .then_inc(F.ys1, 1)
                if there(t):
                    dve.wait_ge(F.ysum, t + 1)
                    dve_residual(dve, F, t, ysum[:, 1 - u, :])
                if there(b):
                    dve.wait_ge(F.ys1, b + 1)
                    dve.wait_ge(F.ys0, 4 * b + 4)
                    dve.tensor_reduce(ysum[:, u, :], ys[:, u, :, :].rearrange("p e d -> p d e"), X, ALU.add)\
                        .then_inc(F.ysum, 1)
                if there(t):
                    dve_stats(dve, F, t)
            body(0, 0)
            body(1, 1)
            with dve.Fori(0, B // 2 - 2) as i:
                body(i * 2 + 2, 0)
                body(i * 2 + 3, 1)
            body(B - 2, 0)
            variances(F.stats, 3, 0, B - 2)
            body(B - 1, 1)
            body(B, 0)
            variances(F.stats, 3, B - 2, B)
            engines_meet(dve, 2)

            dve.wait_ge(ln.rstd, 6)
            dve_xn(dve, Z, 0, 0)

            def norm(b, u, j):
                dve.wait_ge(Z.pv, b * NCH + j + 1)
                got_o = OB[j % 2][:, 0:CH * (D1 + 1)].rearrange("p (h d) -> p h d", h=CH)
                sums = rsum[:, u, CH * j:CH * j + CH]
                dve.reciprocal(sums, got_o[:, :, D1]).then_inc(Z.rsum, 1)
                dve.wait_ge(Z.rsum, b * NCH + j + 1)
                dve.tensor_tensor(o[:, u, CH * D1 * j:CH * D1 * (j + 1)].rearrange("p (h d) -> p h d", h=CH),
                                  got_o[:, :, 0:D1], sums.unsqueeze(2).broadcast_to((128, CH, D1)), ALU.mult)\
                    .then_inc(Z.o, 1)

            def ipa_scores(f, uf):
                dve.wait_ge(Z.ipa_score, f + 1)
                sc = TB[:, 0:H * IPA].rearrange("p (h j) -> p h j", h=H)
                dve.tensor_reduce(ipa_max[:, uf, :], sc, X, ALU.max).then_inc(Z.ipa_step, 1)
                dve.wait_ge(Z.ipa_step, f * 3 + 1)
                dve.tensor_tensor(ipa_s[:, uf, :, :], sc, ipa_max[:, uf, :].unsqueeze(2).broadcast_to((128, H, IPA)),
                                  ALU.subtract).then_inc(Z.ipa_sub, 1)

            def ipa_norm(f, uf):
                dve.wait_ge(Z.ipa_exp, f + 1)
                dve.tensor_reduce(ipa_sum[:, uf, :], ipa_s[:, uf, :, :], X, ALU.add).then_inc(Z.ipa_step, 1)
                dve.wait_ge(Z.ipa_step, f * 3 + 2)
                dve.reciprocal(ipa_sum[:, uf, :], ipa_sum[:, uf, :]).then_inc(Z.ipa_step, 1)
                dve.wait_ge(Z.ipa_step, f * 3 + 3)
                dve.tensor_tensor(ipa_s[:, uf, :, :], ipa_s[:, uf, :, :],
                                  ipa_sum[:, uf, :].unsqueeze(2).broadcast_to((128, H, IPA)), ALU.mult)\
                    .then_inc(Z.ipa_p, 1)

            def body(b, u):
                f, t, uo = b + 1, b - 1, 1 - u
                if there(t):
                    norm(t, uo, 3)
                if isinstance(b, int) and b == B:
                    normalize(xn_all, 0, B - 2, 7, R.xn)
                if there(f):
                    ipa_scores(f, uo)
                    dve.wait_ge(Z.k0, f + 1)
                    dve.tensor_copy(kT[:, uo, 0:4, 0:ORG], blocks(PB[0])[:, :, 0:ORG]).then_inc(Z.k0_sb, 1)
                if there(b):
                    norm(b, u, 0)
                if there(f):
                    dve.wait_ge(Z.k2, f + 1)
                    dve.tensor_copy(kT[:, uo, 8:12, 0:ORG], blocks(PB[0])[:, :, 0:ORG]).then_inc(Z.k2_sb, 1)
                    ipa_norm(f, uo)
                if there(t):
                    dve.wait_ge(Z.proj, t + 1)
                    dve_residual(dve, Z, t, TB[:, 0:D])
                if there(f):
                    dve_max(dve, Z, f, 0, 0, ORG)
                if there(t):
                    dve_stats(dve, Z, t)
                if there(f):
                    dve.wait_ge(Z.v0, f + 1)
                    dve.tensor_copy(v1[0:ORG, uo, 0:8, 0:D1], PB[0][0:ORG, :].rearrange("p (h d) -> p h d", h=8))\
                        .then_inc(Z.v0_sb, 1)
                if there(b):
                    norm(b, u, 1)
                if there(f):
                    dve_max(dve, Z, f, 1, CH, ORG)
                if there(b + 2):
                    dve_xn(dve, Z, b + 2, u)
                if there(f):
                    dve_max(dve, Z, f, 2, 2 * CH, ORG)
                    dve.wait_ge(Z.ipa_turn, f + 1)
                    dve.tensor_copy(ipa_pT[0:H * IPA, uo, :], TB[0:H * IPA, 0:128]).then_inc(Z.ipa_pT, 1)
                    dve_max(dve, Z, f, 3, 3 * CH, ORG)
                if there(f):
                    dve_negmaxT(dve, Z, f, uo, MAXB)
                if there(b):
                    norm(b, u, 2)
            pipelined(dve, body, lambda: variances(Z.stats, 4, 0, B - 2))
            variances(Z.stats, 4, B - 2, B)
            engines_meet(dve, 3)

            normalize(xn_all, B - 2, B, 8, R.xn)
            steps = 0

            def ready():
                nonlocal steps
                after(dve, R.step, steps - 1)
                steps += 1
            for t in range(2):
                dve.wait_ge(R.logit, t + 1)
                ready()
                dve.tensor_reduce(ex_max[:, t, :], bank[4 + t][:, 0:128], X, ALU.max, negate=True).then_inc(R.step, 1)
            for t in range(2):
                dve.wait_ge(R.ex, t + 1)
                ready()
                dve.tensor_reduce(ex_sum[:, t, :], probs[:, t, :], X, ALU.add).then_inc(R.step, 1)
            for t in range(2):
                ready()
                dve.reciprocal(ex_sum[:, t, :], ex_sum[:, t, :]).then_inc(R.step, 1)
            for t in range(2):
                ready()
                dve.tensor_scalar(probs[:, t, :], probs[:, t, :], ex_sum[:, t, :], None, ALU.mult).then_inc(R.step, 1)
            for n in range(CAP // 8):
                eight = slice(8 * n, 8 * n + 8)
                for t in range(2):
                    ready()
                    dve.max(top[:, t, eight], probs[:, t, :]).then_inc(R.step, 1)
                for t in range(2):
                    ready()
                    dve.max_index(top_at[:, t, eight], top[:, t, eight], probs[:, t, :]).then_inc(R.step, 1)
                for t in range(2):
                    if n < CAP // 8 - 1:
                        ready()
                        dve.match_replace(probs[:, t, :], top[:, t, eight], probs[:, t, :], -1.0).then_inc(R.step, 1)
            for t in range(2):
                ready()
                dve.tensor_copy(top_at_f[:, t, :], top_at[:, t, :]).then_inc(R.step, 1)
            for t in range(2):
                ready()
                dve.tensor_reduce(ex_sum[:, t, :], top[:, t, :], X, ALU.add).then_inc(R.step, 1)
            for t in range(2):
                ready()
                dve.tensor_scalar(ex_sum[:, t, :], ex_sum[:, t, :], 1e-9, None, ALU.add).then_inc(R.step, 1)
            for t in range(2):
                ready()
                dve.reciprocal(ex_sum[:, t, :], ex_sum[:, t, :]).then_inc(R.step, 1)
            for t in range(2):
                ready()
                dve.tensor_scalar(top[:, t, :], top[:, t, :], ex_sum[:, t, :], None, ALU.mult).then_inc(R.step, 1)
            for t in range(2):
                dve.wait_ge(R.turned, t + 1)
                for n, to in enumerate((slot_at, slot_w)):
                    dve.tensor_copy(to[:, 8 * t:8 * t + 8, :],
                                    bank[6 + t][:, 32 * n:32 * n + 32].rearrange("p (b g) -> p b g", b=8))\
                        .then_inc(R.slot, 1)
            dve.wait_ge(R.slot, 4)
            dve.wait_ge(R.count, 2)

            def body(b, u):
                after(dve, G.turned, b - 1)
                for g in range(EG):
                    ins = dve.tensor_scalar(oh_bf[:, u, g, :], count[:, :], slot_at[:, b, g:g + 1], None, ALU.is_equal)
                ins.then_inc(G.row, 1)
            body(0, 0)
            body(1, 1)
            with dve.Fori(0, B // 2 - 1) as i:
                body(i * 2 + 2, 0)
                body(i * 2 + 3, 1)
            engines_meet(dve, 4)

            def gated(e, g, q):
                for c in range(2):
                    dve.wait_ge(X1.silu, 2 * e + c + 1)
                    dve.tensor_tensor(hs[:, q % 2, c, :], sg[:, c, :], bank[2 * c + 1][:, :], ALU.mult)\
                        .then_inc(X1.h, 1)

            def body(e, g, q):
                if there_expert(e + 1):
                    gated(e + 1, g, q + 1)
                for k in range(EG):
                    dve.tensor_scalar(ohw[:, e, k, :], count[:, :], slot_at[:, e, k:k + 1],
                                      slot_w[:, e, k:k + 1], ALU.is_equal, ALU.mult)
                dve.wait_ge(X1.eo, e + 1)
                for n in range(4):
                    ins = dve.tensor_copy(eo_rows(g, q, 1, n), eo_got(q, 1, n))
                ins.then_inc(X1.eo_dve, 1)
            dve.drain().then_inc(X1.eo_dve, 2)
            experts(dve, gated, body)
            engines_meet(dve, 5)

            with dve.Fori(0, B // 2) as i:
                for u in range(2):
                    b = i * 2 + u
                    dve.wait_ge(Y.sum, b + 1)
                    dve.tensor_tensor(x_all[:, b, :], bank[u][:, 0:D], x_all[:, b, :], ALU.add).then_inc(Y.x_new, 1)

        @block.scalar
        def _(act):
            act.preload_act_table(ACT.Exp)
            act.wait_ge(got.attn0, 16 * 8)
            act.wait_ge(made.hmask, 3)

            def body(b, u):
                f, uf = b + 1, 1 - u
                if there(f):
                    act_transposed_in(act, A, PB[1], f, uf)
                if there(b):
                    act_exp(act, A, S, D0, b, 0)
                if there(f):
                    act.wait_ge(A.qk, f + 1)
                    act.activation(qT[:, uf, :], PB[0][:, 0:128], ACT.Identity, bias=bq0[:, :])\
                        .then_inc(A.q_sb, 1)
                    act.activation(q_bf[:, uf, :], PB[0][:, 0:128], ACT.Identity, bias=bq0[:, :])\
                        .then_inc(A.q_bf, 1)
                    act.activation(kT[:, uf, 0, :], PB[0][:, 128:256], ACT.Identity, bias=bk0[:, :])\
                        .then_inc(A.k_sb, 1)
                    act.wait_ge(A.k_sb, f + 1)
                    for h in range(H // 2):
                        if h == 4 and there(b):
                            act_exp(act, A, S, D0, b, 1)
                        ins = act.activation(km_bf[:, uf, h, :], kT[:, uf, 0, :], ACT.Copy, scale=hmask[:, h:h + 1])
                        if h % CH == CH - 1:
                            ins.then_inc(A.km, 1)
                elif there(b):
                    act_exp(act, A, S, D0, b, 1)
                if there(b):
                    act_exp(act, A, S, D0, b, 2)
                    act_exp(act, A, S, D0, b, 3)
            pipelined(act, body)
            engines_meet(act, 1)

            for n in range(4):
                act.wait_ge(F.tr, n + 1)
                act.activation(xT0[:, 4 * n:4 * n + 4, :], blocks(turn_bank[n]), ACT.Copy).then_inc(F.xT, 1)
            act.wait_ge(F.step, 3)
            act.activation(ew[:, :, :], ew[:, :, :], ACT.Exp).then_inc(F.ex, 1)
            act.wait_ge(got.attn1, 16 * 20)
            act.activation(alpha[:, :], alpha[:, :], ACT.Copy, scale=1.0 / RANK).then_inc(W.alpha, 1)
            act.wait_ge(W.alpha, 1)
            act.wait_ge(W.turned, 3)
            act.wait_ge(made.ext, 1)
            for n, to in enumerate((downT[:, 0, :], ext[C:C + RANK, 0, :], ext[C:C + RANK, 1, :])):
                rows = down_rows(n)
                act.activation(to, blocks(PB[1])[rows, n, 0:(D, C, C)[n]], ACT.Copy, scale=alpha[rows, n:n + 1])\
                    .then_inc(W.downT, 1)
            for n in range(2):
                act.activation(downT[:, 1 + 4 * n:5 + 4 * n, :], blocks(SCB[n], RANK), ACT.Copy,
                               scale=alpha[0:RANK, 3:4]).then_inc(W.downT, 1)

            def take(s):
                act.wait_ge(W.made, s + 1)
                got_w = fold_bank(s)
                if s < 2:
                    to, got_w = wq1T[:, 4 * s:4 * s + 4, :], blocks(got_w)
                elif s < 4:
                    to = wk1T[:, 4 * (s - 2):4 * (s - 2) + 4, :]
                    got_w = got_w[:, 0:4 * C].rearrange("p (c k) -> p c k", c=4)
                elif s < 6:
                    to, got_w = wv1[0:C, 512 * (s - 4):512 * (s - 4) + 512], got_w[0:C, :]
                elif s < 8:
                    to, got_w = wo1[:, 4 * (s - 6):4 * (s - 6) + 4, :], blocks(got_w)
                elif s < 12:
                    n = s - 8
                    to = mT[0:C, :, :].rearrange("c (n g t) d -> c n t g d", n=2, t=2)[:, n // 2, n % 2, :, :]
                    got_w = blocks(got_w, C)
                elif s == 12:
                    to, got_w = ctx_ipaT[:, :], got_w[0:C, 0:B * IPA]
                elif s < 15:
                    if s == 13:
                        act.wait_ge(W.zeros, 2)
                    to, got_w = (ipa_kT, ipa_vT)[s - 13], got_w[:, :].rearrange("p (c b j) -> p c b j", c=8, b=B)
                    act.activation(to[0:64, :, :, 0, :], got_w[0:64, :, :, :], ACT.Copy)
                    to, got_w = to[64:128, :, :, 1, :], got_w[64:128, :, :, :]
                elif s < 17:
                    n = s - 15
                    to = ipa_k[:, :, 32 * n:32 * n + 32].rearrange("p b (c r) -> p c b r", c=4)
                    got_w = got_w[:, :].rearrange("p (c b r) -> p c b r", c=4, b=B)
                else:
                    to, got_w = ipa_v_rows[:, 4 * (s - 17):4 * (s - 17) + 4, :], blocks(got_w)
                act.activation(to, got_w, ACT.Copy).then_inc(W.taken, 1)
            take(0)
            take(1)
            take(2)
            take(3)
            take(4)
            act.wait_ge(F.step, 12)
            for b in range(B):
                act.wait_ge(F.y, b + 1)
                after(act, F.ysum, b - 1)
                for e in range(E0 // 2):
                    act.activation(ys[:, b % 2, e, :], blocks((SCB, OB)[b % 2][0])[:, e, :], ACT.Copy,
                                   scale=ffn_w[:, b, e:e + 1]).then_inc(F.ys0, 1)
                if 5 + b < FOLDS:
                    take(5 + b)
            engines_meet(act, 2)

            def body(b, u):
                f, t, uo = b + 1, b - 1, 1 - u
                if there(f):
                    act_transposed_in(act, Z, TB, f, uo)
                    act.wait_ge(Z.xc_T, 2 * f + 1)
                    act.activation(x_bf[:, uo, :], xT[:, uo, :], ACT.Copy).then_inc(Z.x_bf, 1)
                if there(b):
                    act_exp(act, Z, ORG, D1, b, 0)
                if there(t):
                    for half, done in enumerate((Z.oTr0, Z.oTr1)):
                        act.wait_ge(done, t + 1)
                        act.activation(oT[:, uo, 4 * half:4 * half + 4, :], blocks(PB[half]), ACT.Copy)\
                            .then_inc(Z.oT_sb, 1)
                if there(b):
                    act_exp(act, Z, ORG, D1, b, 1)
                if there(f):
                    act.wait_ge(Z.ipa_sub, f + 1)
                    act.activation(ipa_s[:, uo, :, :], ipa_s[:, uo, :, :], ACT.Exp, scale=D1 ** -0.5)\
                        .then_inc(Z.ipa_exp, 1)
                    for n, (done, copied, other) in enumerate(((Z.k1, Z.k1_sb, Z.k0_sb), (Z.k3, Z.k3_sb, Z.k2_sb))):
                        act.wait_ge(done, f + 1)
                        act.activation(kT[:, uo, 8 * n + 4:8 * n + 8, 0:ORG], blocks(PB[1])[:, :, 0:ORG], ACT.Copy)\
                            .then_inc(copied, 1)
                        act.wait_ge(other, f + 1)
                        act.wait_ge(copied, f + 1)
                        after(act, Z.smax, (f - 1) * NCH)
                        act.activation(k_bf[:, uo, 8 * n:8 * n + 8, 0:ORG], kT[:, uo, 8 * n:8 * n + 8, 0:ORG], ACT.Copy)\
                            .then_inc(Z.k_bf, 1)
                if there(b):
                    act_exp(act, Z, ORG, D1, b, 2)
                if there(f):
                    act.wait_ge(Z.v1, f + 1)
                    act.activation(v1[0:ORG, uo, 8:16, 0:D1], PB[1][0:ORG, :].rearrange("p (h d) -> p h d", h=8),
                                   ACT.Copy).then_inc(Z.v1_sb, 1)
                if there(b):
                    act_exp(act, Z, ORG, D1, b, 3)
            pipelined(act, body)
            act.preload_act_table(ACT.Silu)
            engines_meet(act, 3)
            for n in range(4):
                act.wait_ge(R.tr, n + 1)
                act.activation(xT4[:, n, :, :], blocks(bank[n]), ACT.Copy).then_inc(R.xT, 1)
            for n in range(4):
                act.wait_ge(R.hid, n + 1)
                act.activation(hT4[:, n, :, :], blocks(bank[n]), ACT.Silu).then_inc(R.h, 1)
            act.preload_act_table(ACT.Exp)
            for t in range(2):
                act.wait_ge(R.step, t + 1)
                act.activation(probs[:, t, :], bank[4 + t][:, 0:128], ACT.Exp, bias=ex_max[:, t, :]).then_inc(R.ex, 1)

            def body(b, u):
                t = b - 1
                if there(b):
                    act.wait_ge(G.turned, b + 1)
                    after(act, G.got, b - 1)
                    act.activation(oh[:, u, 0:4, 0:128], blocks(bank[u]), ACT.Copy).then_inc(G.oh, 1)
                if there(t):
                    act.wait_ge(G.got, t + 1)
                    act.activation(xgT[:, t, :, :], bank[2 + (1 - u)][:, :].rearrange("p (e s) -> p e s", e=E1), ACT.Copy)\
                        .then_inc(G.xg, 1)
            body(0, 0)
            body(1, 1)
            with act.Fori(0, B // 2 - 1) as i:
                body(i * 2 + 2, 0)
                body(i * 2 + 3, 1)
            body(B, 0)
            act.preload_act_table(ACT.Silu)
            engines_meet(act, 4)

            def silus(e, g, q):
                for c in range(2):
                    act.wait_ge(X1.gv, 2 * e + c + 1)
                    after(act, X1.h, 2 * e + c - 1)
                    act.activation(sg[:, c, :], bank[2 * c][:, :], ACT.Silu).then_inc(X1.silu, 1)

            def body(e, g, q):
                if there_expert(e + 1):
                    silus(e + 1, g, q + 1)
                act.wait_ge(X1.eo, e + 1)
                for n in range(4):
                    ins = act.activation(eo_rows(g, q, 0, n), eo_got(q, 0, n), ACT.Copy)
                ins.then_inc(X1.eo_act, 1)
            act.drain().then_inc(X1.eo_act, 2)
            experts(act, silus, body)
            engines_meet(act, 5)

        @block.tensor
        def _(pe):
            pe.wait_ge(made.ident, 4)
            pe.wait_ge(made.pad, 1)
            pe.wait_ge(made.ones, 2)
            pe.wait_ge(got.attn0, 16 * 8)

            def maxima(f, uf, j):
                if j < 2:
                    pe.wait_ge(A.km, 2 * f + j + 1)
                else:
                    pe.wait_ge(A.km_pool, f + 1)
                after(pe, A.maxed, f * NCH + j)
                pe.matmul(blocks(MAXB), q_bf[:, uf, :], km_bf[:, uf, CH * j:CH * j + CH, :],
                          start=True, stop=True).then_inc(A.smax, 1)

            def scores(b, u, j):
                if isinstance(b, int) and b == 0:
                    pe.wait_ge(made.pick, 2)
                if j == 0:
                    pe.wait_ge(A.negT_sb, b + 1)
                    pe.wait_ge(A.qm, b + 1)
                    pe.wait_ge(A.k_sb, b + 1)
                after(pe, A.exp, b * NCH + j - 1)
                for g in range(CH):
                    h = CH * j + g
                    to = blocks(SCB[j % 2])[:, g, :]
                    pe.matmul(to, pick[0:H, h, :], negmaxT[0:H, u, :], start=True, stop=False)
                    mm = pe.matmul(to, kT[:, u, 0, :], qm[:, u, h, :], start=False, stop=True)
                mm.then_inc(A.score, 1)

            def values(b, u, j):
                pe.wait_ge(A.exp, b * NCH + j + 1)
                if isinstance(b, int) and b == 0:
                    pe.wait_ge(made.vm0, 2)
                if j == 0:
                    pe.wait_ge(A.v_sb, b + 1)
                    after(pe, A.o, b - 1)
                half = j // 2
                for g in range(CH):
                    h = CH * (j % 2) + g
                    own = vm[:, u, half, :, :].rearrange("p h c -> p (h c)")[:, 128 * h:128 * h + 128]
                    mm = pe.matmul(OB[u][:, half * 128:half * 128 + 128], own, pT[:, j % 2, g, :],
                                   start=(h == 0), stop=(h == 7))
                mm.then_inc(A.pv, 1)

            def body(b, u):
                f, t, uo = b + 1, b - 1, 1 - u
                if there(f):
                    pe_transpose_in(pe, A, PB[1], f, uo, f)
                if there(b):
                    scores(b, u, 0)
                if there(f):
                    pe.wait_ge(A.xc_T, 2 * f + 2)
                    after(pe, A.km, 2 * f)
                    pe.matmul(PB[0][:, 0:128], wq0[:, :], xT[:, uo, :], start=True, stop=True)
                    pe.matmul(PB[0][:, 128:256], wk0[:, :], cT[0:C, uo, :], start=True, stop=True).then_inc(A.qk, 1)
                    pe.matmul(PB[1][:, 0:D], cT[0:C, uo, :], wv0[:, :], start=True, stop=True).then_inc(A.v, 1)
                if there(b):
                    scores(b, u, 1)
                if there(t):
                    pe.wait_ge(A.o, t + 1)
                    if there(f):
                        after(pe, A.negT_sb, f)
                    pe.matmul(TB[:, 0:D], o0T[0:64, uo, 0, :], wo0[0:64, 0, :], start=True, stop=False)
                    pe.matmul(TB[:, 0:D], o0T[:, uo, 1, :], wo0[:, 1, :], start=False, stop=True).then_inc(A.proj, 1)
                if there(b):
                    values(b, u, 0)
                if there(f):
                    maxima(f, uo, 0)
                if there(b):
                    scores(b, u, 2)
                if there(f):
                    maxima(f, uo, 1)
                if there(b):
                    values(b, u, 1)
                if there(f):
                    maxima(f, uo, 2)
                if there(b):
                    scores(b, u, 3)
                if there(f):
                    maxima(f, uo, 3)
                if there(b):
                    values(b, u, 2)
                if there(f):
                    after(pe, A.x_new, f - 1)
                    pe.wait_ge(A.maxed, f * NCH + NCH)
                    pe.matmul(TB[0:H, 0:128], negmax[:, 0:H], ident_bf[:, :], start=True, stop=True)\
                        .then_inc(A.negT, 1)
                if there(b):
                    values(b, u, 3)
            pipelined(pe, body)
            engines_meet(pe, 1)
            pe.wait_ge(got.ffn0, 32)
            pe.transpose(TB[:, 0:E0], gate_in[:, :], ident[0:E0, 0:E0]).then_inc(F.gate_tr, 1)

            def logits(n):
                pe.wait_ge(F.xT, n + 1)
                for b in range(4 * n, 4 * n + 4):
                    mm = pe.matmul(PB[0][:, E0 * b:E0 * b + E0], xT0[:, b, :], gateT[:, :], start=True, stop=True)
                mm.then_inc(F.logit, 1)
            for n in range(4):
                pe.wait_ge(F.xn, 4 * n + 4)
                if n == 3:
                    pe.wait_ge(F.gateT, 1)
                    logits(0)
                for k in range(4):
                    mm = pe.transpose(blocks(turn_bank[n])[:, k, :], xn0[:, 4 * n + k, :], ident[:, :])
                mm.then_inc(F.tr, 1)
            for n in range(1, 4):
                logits(n)
            pe.wait_ge(got.attn1, 16 * 20)
            for n, rows in enumerate((D, C, C)):
                mm = pe.matmul(PB[1][down_rows(n), 128 * n:128 * n + rows], down[0:rows, n, :], ident[0:rows, 0:rows],
                               start=True, stop=True)
            mm.then_inc(W.turned, 1)
            for n in range(2):
                for c in range(4):
                    mm = pe.transpose(blocks(SCB[n], RANK)[:, c, :], down_o[:, 4 * n + c, :], ident[:, :])
                mm.then_inc(W.turned, 1)

            def fold(s):
                to = fold_bank(s)
                if s >= 6:
                    pe.wait_ge(W.taken, s - 3)
                if s < 2:
                    for c in range(4):
                        part = slice(128 * (4 * s + c), 128 * (4 * s + c) + 128)
                        pe.matmul(blocks(to)[:, c, :], wq1[:, part], ident[:, :], start=True, stop=False)
                        mm = pe.matmul(blocks(to)[:, c, :], up_q[:, part], downT[:, 0, :], start=False, stop=True)
                elif s < 4:
                    for c in range(4):
                        part = slice(128 * (4 * (s - 2) + c), 128 * (4 * (s - 2) + c) + 128)
                        mm = pe.matmul(to[:, C * c:C * c + C], wk1[:, part], ext[:, 0, :], start=True, stop=True)
                elif s < 6:
                    mm = pe.matmul(to[0:C, :], ext[:, 1, :], wv1[:, 512 * (s - 4):512 * (s - 4) + 512], start=True, stop=True)
                elif s < 8:
                    for c in range(4):
                        n = 4 * (s - 6) + c
                        pe.matmul(blocks(to)[:, c, :], ident[:, :], wo1[:, n, :], start=True, stop=False)
                        mm = pe.matmul(blocks(to)[:, c, :], downT[:, 1 + n, :], up_o[:, :], start=False, stop=True)
                elif s < 12:
                    n = s - 8
                    rows = slice(D1 * (n % 2), D1 * (n % 2) + D1)
                    for g in range(CH):
                        c = CH * (n // 2) + g
                        mm = pe.matmul(blocks(to, C)[:, g, :], wk1T[rows, c, :], wq1T[rows, c, :], start=True, stop=True)
                elif s == 12:
                    mm = pe.transpose(to[0:C, 0:B * IPA], ctx_ipa[:, :], ident[0:B * IPA, 0:B * IPA])
                elif s < 15:
                    pe.wait_ge(W.taken, 13)
                    for c in range(8):
                        mm = pe.matmul(to[:, 64 * c:64 * c + 64], (wki, wvi)[s - 13][:, 128 * c:128 * c + 128],
                                       ctx_ipaT[:, :], start=True, stop=True)
                elif s < 17:
                    pe.wait_ge(W.taken, 14)
                    for c in range(4):
                        n = 4 * (s - 15) + c
                        mm = pe.matmul(blocks(to)[:, c, :], wq1T[:, n, :], ipa_kT[:, n, :, :, :], start=True, stop=True)
                else:
                    pe.wait_ge(W.taken, 15)
                    for c in range(4):
                        n = 4 * (s - 17) + c
                        mm = pe.matmul(blocks(to)[:, c, :], ipa_vT[:, n, :, :, :], wo1[:, n, :], start=True, stop=True)
                mm.then_inc(W.made, 1)
            pe.wait_ge(F.xT, 4)
            pe.wait_ge(W.downT, 5)
            fold(0)
            fold(1)
            fold(2)
            fold(3)
            fold(4)
            pe.wait_ge(W.taken, 2)
            pe.wait_ge(F.step, 1)
            for b in range(B):
                if b >= 2:
                    pe.wait_ge(F.ys0, 4 * (b - 1))
                    pe.wait_ge(F.ys1, b - 1)
                for half in range(2):
                    mm = pe.matmul(blocks((SCB, OB)[b % 2][half]), xT0[:, b, :], we[:, 4 * half:4 * half + 4, :],
                                   start=True, stop=True)
                mm.then_inc(F.y, 1)
                if 5 + b < FOLDS:
                    fold(5 + b)
            engines_meet(pe, 2)

            def maxima(f, uf, j):
                if j == 0:
                    pe.wait_ge(Z.x_bf, f + 1)
                pe.wait_ge(Z.k_bf, 2 * f + 1 + j // 2)
                after(pe, Z.maxed, f * NCH + j)
                pe.matmul(blocks(MAXB)[:, :, 0:ORG], x_bf[:, uf, :], k_bf[:, uf, CH * j:CH * j + CH, 0:ORG],
                          start=True, stop=True).then_inc(Z.smax, 1)

            def scores(b, u, j):
                if j == 0:
                    for s in (Z.negT_sb, Z.k0_sb, Z.k1_sb, Z.k2_sb, Z.k3_sb):
                        pe.wait_ge(s, b + 1)
                after(pe, Z.exp, b * NCH + j - 1)
                for g in range(CH):
                    h = CH * j + g
                    to = blocks(SCB[j % 2], ORG)[:, g, :]
                    pe.matmul(to, pick[0:H, h, 0:ORG], negmaxT[0:H, u, :], start=True, stop=False)
                    mm = pe.matmul(to, kT[:, u, h, 0:ORG], xT[:, u, :], start=False, stop=True)
                mm.then_inc(Z.score, 1)

            def values(b, u, j):
                pe.wait_ge(Z.exp, b * NCH + j + 1)
                if j == 0:
                    pe.wait_ge(Z.v0_sb, b + 1)
                    pe.wait_ge(Z.v1_sb, b + 1)
                after(pe, Z.o, b * NCH + j - 1)
                for g in range(CH):
                    mm = pe.matmul(OB[j % 2][:, (D1 + 1) * g:(D1 + 1) * (g + 1)], pT[0:ORG, j % 2, g, :],
                                   v1[0:ORG, u, CH * j + g, :], start=True, stop=True)
                mm.then_inc(Z.pv, 1)

            def keys(n, uf, f, done, freed_by):
                after(pe, *freed_by)
                for g in range(CH):
                    mm = pe.matmul(blocks(PB[n % 2])[:, g, 0:ORG], mT[:, CH * n + g, :], cT[:, uf, 0:ORG],
                                   start=True, stop=True)
                mm.then_inc(done, 1)

            def body(b, u):
                f, t, uo = b + 1, b - 1, 1 - u
                if there(f):
                    pe.wait_ge(Z.xn, f + 1)
                    pe.wait_ge(Z.ctx_in, f + 1)
                    after(pe, Z.ipa_pT, f)
                    pe.transpose(TB[:, 0:128], xn[:, uo, :], ident[:, :])
                    pe.transpose(TB[:, 128:256], ctx_in[:, uo, :], ident[:, :]).then_inc(Z.tr, 1)
                if there(b):
                    scores(b, u, 0)
                if there(t):
                    pe.wait_ge(Z.o, t * NCH + NCH)
                    pe.wait_ge(Z.v0_sb, t + 2) if there(b) else None
                    pe.wait_ge(Z.v1_sb, t + 2) if there(b) else None
                    for half, done in enumerate((Z.oTr0, Z.oTr1)):
                        for c in range(4):
                            n = 4 * half + c
                            mm = pe.transpose(blocks(PB[half])[:, c, :], o[:, uo, 128 * n:128 * n + 128], ident[:, :])
                        mm.then_inc(done, 1)
                if there(b):
                    scores(b, u, 1)
                if there(f):
                    pe.wait_ge(Z.xc_T, 2 * f + 2)
                    pe.matmul(TB[:, 0:H * IPA], xT[:, uo, :], ipa_k[:, f, :], start=True, stop=True)\
                        .then_inc(Z.ipa_score, 1)
                    if there(t):
                        pe.wait_ge(Z.oT_sb, 2 * t + 2)
                    keys(0, uo, f, Z.k0, (Z.v0_sb, f))
                    keys(1, uo, f, Z.k1, (Z.v1_sb, f))
                if there(b):
                    values(b, u, 0)
                if there(f):
                    keys(2, uo, f, Z.k2, (Z.k0_sb, f + 1))
                    keys(3, uo, f, Z.k3, (Z.k1_sb, f + 1))
                if there(t):
                    pe.wait_ge(Z.oT_sb, 2 * t + 2)
                    if there(f):
                        pe.wait_ge(Z.ipa_sub, f + 1)
                    for c in range(8):
                        pe.matmul(TB[:, 0:D], oT[:, uo, c, :], wo1[:, c, :], start=(c == 0), stop=False)
                    if isinstance(t, int) and t == 0:
                        pe.wait_ge(W.back, 16 * 8)
                    pe.matmul(TB[:, 0:D], ipa_pT[:, uo, :], ipa_v[:, t, :], start=False, stop=True).then_inc(Z.proj, 1)
                if there(b):
                    scores(b, u, 2)
                if there(f):
                    maxima(f, uo, 0)
                    for n, (done, freed) in enumerate(((Z.v0, Z.k2_sb), (Z.v1, Z.k3_sb))):
                        pe.wait_ge(freed, f + 1)
                        pe.matmul(PB[n][0:ORG, :], cT[:, uo, 0:ORG], wv1[:, 512 * n:512 * n + 512],
                                  start=True, stop=True).then_inc(done, 1)
                if there(b):
                    values(b, u, 1)
                if there(f):
                    maxima(f, uo, 1)
                if there(b):
                    scores(b, u, 3)
                if there(f):
                    maxima(f, uo, 2)
                    after(pe, Z.x_new, f - 1)
                    pe.wait_ge(Z.ipa_p, f + 1)
                    pe.matmul(TB[0:H * IPA, 0:128], ipa_s[:, uo, :, :].rearrange("p h j -> p (h j)"), ident[:, :],
                              start=True, stop=True).then_inc(Z.ipa_turn, 1)
                if there(b):
                    values(b, u, 2)
                if there(f):
                    maxima(f, uo, 3)
                if there(b):
                    values(b, u, 3)
                if there(f):
                    pe.wait_ge(Z.maxed, f * NCH + NCH)
                    pe.matmul(MAXB[0:H, 0:128], negmax[:, 0:H], ident_bf[:, :], start=True, stop=True).then_inc(Z.negT, 1)
            pipelined(pe, body)
            engines_meet(pe, 3)

            pe.wait_ge(R.wide, 2)
            for n in range(4):
                pe.wait_ge(R.xn, 4 * n + 4)
                for k in range(4):
                    mm = pe.transpose(blocks(bank[n])[:, k, :], xn_all[:, 4 * n + k, :], ident[:, :])
                mm.then_inc(R.tr, 1)
            for n in range(4):
                pe.wait_ge(R.xT, n + 1)
                pe.matmul(bank[n][:, :], rw1[:, :], xT4[:, n, :, :], start=True, stop=True).then_inc(R.hid, 1)
            for b in range(B):
                pe.wait_ge(R.h, b // 4 + 1)
                mm = pe.matmul(bank[4 + b // 8][:, 0:128], rw2_of(b), hT4[:, b // 4, b % 4, :],
                               start=(b % 8 == 0), stop=(b % 8 == 7))
                if b % 8 == 7:
                    mm.then_inc(R.logit, 1)
            ident4 = ident[:, :].rearrange("p (b g q) -> p q b g", b=8, g=EG)
            for t in range(2):
                pe.wait_ge(R.step, 2 * (4 + 11 + 5) - 1 + t)
                for n, what in enumerate((top_at_f, top)):
                    for q in range(4):
                        mm = pe.matmul(bank[6 + t][32 * q:32 * q + 32, 32 * n:32 * n + 32], what[:, t, :],
                                       ident4[:, q, :, :], start=True, stop=True)
                mm.then_inc(R.turned, 1)

            def body(b, u):
                t = b - 1
                if there(b):
                    pe.wait_ge(G.row, b + 1)
                    after(pe, G.oh, b - 1)
                    for g in range(EG):
                        mm = pe.matmul(blocks(bank[u])[:, g, :], oh_bf[:, u, g, :], ident_bf[:, :],
                                       start=True, stop=True)
                    mm.then_inc(G.turned, 1)
                if there(t):
                    pe.wait_ge(G.oh, t + 1)
                    pe.wait_ge(G.xn, t + 1)
                    after(pe, G.xg, t - 1)
                    pe.matmul(bank[2 + (1 - u)][:, :], xn[:, 1 - u, :], oh[:, 1 - u, 0:4, 0:128], start=True, stop=True)\
                        .then_inc(G.got, 1)
            body(0, 0)
            body(1, 1)
            with pe.Fori(0, B // 2 - 1) as i:
                body(i * 2 + 2, 0)
                body(i * 2 + 3, 1)
            body(B, 0)
            engines_meet(pe, 4)

            def inner(e, g, q):
                pe.wait_ge(w_in[q % 4], 48 * (g + q // 4 + 1))
                for c in range(2):
                    after(pe, X1.h, 2 * e + c - 1)
                    for n, w in enumerate((ew1, ew2)):
                        mm = pe.matmul(bank[2 * c + n][:, :], w[:, q % 4, 128 * c:128 * c + 128], xgT[:, :, e, :],
                                       start=True, stop=True)
                    mm.then_inc(X1.gv, 1)

            def body(e, g, q):
                if there_expert(e + 1):
                    inner(e + 1, g, q + 1)
                pe.wait_ge(X1.h, 2 * e + 2)
                pe.wait_ge(X1.eo_act, e + 1)
                pe.wait_ge(X1.eo_dve, e + 1)
                for k in range(4):
                    for c in range(2):
                        mm = pe.matmul(bank[4 + 2 * (q % 2) + k // 2][:, D * (k % 2):D * (k % 2) + D],
                                       hs[:, q % 2, c, 128 * k:128 * k + 128], ew3[:, q % 4, c, :],
                                       start=(c == 0), stop=(c == 1))
                mm.then_inc(X1.eo, 1)
            experts(pe, inner, body)
            engines_meet(pe, 5)

            for b in range(B):
                after(pe, Y.x_new, b - 1)
                for g in range(EG):
                    mm = pe.matmul(bank[b % 2][:, 0:D], ohw[:, b, g, :], eo_all[:, b, g, :], start=(g == 0),
                                   stop=(g == EG - 1))
                mm.then_inc(Y.sum, 1)


def kernel(**inputs):
    import numpy as _np
    import concourse.bacc as _bacc
    from concourse.bass_utils import run_bass_kernel_spmd as _run

    nc = _bacc.Bacc("TRN2", target_bir_lowering=False, num_devices=1)
    arrays, tensors = {}, {}
    for name, value in inputs.items():
        a = _np.ascontiguousarray(value)
        arrays[f"in_{name}_dram"] = a
        tensors[name] = nc.dram_tensor(f"in_{name}_dram", a.shape, mybir.dt.from_np(a.dtype), kind="ExternalInput").ap()
    out = nc.dram_tensor("out_0_dram", (B, S, D), F32, kind="ExternalOutput").ap()
    build_program(nc, tensors, out)
    r = _run(nc, [arrays], core_ids=[0])
    return r.results[0]["out_0_dram"]
```
